# Optimizing a Trainium2 kernel written in Bass

```python
import numpy as np
import jax
import jax.numpy as jnp

def _softmax(x, axis=-1):
    return jax.nn.softmax(x, axis=axis)

def _gelu(x):
    return jax.nn.gelu(x, approximate=True)

def _silu(x):
    return jax.nn.silu(x)

def _sigmoid(x):
    return jax.nn.sigmoid(x)

def _layernorm(x, axis=-1, eps=1e-05):
    m = jnp.mean(x, axis=axis, keepdims=True)
    v = jnp.var(x, axis=axis, keepdims=True)
    return (x - m) / jnp.sqrt(v + eps)

def _scatter_add(tgt, idx, src, axis=0):
    return tgt.at[idx].add(src)

def _segment_sum(src, seg, n):
    return jax.ops.segment_sum(src, seg, n)
kernel_name = 'mk_flamingo_gated_d2_seqx_r4_fe3655'

def setup_inputs(seed: int=0):
    np.random.seed(seed)
    _w = jnp.asarray

    def _rec_inputs():
        import jax
        import jax.numpy as jnp
        _rk = jax.random.key(seed)
        x = -0.0002928 + 1 * jax.random.normal(jax.random.fold_in(_rk, 1), (64, 128, 256), jnp.float32)
        _lenS = 128 - jax.random.randint(jax.random.fold_in(_rk, 7), (64,), 0, max(1, 128 // 4) + 1, jnp.int32)
        _lenS2 = 128 - jax.random.randint(jax.random.fold_in(_rk, 8), (64,), 0, max(1, 128 // 4) + 1, jnp.int32)
        _ctx_1024P = jax.random.normal(jax.random.fold_in(_rk, 11), (64, 16, 256), jnp.float32)
        _ctx_1024c = jax.random.dirichlet(jax.random.fold_in(_rk, 511), 0.3 * jnp.ones((16,), jnp.float32), (64, 128))
        _ctx_1024t = jnp.einsum('bsk,bkd->bsd', _ctx_1024c, _ctx_1024P)
        _ctx_1024t = _ctx_1024t * jax.lax.rsqrt(jnp.mean(jnp.square(_ctx_1024t)) + 1e-12) * 0.953939
        ctx_1024 = -1.39393e-06 + 0.999914 * (_ctx_1024t + 0.3 * jax.random.normal(jax.random.fold_in(_rk, 611), (64, 128, 256), jnp.float32))
        _g = jax.random.normal(jax.random.fold_in(_rk, 9001), (2, 2), jnp.float32)
        _g = jnp.sign(_g) * jnp.maximum(jnp.abs(_g), 1.0) + (_g == 0) * 1.0
        g_xattn = _g[0]
        g_ffn = _g[1]
        return (x, ctx_1024, g_xattn, g_ffn)
    x, ctx_1024, g_xattn, g_ffn = _rec_inputs()

    def _L0_xattn_setup():
        import jax, jax.numpy as jnp
        import numpy as np
        NUM_HEADS = 16
        key = jax.random.key(seed)
        kq, kk, kv = jax.random.split(key, 3)
        b, s, h = (1, 1024, 256)
        q = jax.random.normal(kq, (b, s, h), dtype=jnp.float32)
        k = jax.random.normal(kk, (b, s, h), dtype=jnp.float32)
        v = jax.random.normal(kv, (b, s, h), dtype=jnp.float32)
        return {'q': q, 'k': k, 'v': v}
    _L0_xattn_all = _L0_xattn_setup()
    _L0_xattn_in = {k: v for k, v in _L0_xattn_all.items() if k in ()}
    del _L0_xattn_all

    def _L0_ffn_setup():
        import jax, jax.numpy as jnp
        import numpy as np
        B, S, D_MODEL, D_HIDDEN = (4, 512, 256, 1024)

        def act_quant(x):
            scale = 127.0 / jnp.clip(jnp.max(jnp.abs(x), axis=-1, keepdims=True), 1e-05)
            return jnp.clip(jnp.round(x * scale), -128, 127) / scale

        def weight_quant(w):
            scale = 1.0 / jnp.clip(jnp.mean(jnp.abs(w)), 1e-05)
            return jnp.clip(jnp.round(w * scale), -1, 1) / scale

        def bit_linear(x, w):
            xq = x + jax.lax.stop_gradient(act_quant(x) - x)
            wq = w + jax.lax.stop_gradient(weight_quant(w) - w)
            return jnp.einsum('bsd,hd->bsh', xq, wq)

        def depthwise_conv1d(x_bcl, w, b):
            y = jax.lax.conv_general_dilated(x_bcl, w, window_strides=(1,), padding=[(1, 1)], dimension_numbers=('NCH', 'OIH', 'NCH'), feature_group_count=x_bcl.shape[1])
            return y + b[None, :, None]
        key = jax.random.key(seed)
        ks = jax.random.split(key, 5)
        lim1 = 1.0 / np.sqrt(D_MODEL)
        lim2 = 1.0 / np.sqrt(D_HIDDEN)
        limc = 1.0 / np.sqrt(3.0)
        return {'x': jax.random.normal(ks[0], (B, S, D_MODEL), dtype=jnp.float32), 'w1': jax.random.uniform(ks[1], (D_HIDDEN, D_MODEL), jnp.float32, -lim1, lim1), 'conv_w': jax.random.uniform(ks[2], (D_HIDDEN, 1, 3), jnp.float32, -limc, limc), 'conv_b': jax.random.uniform(ks[3], (D_HIDDEN,), jnp.float32, -limc, limc), 'w2': jax.random.uniform(ks[4], (D_MODEL, D_HIDDEN), jnp.float32, -lim2, lim2)}
    _L0_ffn_all = _L0_ffn_setup()
    _L0_ffn_in = {k: v for k, v in _L0_ffn_all.items() if k in ('w1', 'conv_w', 'conv_b', 'w2')}
    del _L0_ffn_all

    def _L1_xattn_setup():
        import jax, jax.numpy as jnp
        import numpy as np
        BETA = 256
        NUM_HEADS = 16
        NORM = (BETA // NUM_HEADS) ** (-0.5)
        key = jax.random.key(seed)
        ks = jax.random.split(key, 6)
        B, N = (4, 512)
        D_in_q = D_in_k = D_in_v = 256
        D_out_k = D_out_v = 256
        q = jax.random.normal(ks[0], (B, N, D_in_q), dtype=jnp.float32)
        k = jax.random.normal(ks[1], (B, N, D_in_k), dtype=jnp.float32)
        v = jax.random.normal(ks[2], (B, N, D_in_v), dtype=jnp.float32)
        Wq = jax.random.normal(ks[3], (D_out_k, D_in_q), dtype=jnp.float32) * D_in_q ** (-0.5)
        Wk = jax.random.normal(ks[4], (D_out_k, D_in_k), dtype=jnp.float32) * D_in_k ** (-0.5)
        Wv = jax.random.normal(ks[5], (D_out_v, D_in_v), dtype=jnp.float32) * D_in_v ** (-0.5)
        return {'q': q, 'k': k, 'v': v, 'Wq': Wq, 'Wk': Wk, 'Wv': Wv}
    _L1_xattn_all = _L1_xattn_setup()
    _L1_xattn_in = {k: v for k, v in _L1_xattn_all.items() if k in ('Wq', 'Wk', 'Wv')}
    del _L1_xattn_all

    def _L1_ffn_setup():
        import jax, jax.numpy as jnp
        import numpy as np
        H = 256
        I = 128
        E = 8
        TOPK = 2
        NGROUP = 4
        TOPKG = 2
        SCALE = 1.0
        B, S = (4, 256)

        def _gate(xf, gate_weight, bias):
            T = xf.shape[0]
            logits = xf @ gate_weight.T
            scores = jax.nn.sigmoid(logits)
            scores_for_choice = scores + bias[None, :]
            gsz = E // NGROUP
            grp = scores_for_choice.reshape(T, NGROUP, gsz)
            group_scores = jax.lax.top_k(grp, 2)[0].sum(-1)
            _, group_idx = jax.lax.top_k(group_scores, TOPKG)
            rows = jnp.arange(T)[:, None]
            group_mask = jnp.zeros((T, NGROUP), xf.dtype).at[rows, group_idx].set(1.0)
            score_mask = jnp.broadcast_to(group_mask[:, :, None], (T, NGROUP, gsz)).reshape(T, E)
            tmp_scores = jnp.where(score_mask > 0, scores_for_choice, 0.0)
            _, topk_idx = jax.lax.top_k(tmp_scores, TOPK)
            topk_weight = jnp.take_along_axis(scores, topk_idx, axis=1)
            if TOPK > 1:
                topk_weight = topk_weight / (topk_weight.sum(-1, keepdims=True) + 1e-20)
            topk_weight = topk_weight * SCALE
            return (topk_idx, topk_weight)
        key = jax.random.key(seed)
        k0, k1, k2, k3, k4 = jax.random.split(key, 5)
        return {'hidden_states': jax.random.normal(k0, (B, S, H), jnp.float32), 'gate_weight': jax.random.normal(k1, (E, H), jnp.float32) * (1.0 / np.sqrt(H)), 'e_score_correction_bias': jnp.zeros((E,), jnp.float32), 'gate_proj': jax.random.normal(k2, (E, I, H), jnp.float32) * 0.02, 'up_proj': jax.random.normal(k3, (E, I, H), jnp.float32) * 0.02, 'down_proj': jax.random.normal(k4, (E, H, I), jnp.float32) * 0.02}
    _L1_ffn_all = _L1_ffn_setup()
    _L1_ffn_in = {k: v for k, v in _L1_ffn_all.items() if k in ('gate_weight', 'e_score_correction_bias', 'gate_proj', 'up_proj', 'down_proj')}
    del _L1_ffn_all
    return {'x': x, 'ctx_1024': ctx_1024, 'g_xattn': g_xattn, 'g_ffn': g_ffn, 'L0_ffn_w1': _L0_ffn_in['w1'], 'L0_ffn_conv_w': _L0_ffn_in['conv_w'], 'L0_ffn_conv_b': _L0_ffn_in['conv_b'], 'L0_ffn_w2': _L0_ffn_in['w2'], 'L1_xattn_Wq': _L1_xattn_in['Wq'], 'L1_xattn_Wk': _L1_xattn_in['Wk'], 'L1_xattn_Wv': _L1_xattn_in['Wv'], 'L1_ffn_gate_weight': _L1_ffn_in['gate_weight'], 'L1_ffn_e_score_correction_bias': _L1_ffn_in['e_score_correction_bias'], 'L1_ffn_gate_proj': _L1_ffn_in['gate_proj'], 'L1_ffn_up_proj': _L1_ffn_in['up_proj'], 'L1_ffn_down_proj': _L1_ffn_in['down_proj']}

def reference(x, ctx_1024, g_xattn, g_ffn, L0_ffn_w1, L0_ffn_conv_w, L0_ffn_conv_b, L0_ffn_w2, L1_xattn_Wq, L1_xattn_Wk, L1_xattn_Wv, L1_ffn_gate_weight, L1_ffn_e_score_correction_bias, L1_ffn_gate_proj, L1_ffn_up_proj, L1_ffn_down_proj):
    import jax
    import jax.numpy as jnp

    def _L0_xattn_ref(q, k, v):
        import jax, jax.numpy as jnp
        import numpy as np
        NUM_HEADS = 16
        b, s, hd = q.shape
        n = NUM_HEADS
        d = hd // n
        qh = q.reshape(b, s, n, d)
        kh = k.reshape(b, s, n, d)
        vh = v.reshape(b, s, n, d)
        scale = 1.0 / jnp.sqrt(jnp.float32(d))
        scores = jnp.einsum('bqnd,bknd->bnqk', qh, kh) * scale
        probs = jax.nn.softmax(scores, axis=-1)
        out = jnp.einsum('bnqk,bknd->bqnd', probs, vh)
        return out.reshape(b, s, hd)

    def _L0_ffn_ref(x, w1, conv_w, conv_b, w2):
        import jax, jax.numpy as jnp
        import numpy as np
        B, S, D_MODEL, D_HIDDEN = (4, 512, 256, 1024)

        def act_quant(x):
            scale = 127.0 / jnp.clip(jnp.max(jnp.abs(x), axis=-1, keepdims=True), 1e-05)
            return jnp.clip(jnp.round(x * scale), -128, 127) / scale

        def weight_quant(w):
            scale = 1.0 / jnp.clip(jnp.mean(jnp.abs(w)), 1e-05)
            return jnp.clip(jnp.round(w * scale), -1, 1) / scale

        def bit_linear(x, w):
            xq = x + jax.lax.stop_gradient(act_quant(x) - x)
            wq = w + jax.lax.stop_gradient(weight_quant(w) - w)
            return jnp.einsum('bsd,hd->bsh', xq, wq)

        def depthwise_conv1d(x_bcl, w, b):
            y = jax.lax.conv_general_dilated(x_bcl, w, window_strides=(1,), padding=[(1, 1)], dimension_numbers=('NCH', 'OIH', 'NCH'), feature_group_count=x_bcl.shape[1])
            return y + b[None, :, None]
        h = bit_linear(x, w1)
        h = depthwise_conv1d(h.transpose(0, 2, 1), conv_w, conv_b)
        h = h.transpose(0, 2, 1)
        h = jax.nn.silu(h)
        return bit_linear(h, w2)

    def _L1_xattn_ref(q, k, v, Wq, Wk, Wv):
        import jax, jax.numpy as jnp
        import numpy as np
        BETA = 256
        NUM_HEADS = 16
        NORM = (BETA // NUM_HEADS) ** (-0.5)
        qp = jax.nn.relu(jnp.einsum('bnd,od->bno', q, Wq))
        kp = jax.nn.relu(jnp.einsum('bnd,od->bno', k, Wk))
        vp = jax.nn.relu(jnp.einsum('bnd,od->bno', v, Wv))
        B, N, D = qp.shape
        dh = D // NUM_HEADS
        qh = qp.reshape(B, N, NUM_HEADS, dh)
        kh = kp.reshape(B, N, NUM_HEADS, dh)
        vh = vp.reshape(B, N, NUM_HEADS, vp.shape[-1] // NUM_HEADS)
        E = NORM * jnp.einsum('bqhd,bkhd->bhqk', qh, kh)
        A = jax.nn.softmax(E, axis=-1)
        out = jnp.einsum('bhqk,bkhd->bqhd', A, vh)
        return out.reshape(B, N, -1)

    def _L1_ffn_ref(hidden_states, gate_weight, e_score_correction_bias, gate_proj, up_proj, down_proj):
        import jax, jax.numpy as jnp
        import numpy as np
        H = 256
        I = 128
        E = 8
        TOPK = 2
        NGROUP = 4
        TOPKG = 2
        SCALE = 1.0
        B, S = (4, 256)

        def _gate(xf, gate_weight, bias):
            T = xf.shape[0]
            logits = xf @ gate_weight.T
            scores = jax.nn.sigmoid(logits)
            scores_for_choice = scores + bias[None, :]
            gsz = E // NGROUP
            grp = scores_for_choice.reshape(T, NGROUP, gsz)
            group_scores = jax.lax.top_k(grp, 2)[0].sum(-1)
            _, group_idx = jax.lax.top_k(group_scores, TOPKG)
            rows = jnp.arange(T)[:, None]
            group_mask = jnp.zeros((T, NGROUP), xf.dtype).at[rows, group_idx].set(1.0)
            score_mask = jnp.broadcast_to(group_mask[:, :, None], (T, NGROUP, gsz)).reshape(T, E)
            tmp_scores = jnp.where(score_mask > 0, scores_for_choice, 0.0)
            _, topk_idx = jax.lax.top_k(tmp_scores, TOPK)
            topk_weight = jnp.take_along_axis(scores, topk_idx, axis=1)
            if TOPK > 1:
                topk_weight = topk_weight / (topk_weight.sum(-1, keepdims=True) + 1e-20)
            topk_weight = topk_weight * SCALE
            return (topk_idx, topk_weight)
        Bv, Sv, Hv = hidden_states.shape
        xf = hidden_states.reshape(-1, Hv).astype(jnp.float32)
        topk_idx, topk_weight = _gate(xf, gate_weight.astype(jnp.float32), e_score_correction_bias.astype(jnp.float32))
        y = jnp.zeros_like(xf)
        for e in range(E):
            combine_w = jnp.where(topk_idx == e, topk_weight, 0.0).sum(-1)
            g = xf @ gate_proj[e].T
            u = xf @ up_proj[e].T
            o = jax.nn.silu(g) * u @ down_proj[e].T
            y = y + combine_w[:, None] * o
        return y.reshape(Bv, Sv, Hv)
    x = x + jnp.tanh(g_xattn[0]) * _L0_xattn_ref(_layernorm(x, axis=-1), ctx_1024, ctx_1024)
    x = x + jnp.tanh(g_ffn[0]) * _L0_ffn_ref(_layernorm(x, axis=-1), L0_ffn_w1, L0_ffn_conv_w, L0_ffn_conv_b, L0_ffn_w2)
    x = x + jnp.tanh(g_xattn[1]) * _L1_xattn_ref(_layernorm(x, axis=-1), ctx_1024, ctx_1024, L1_xattn_Wq, L1_xattn_Wk, L1_xattn_Wv)
    x = x + jnp.tanh(g_ffn[1]) * _L1_ffn_ref(_layernorm(x, axis=-1), L1_ffn_gate_weight, L1_ffn_e_score_correction_bias, L1_ffn_gate_proj, L1_ffn_up_proj, L1_ffn_down_proj)
    return x

_drawn_inputs = setup_inputs


def setup_inputs(seed=0):
    import zlib

    import numpy as np

    out = dict(_drawn_inputs(seed))
    spreads = {'g_ffn': (-1.0, 0.6), 'L1_ffn_e_score_correction_bias': (0.0, 0.8)}
    factors = {'L1_ffn_gate_weight': 8.0,
     'L1_ffn_gate_proj': 8.0,
     'L1_ffn_up_proj': 8.0,
     'L1_ffn_down_proj': 8.0}
    for name, (base, spread) in spreads.items():
        noise = np.random.default_rng([zlib.crc32(name.encode()), seed]).standard_normal(out[name].shape)
        drawn = base * np.exp(spread * noise) if base else spread * noise
        out[name] = jnp.asarray(drawn.astype(out[name].dtype))
    for name, factor in factors.items():
        out[name] = (out[name] * factor).astype(out[name].dtype)
    return out
```

```python
from contextlib import ExitStack

import concourse.bass as bass
from concourse import mybir

F32 = mybir.dt.float32
F16 = mybir.dt.float16
ALU = mybir.AluOpType
ACT = mybir.ActivationFunctionType
AX = mybir.AxisListType

P = 128
TILES = 64
D = 256
DC = D // P
HEADS = 16
DH = D // HEADS
SLOT = 4 * DH
HG = 4
NG = HEADS // HG
PAIRS = HEADS // 2
UNROLL = 4
HID = 1024
HC = HID // P
GT = 4
GROUPS = TILES // GT
GW = GT * P
EXPERTS = 8
EGROUPS = 4
TOP = 2
WS = 32.0
XS = 64.0
LN_EPS = 1e-5
MAGIC = 12582912.0


def reach(engine, semaphore, value):
    if isinstance(value, int) and value <= 0:
        return
    engine.wait_ge(semaphore, value)


def run_steps(engine, step, period, head, count, tail):
    for i in range(head):
        step(i, i % period)
    with engine.Fori(head // period, count // period) as j:
        for u in range(period):
            step(j * period + u, u)
    for i in range(count, count + tail):
        step(i, i % period)


def head_of(g, k):
    return 8 * (g // 2) + 2 * k + g % 2, g % 2


def inside(t, count):
    return not isinstance(t, int) or 0 <= t < count


class Shared:
    pass


def load_stage(nc, io, m, sem):
    chunks = 4
    per = TILES // chunks
    x_in = [sem(f"x_loaded{c}") for c in range(chunks)]
    ctx_in = [sem(f"ctx_loaded{c}") for c in range(chunks)]
    gates_in = sem("gates_loaded")
    const_made = sem("constants_made")
    tanh_made = sem("tanh_made")
    x_view = io["x"].rearrange("b s d -> s b d")
    ctx_view = io["ctx_1024"].rearrange("b s d -> s b d")
    with nc.Block() as block:

        @block.sync
        def _(sp):
            for c in range(chunks):
                sp.dma_start(m.x[:, c * per:(c + 1) * per, :], x_view[:, c * per:(c + 1) * per, :]).then_inc(x_in[c], 16)
            for c in range(chunks):
                sp.wait_ge(ctx_in[c], 16)

        @block.scalar
        def _(act):
            act.dma_start(m.gates[:, 0:2], io["g_xattn"].rearrange("(a n) -> a n", a=1).broadcast_to([P, 2])).then_inc(gates_in, 16)
            act.dma_start(m.gates[:, 2:4], io["g_ffn"].rearrange("(a n) -> a n", a=1).broadcast_to([P, 2])).then_inc(gates_in, 16)
            for c in range(chunks):
                act.dma_start(m.ctx[:, c * per:(c + 1) * per, :], ctx_view[:, c * per:(c + 1) * per, :]).then_inc(ctx_in[c], 16)
            act.wait_ge(gates_in, 32)
            nc.scalar.activation(m.tanh_gates[:, :], m.gates[:, :], ACT.Tanh).then_inc(tanh_made, 1)
            act.wait_ge(tanh_made, 1)

        @block.gpsimd
        def _(pool):
            nc.gpsimd.memset(m.ident32[:, :], 1.0).then_inc(const_made, 1)
            pool.wait_ge(const_made, 1)
            nc.gpsimd.affine_select(out=m.ident32[:, :], in_=m.ident32[:, :], pattern=[[-1, P]], compare_op=ALU.is_equal,
                                    fill=0.0, base=0, channel_multiplier=1).then_inc(const_made, 1)
            pool.wait_ge(const_made, 2)
            nc.gpsimd.tensor_copy(m.ident16[:, :], m.ident32[:, :]).then_inc(const_made, 1)
            nc.gpsimd.memset(m.ones32[:, :], 1.0).then_inc(const_made, 1)
            pool.wait_ge(const_made, 4)

        @block.vector
        def _(dve):
            for c in range(chunks):
                dve.wait_ge(x_in[c], 16)
                with dve.Fori(c * per // UNROLL, (c + 1) * per // UNROLL) as j:
                    for u in range(UNROLL):
                        nc.vector.bn_stats(m.stats[:, j * UNROLL + u, :], m.x[:, j * UNROLL + u, :])


def deviation_stage(nc, m, sem, name):
    joined = sem(f"{name}_joined")
    biased = sem(f"{name}_biased")
    rooted = sem(f"{name}_rooted")
    inverted = sem(f"{name}_inverted")
    with nc.Block() as block:

        @block.vector
        def _(dve):
            even_mean, even_dev, odd_mean, odd_dev = (m.stats[:, :, k] for k in (1, 2, 4, 5))
            nc.vector.tensor_tensor(m.mean[:, :], even_mean, odd_mean, ALU.add).then_inc(joined, 1)
            nc.vector.tensor_tensor(m.root[:, :], even_mean, odd_mean, ALU.subtract).then_inc(joined, 1)
            nc.vector.tensor_tensor(m.rstd[:, :], even_dev, odd_dev, ALU.add).then_inc(joined, 1)
            dve.wait_ge(joined, 3)
            nc.vector.tensor_scalar(m.mean[:, :], m.mean[:, :], 0.5, None, ALU.mult).then_inc(joined, 1)
            nc.vector.scalar_tensor_tensor(out=m.root[:, :], in0=m.root[:, :], scalar=D / 4.0, in1=m.root[:, :],
                                           op0=ALU.mult, op1=ALU.mult).then_inc(joined, 1)
            dve.wait_ge(joined, 5)
            nc.vector.tensor_tensor(m.rstd[:, :], m.rstd[:, :], m.root[:, :], ALU.add).then_inc(joined, 1)
            dve.wait_ge(joined, 6)
            nc.vector.tensor_scalar(m.rstd[:, :], m.rstd[:, :], 1.0 / D, LN_EPS, ALU.mult, ALU.add).then_inc(biased, 1)
            dve.wait_ge(rooted, 1)
            nc.vector.reciprocal(m.rstd[:, :], m.root[:, :]).then_inc(inverted, 1)
            dve.wait_ge(inverted, 1)

        @block.scalar
        def _(act):
            act.wait_ge(biased, 1)
            nc.scalar.activation(m.root[:, :], m.rstd[:, :], ACT.Sqrt).then_inc(rooted, 1)


def projection_weights(nc, io, m, w_hi, w_lo, psum, sem):
    with ExitStack() as ctx:
        raw = ctx.enter_context(nc.sbuf_tensor("proj_raw", [P, 3, DC, D], F32))
        scaled = ctx.enter_context(nc.sbuf_tensor("proj_scaled", [P, 3, DC, D], F32))
        hi = ctx.enter_context(nc.sbuf_tensor("proj_hi", [P, 3, DC, D], F16))
        lo = ctx.enter_context(nc.sbuf_tensor("proj_lo", [P, 3, DC, D], F16))
        loaded, scaled_ok, hi_ok, lo_ok, turned, copied = (sem(f"proj_{n}") for n in (
            "loaded", "scaled_ok", "hi_ok", "lo_ok", "turned", "copied"))
        block = ctx.enter_context(nc.Block())

        @block.sync
        def _(sp):
            for n, name in enumerate(("L1_xattn_Wq", "L1_xattn_Wk", "L1_xattn_Wv")):
                sp.dma_start(raw[:, n, :, :], io[name].rearrange("(c p) d -> p c d", p=P)).then_inc(loaded, 16)
            sp.wait_ge(loaded, 48)

        @block.vector
        def _(dve):
            dve.wait_ge(loaded, 48)
            nc.vector.tensor_scalar(scaled[:], raw[:], WS, None, ALU.mult).then_inc(scaled_ok, 1)
            dve.wait_ge(hi_ok, 1)
            nc.vector.tensor_tensor(lo[:], scaled[:], hi[:], ALU.subtract).then_inc(lo_ok, 1)
            for n in range(4):
                dve.wait_ge(turned, n + 1)
                dst = (w_hi, w_lo)[n // 2][:, n % 2, :]
                nc.vector.tensor_copy(dst, psum[n % 2][:, 0:6 * P]).then_inc(copied, 1)
            dve.wait_ge(copied, 4)

        @block.scalar
        def _(act):
            act.wait_ge(scaled_ok, 1)
            nc.scalar.activation(hi[:], scaled[:], ACT.Copy).then_inc(hi_ok, 1)

        @block.tensor
        def _(pe):
            for n in range(4):
                pe.wait_ge(lo_ok, 1)
                reach(pe, copied, n - 1)
                src = (hi, lo)[n // 2]
                for k in range(6):
                    last = nc.tensor.transpose(psum[n % 2][:, k * P:(k + 1) * P],
                                               src[:, k // 2, k % 2, (n % 2) * P:(n % 2 + 1) * P], m.ident16[:, :])
                last.then_inc(turned, 1)


def attention_stage(nc, io, m, layer, sem_scope):
    L = layer
    scale = WS if layer else 1.0
    last_lag = 4 + L
    head = UNROLL * (-(-last_lag // UNROLL))
    with ExitStack() as ctx:
        def sem(name):
            return ctx.enter_context(nc.semaphore(f"a{layer}_{name}"))

        def sb(name, shape, dt):
            return ctx.enter_context(nc.sbuf_tensor(f"a{layer}_{name}", shape, dt))

        def bank(name, dt=F32):
            return ctx.enter_context(nc.psum_tensor(f"a{layer}_{name}", [P, 2048 // (4 if dt == F32 else 2)], dt))

        turn = [bank("turn0", F16), bank("turn1", F16)]
        if layer:
            w_hi, w_lo = sb("w_hi", [P, DC, 3 * D], F16), sb("w_lo", [P, DC, 3 * D], F16)
            projection_weights(nc, io, m, w_hi, w_lo, turn, sem)
        score = [bank(f"score{n}") for n in range(1 if layer else 2)]
        score_t = [bank("score_t0"), bank("score_t1")]
        out = bank("out")
        if layer:
            q_ps, kv_ps = bank("q_ps"), bank("kv_ps")

        KR = 2 if layer else 4
        q_stack = sb("q_stack", [P, 2, HEADS, 4, DH], F16)
        k_stack = sb("k_stack", [P, KR, HEADS, 4, DH], F16)
        q_turned = sb("q_turned", [P, 4, HEADS // 2, P], F16)
        k_turned = sb("k_turned", [P, 4, HEADS // 2, P], F16)
        normed = sb("normed", [P, 2, D], F32)
        exp32 = sb("exp32", [P, NG, HG * P], F32)
        exp_hi = sb("exp_hi", [P, 2, NG, HG, P], F16)
        exp_lo = sb("exp_lo", [P, 2, NG, HG, P], F16)
        maxes = sb("maxes", [P, HEADS], F32)
        neg_max = sb("neg_max", [P, 2, 2, SLOT], F16)
        neg_max_t = sb("neg_max_t", [P, 2, P], F16)
        spread = sb("spread", [P, PAIRS, P], F16)
        rsum = sb("rsum", [P, HEADS], F32)
        mixed = sb("mixed", [P, HEADS, DH], F32)
        gate = sb("gate", [P, 1], F32)
        if layer:
            split = sb("split", [P, 2, 4, D], F16)
            split_t = sb("split_t", [P, 2, 4 * DC, P], F16)
            v_hi = sb("v_hi", [P, 4, HEADS, DH + 1], F16)
            v_lo = sb("v_lo", [P, 4, HEADS, DH], F16)

        made, nf_ok, qh_ok, ql_ok, kh_ok, kl_ok = (sem(n) for n in ("made", "nf_ok", "qh_ok", "ql_ok", "kh_ok", "kl_ok"))
        q_turn, k_turn, m_turn = sem("q_turn"), sem("k_turn"), sem("m_turn")
        q_copied, k_copied, m_copied = sem("q_copied"), sem("k_copied"), sem("m_copied")
        scores_ok, max_ok, neg_ok = sem("scores_ok"), sem("max_ok"), sem("neg_ok")
        scores_t_ok, exp_ok, exp_lo_ok = sem("scores_t_ok"), sem("exp_ok"), sem("exp_lo_ok")
        values_ok, out_read, fin_ok = sem("values_ok"), sem("out_read"), sem("fin_ok")
        if layer:
            nh_ok, nl_ok, cl_ok = sem("nh_ok"), sem("nl_ok"), sem("cl_ok")
            s_turn, s_copied, q_proj, kv_proj, vl_ok = sem("s_turn"), sem("s_copied"), sem("q_proj"), sem("kv_proj"), sem("vl_ok")

        with nc.Block() as block:

            @block.vector
            def _(dve):
                nc.vector.memset(q_stack[:], 0.0).then_inc(made, 1)
                nc.vector.memset(neg_max[:], 0.0).then_inc(made, 1)
                nc.vector.memset(k_stack[:], 0.0).then_inc(made, 1)
                dve.wait_ge(made, 3)
                nc.vector.memset(k_stack[:, :, :, 3, 0:1], 1.0).then_inc(made, 1)
                nc.vector.tensor_scalar(gate[:], m.tanh_gates[:, layer:layer + 1], 1.0 / scale, None, ALU.mult).then_inc(made, 1)
                if layer:
                    nc.vector.memset(v_hi[:, :, :, DH:DH + 1], 1.0).then_inc(made, 1)
                dve.wait_ge(made, 5 + L)

            @block.gpsimd
            def _(pool):
                nc.gpsimd.memset(spread[:], scale * scale).then_inc(kl_ok, 1)
                pool.wait_ge(kl_ok, 1)
                nc.gpsimd.affine_select(out=spread[:], in_=spread[:], pattern=[[-1, PAIRS], [0, P]],
                                        compare_op=ALU.is_equal, fill=0.0, base=0, channel_multiplier=1).then_inc(kl_ok, 1)
                pool.wait_ge(kl_ok, 2)
                nc.gpsimd.affine_select(out=spread[:], in_=spread[:], pattern=[[-1, PAIRS], [0, P]],
                                        compare_op=ALU.not_equal, fill=scale * scale, base=-SLOT, channel_multiplier=1).then_inc(kl_ok, 1)
                pool.wait_ge(kl_ok, 3)
        KL0 = 3

        with nc.Block() as block:

            @block.tensor
            def _(pe):
                def do_scores(t, q4, g):
                    if g == 0:
                        reach(pe, k_copied, t + 1)
                    reach(pe, max_ok, t * NG + (g + 1 - len(score)))
                    for k in range(HG):
                        h, half = head_of(g, k)
                        r = SLOT * half
                        last = nc.tensor.matmul(score[g % len(score)][:, k * P:(k + 1) * P], q_turned[r:r + SLOT, q4, h // 2, :],
                                                k_turned[r:r + SLOT, q4, h // 2, :], start=True, stop=True)
                    last.then_inc(scores_ok, 1)

                def do_scores_t(t, q4, g):
                    if g == 0:
                        reach(pe, m_copied, t + 1)
                    reach(pe, exp_ok, t * NG + (g - 1))
                    for k in range(HG):
                        h, half = head_of(g, k)
                        r = SLOT * half
                        dst = score_t[g % 2][:, k * P:(k + 1) * P]
                        nc.tensor.matmul(dst, k_turned[r:r + SLOT, q4, h // 2, :], q_turned[r:r + SLOT, q4, h // 2, :],
                                         start=True, stop=False)
                        last = nc.tensor.matmul(dst, spread[r:r + SLOT, h // 2, :], neg_max_t[r:r + SLOT, q4 % 2, :], start=False, stop=True)
                    last.then_inc(scores_t_ok, 1)

                def do_values(t, q4, g):
                    reach(pe, exp_lo_ok, t * NG + (g + 1))
                    if g == 0:
                        reach(pe, out_read, t)
                    for k in range(HG):
                        h, _ = head_of(g, k)
                        c = h * (DH + 1)
                        if layer:
                            vh, vl = v_hi[:, q4, h, :], v_lo[:, q4, h, :]
                        else:
                            one = k_stack[:, q4, h, :, :].rearrange("p a d -> p (a d)")
                            vh, vl = one[:, 2 * DH:3 * DH + 1], one[:, DH:2 * DH]
                        nc.tensor.matmul(out[:, c:c + DH + 1], exp_hi[:, q4 % 2, g, k, :], vh, start=True, stop=False)
                        nc.tensor.matmul(out[:, c:c + DH], exp_hi[:, q4 % 2, g, k, :], vl, start=False, stop=False)
                        last = nc.tensor.matmul(out[:, c:c + DH + 1], exp_lo[:, q4 % 2, g, k, :], vh, start=False, stop=True)
                    if g == NG - 1:
                        last.then_inc(values_ok, 1)

                def step(i, u):
                    if inside(i - 2 - L, TILES):
                        t, q4 = i - (2 + L), (u - 2 - L) % 4
                        reach(pe, neg_ok, t + 1)
                        if inside(i - 1 - L, TILES):
                            reach(pe, q_copied, i - L)
                        nc.tensor.transpose(turn[0][:, 0:P], neg_max[:, q4 % 2, :, :].rearrange("p r n -> p (r n)"), m.ident16[:, :]).then_inc(m_turn, 1)
                    for g in range(NG):
                        if g == NG - 1 and inside(i - L, TILES):
                            t, q4 = i - L, (u - L) % 4
                            reach(pe, ql_ok, t + 1)
                            if inside(i - 2 - L, TILES):
                                reach(pe, m_copied, i - (1 + L))
                            else:
                                reach(pe, q_copied, t)
                            for n in range(HEADS // 2):
                                last = nc.tensor.transpose(turn[0][:, n * P:(n + 1) * P],
                                                           q_stack[:, q4 % 2, 2 * n:2 * n + 2, :, :].rearrange("p h a d -> p (h a d)"),
                                                           m.ident16[:, :])
                            last.then_inc(q_turn, 1)
                            reach(pe, kl_ok, t + (1 + KL0))
                            if layer:
                                reach(pe, s_copied, t + 1)
                            else:
                                reach(pe, k_copied, t)
                            for n in range(HEADS // 2):
                                last = nc.tensor.transpose(turn[1][:, n * P:(n + 1) * P],
                                                           k_stack[:, q4 % KR, 2 * n:2 * n + 2, :, :].rearrange("p h a d -> p (h a d)"),
                                                           m.ident16[:, :])
                            last.then_inc(k_turn, 1)
                        if inside(i - 1 - L, TILES):
                            do_scores(i - (1 + L), (u - 1 - L) % 4, g)
                        if inside(i - 2 - L, TILES):
                            do_scores_t(i - (2 + L), (u - 2 - L) % 4, g)
                        if inside(i - 3 - L, TILES):
                            do_values(i - (3 + L), (u - 3 - L) % 4, g)
                        if layer and g == 0 and inside(i - 1, TILES):
                            t, q2 = i - 1, (u - 1) % 2
                            reach(pe, s_copied, t + 1)
                            reach(pe, ql_ok, t)
                            terms = ((0, w_hi), (0, w_lo), (2, w_hi))
                            for n, (part, w) in enumerate(terms):
                                for c in range(DC):
                                    last = nc.tensor.matmul(q_ps[:, 0:D], split_t[:, q2, part * DC + c, :], w[:, c, 0:D],
                                                            start=(n == 0 and c == 0), stop=(n == 2 and c == DC - 1))
                            last.then_inc(q_proj, 1)
                            reach(pe, vl_ok, t)
                            for n, (part, w) in enumerate(terms):
                                for c in range(DC):
                                    last = nc.tensor.matmul(kv_ps[:, 0:2 * D], split_t[:, q2, (part + 1) * DC + c, :], w[:, c, D:3 * D],
                                                            start=(n == 0 and c == 0), stop=(n == 2 and c == DC - 1))
                            last.then_inc(kv_proj, 1)
                    if layer and inside(i, TILES):
                        reach(pe, nl_ok, i + 1)
                        reach(pe, cl_ok, i + 1)
                        if inside(i - L, TILES):
                            reach(pe, k_copied, i - L + 1)
                        for n in range(4 * DC):
                            last = nc.tensor.transpose(turn[1][:, n * P:(n + 1) * P],
                                                       split[:, u % 2, n // DC, (n % DC) * P:(n % DC + 1) * P], m.ident16[:, :])
                        last.then_inc(s_turn, 1)

                run_steps(pe, step, UNROLL, head, TILES, last_lag)

            @block.vector
            def _(dve):
                def take_max(t, g):
                    reach(dve, scores_ok, t * NG + (g + 1))
                    nc.vector.tensor_reduce(maxes[:, g * HG:(g + 1) * HG],
                                            score[g % len(score)][:, :].rearrange("p (h k) -> p h k", h=HG),
                                            AX.X, ALU.max).then_inc(max_ok, 1)

                def step(i, u):
                    if inside(i - 4 - L, TILES):
                        t = i - (4 + L)
                        reach(dve, values_ok, t + 1)
                        sums = out[:, 0:HEADS * (DH + 1)].rearrange("p (h d) -> p h d", h=HEADS)
                        nc.vector.reciprocal(rsum[:, :], sums[:, :, DH]).then_inc(fin_ok, 1)
                        reach(dve, fin_ok, t * 3 + 1)
                        nc.vector.tensor_tensor(mixed[:], sums[:, :, 0:DH], rsum[:, :, None].broadcast_to([P, HEADS, DH]),
                                                ALU.mult).then_inc(out_read, 1)
                        reach(dve, out_read, t + 1)
                        nc.vector.scalar_tensor_tensor(out=m.x[:, t, :], in0=mixed[:].rearrange("p h d -> p (h d)"), scalar=gate[:, 0:1],
                                                       in1=m.x[:, t, :], op0=ALU.mult, op1=ALU.add).then_inc(fin_ok, 1)
                        reach(dve, fin_ok, t * 3 + 2)
                    if inside(i - 2 - L, TILES):
                        reach(dve, m_turn, i - (1 + L))
                        nc.vector.tensor_copy(neg_max_t[:, (u - 2 - L) % 2, :], turn[0][:, 0:P]).then_inc(m_copied, 1)
                    if layer and inside(i - 1, TILES):
                        reach(dve, s_turn, i)
                        nc.vector.tensor_copy(split_t[:, (u - 1) % 2, :, :], turn[1][:, :].rearrange("p (n k) -> p n k", k=P)).then_inc(s_copied, 1)
                    if inside(i, TILES):
                        if layer:
                            reach(dve, nh_ok, i - 1)
                            reach(dve, nl_ok, i - 1)
                        else:
                            reach(dve, qh_ok, i - 1)
                            reach(dve, ql_ok, i - 1)
                        nc.vector.tensor_scalar(normed[:, u % 2, :], m.x[:, i, :], m.mean[:, bass.ds(i, 1)], m.rstd[:, bass.ds(i, 1)],
                                                ALU.subtract, ALU.mult).then_inc(nf_ok, 1)
                    if inside(i - 4 - L, TILES):
                        nc.vector.bn_stats(m.stats[:, i - (4 + L), :], m.x[:, i - (4 + L), :]).then_inc(fin_ok, 1)
                    if inside(i - 1 - L, TILES):
                        take_max(i - (1 + L), 0)
                        if layer:
                            take_max(i - (1 + L), 1)
                    if layer and inside(i - 1, TILES):
                        t, q2, q4 = i - 1, (u - 1) % 2, (u - 1) % 4
                        heads = lambda ap: ap.rearrange("p (h d) -> p h d", h=HEADS)
                        reach(dve, qh_ok, t + 1)
                        nc.vector.scalar_tensor_tensor(out=q_stack[:, q2, :, 2, :], in0=heads(q_ps[:, 0:D]), scalar=0.0,
                                                       in1=q_stack[:, q2, :, 0, :], op0=ALU.max, op1=ALU.subtract).then_inc(ql_ok, 1)
                        reach(dve, kh_ok, t + 1)
                        nc.vector.scalar_tensor_tensor(out=k_stack[:, q2, :, 1, :], in0=heads(kv_ps[:, 0:D]), scalar=0.0,
                                                       in1=k_stack[:, q2, :, 0, :], op0=ALU.max, op1=ALU.subtract).then_inc(kl_ok, 1)
                        nc.vector.scalar_tensor_tensor(out=v_lo[:, q4, :, :], in0=heads(kv_ps[:, D:2 * D]), scalar=0.0,
                                                       in1=v_hi[:, q4, :, 0:DH], op0=ALU.max, op1=ALU.subtract).then_inc(vl_ok, 1)
                    if inside(i - 1 - L, TILES) and not layer:
                        take_max(i - (1 + L), 1)
                    if inside(i, TILES):
                        if layer:
                            reach(dve, nh_ok, i + 1)
                            nc.vector.tensor_tensor(split[:, u % 2, 2, :], normed[:, u % 2, :], split[:, u % 2, 0, :],
                                                    ALU.subtract).then_inc(nl_ok, 1)
                        else:
                            reach(dve, qh_ok, i + 1)
                            nc.vector.tensor_tensor(q_stack[:, u % 2, :, 2, :], normed[:, u % 2, :].rearrange("p (h d) -> p h d", h=HEADS),
                                                    q_stack[:, u % 2, :, 0, :], ALU.subtract).then_inc(ql_ok, 1)
                    if inside(i - 1 - L, TILES):
                        take_max(i - (1 + L), 2)
                    if inside(i - L, TILES):
                        reach(dve, q_turn, i - L + 1)
                        nc.vector.tensor_copy(q_turned[:, (u - L) % 4, :, :], turn[0][:, :].rearrange("p (n k) -> p n k", k=P)).then_inc(q_copied, 1)
                        reach(dve, k_turn, i - L + 1)
                        nc.vector.tensor_copy(k_turned[:, (u - L) % 4, :, :], turn[1][:, :].rearrange("p (n k) -> p n k", k=P)).then_inc(k_copied, 1)
                    if inside(i - 1 - L, TILES):
                        t = i - (1 + L)
                        take_max(t, 3)
                        reach(dve, max_ok, t * NG + NG)
                        nc.vector.tensor_scalar(neg_max[:, (u - 1 - L) % 2, :, 0:PAIRS].rearrange("p r (a k) -> p r a k", k=HG),
                                                maxes[:, :].rearrange("p (a r k) -> p r a k", r=2, k=HG), -1.0 / (scale * scale), None,
                                                ALU.mult).then_inc(neg_ok, 1)
                        reach(dve, neg_ok, t + 1)

                run_steps(dve, step, UNROLL, head, TILES, last_lag)

            @block.scalar
            def _(act):
                nc.scalar.preload_act_table(ACT.Exp)

                def do_exp(t, q4, g):
                    reach(act, scores_t_ok, t * NG + (g + 1))
                    if g == 0:
                        reach(act, values_ok, t - 1)
                    reach(act, exp_lo_ok, t * NG + (g - NG + 1))
                    nc.scalar.activation(exp32[:, g, :], score_t[g % 2][:, :], ACT.Exp, scale=DH ** -0.5 / (scale * scale))
                    nc.scalar.activation(exp_hi[:, q4 % 2, g, :, :].rearrange("p h q -> p (h q)"), score_t[g % 2][:, :],
                                         ACT.Exp, scale=DH ** -0.5 / (scale * scale)).then_inc(exp_ok, 1)

                def step(i, u):
                    run_exp = inside(i - 2 - L, TILES)
                    if run_exp:
                        do_exp(i - (2 + L), (u - 2 - L) % 4, 0)
                    if inside(i, TILES):
                        reach(act, nf_ok, i + 1)
                        if layer:
                            reach(act, s_turn, i - 1)
                            nc.scalar.activation(split[:, u % 2, 0, :], normed[:, u % 2, :], ACT.Copy)
                            nc.scalar.activation(split[:, u % 2, 1, :], m.ctx[:, i, :], ACT.Copy).then_inc(nh_ok, 1)
                        else:
                            reach(act, q_turn, i - 1)
                            nc.scalar.activation(q_stack[:, u % 2, :, 0:2, :],
                                                 normed[:, u % 2, :].rearrange("p (h a d) -> p h a d", h=HEADS, a=1).broadcast_to([P, HEADS, 2, DH]),
                                                 ACT.Copy).then_inc(qh_ok, 1)
                            reach(act, values_ok, i - 3)
                            nc.scalar.activation(k_stack[:, u % 4, :, 0:3:2, :],
                                                 m.ctx[:, i, :].rearrange("p (h a d) -> p h a d", h=HEADS, a=1).broadcast_to([P, HEADS, 2, DH]),
                                                 ACT.Copy).then_inc(kh_ok, 1)
                    if run_exp:
                        do_exp(i - (2 + L), (u - 2 - L) % 4, 1)
                    if layer and inside(i - 1, TILES):
                        t, q2, q4 = i - 1, (u - 1) % 2, (u - 1) % 4
                        twice = lambda ap: ap.rearrange("p (h a d) -> p h a d", h=HEADS, a=1).broadcast_to([P, HEADS, 2, DH])
                        reach(act, q_proj, t + 1)
                        reach(act, k_turn, t - 1)
                        nc.scalar.activation(q_stack[:, q2, :, 0:2, :], twice(q_ps[:, 0:D]), ACT.Relu).then_inc(qh_ok, 1)
                        reach(act, kv_proj, t + 1)
                        nc.scalar.activation(k_stack[:, q2, :, 0:3:2, :], twice(kv_ps[:, 0:D]), ACT.Relu)
                        reach(act, values_ok, t - 3)
                        nc.scalar.activation(v_hi[:, q4, :, 0:DH], kv_ps[:, D:2 * D].rearrange("p (h d) -> p h d", h=HEADS),
                                             ACT.Relu).then_inc(kh_ok, 1)
                    if run_exp:
                        do_exp(i - (2 + L), (u - 2 - L) % 4, 2)
                        do_exp(i - (2 + L), (u - 2 - L) % 4, 3)

                run_steps(act, step, UNROLL, head, TILES, last_lag)

            @block.gpsimd
            def _(pool):
                def do_lo(t, q4, g):
                    reach(pool, exp_ok, t * NG + (g + 1))
                    nc.gpsimd.tensor_tensor(exp_lo[:, q4 % 2, g, :, :].rearrange("p h q -> p (h q)"), exp32[:, g, :],
                                            exp_hi[:, q4 % 2, g, :, :].rearrange("p h q -> p (h q)"),
                                            ALU.subtract).then_inc(exp_lo_ok, 1)

                def step(i, u):
                    run_lo = inside(i - 2 - L, TILES)
                    if run_lo:
                        do_lo(i - (2 + L), (u - 2 - L) % 4, 0)
                    if inside(i, TILES):
                        if layer:
                            reach(pool, nh_ok, i + 1)
                            nc.gpsimd.tensor_tensor(split[:, u % 2, 3, :], m.ctx[:, i, :], split[:, u % 2, 1, :],
                                                    ALU.subtract).then_inc(cl_ok, 1)
                        else:
                            reach(pool, kh_ok, i + 1)
                            nc.gpsimd.tensor_tensor(k_stack[:, u % 4, :, 1, :], m.ctx[:, i, :].rearrange("p (h d) -> p h d", h=HEADS),
                                                    k_stack[:, u % 4, :, 0, :], ALU.subtract).then_inc(kl_ok, 1)
                    if run_lo:
                        for g in range(1, NG):
                            do_lo(i - (2 + L), (u - 2 - L) % 4, g)

                run_steps(pool, step, UNROLL, head, TILES, last_lag)


def bitnet_stage(nc, io, m):
    lag, head = 3, 4
    with ExitStack() as ctx:
        def sem(name):
            return ctx.enter_context(nc.semaphore(f"b_{name}"))

        def sb(name, shape, dt=F32):
            return ctx.enter_context(nc.sbuf_tensor(f"b_{name}", shape, dt))

        def bank(name, dt=F32):
            return ctx.enter_context(nc.psum_tensor(f"b_{name}", [P, 2048 // (4 if dt == F32 else 2)], dt))

        turn = [bank("turn0", F16), bank("turn1", F16)]
        hid = [bank("hid0"), bank("hid1")]
        out = [bank("out0"), bank("out1")]
        peaks, spread_ps = bank("peaks"), bank("spread_ps")
        w1t = sb("w1t", [P, DC, HID], F16)
        w2t = sb("w2t", [P, HC, D], F16)
        taps = sb("taps", [P, HC, 3])
        conv_b = sb("conv_b", [P, HC])
        weight_mean = sb("weight_mean", [P, 2])
        in_back = sb("in_back", [P, 1])
        out_back = sb("out_back", [P, 1])

        with ExitStack() as prep:
            raw = [prep.enter_context(nc.sbuf_tensor(f"b_raw{n}", [P, 2048], F32)) for n in range(2)]
            scaled = [prep.enter_context(nc.sbuf_tensor(f"b_scaled{n}", [P, 2048], F32)) for n in range(2)]
            tern = [prep.enter_context(nc.sbuf_tensor(f"b_tern{n}", [P, 2048], F16)) for n in range(2)]
            rows = prep.enter_context(nc.sbuf_tensor("b_rows", [P, 2], F32))
            inverse = prep.enter_context(nc.sbuf_tensor("b_inverse", [P, 2], F32))
            w_in, taps_in, rows_ok, total_ok, chain, turned, copied, w1_in = (sem(n) for n in (
                "w_in", "taps_in", "rows_ok", "total_ok", "chain", "turned", "copied", "w1_in"))
            block = prep.enter_context(nc.Block())

            @block.sync
            def _(sp):
                sp.dma_start(raw[0][:].rearrange("p (c d) -> p c d", c=HC), io["L0_ffn_w1"].rearrange("(c p) d -> p c d", p=P)).then_inc(w1_in, 16)
                sp.dma_start(raw[1][:].rearrange("p (c d) -> p c d", c=DC), io["L0_ffn_w2"].rearrange("(c p) d -> p c d", p=P)).then_inc(w_in, 16)
                with nc.allow_non_contiguous_dma(reason="small"):
                    sp.dma_start(taps[:], io["L0_ffn_conv_w"].rearrange("(c p) a k -> p c (a k)", p=P)).then_inc(taps_in, 16)
                    sp.dma_start(conv_b[:], io["L0_ffn_conv_b"].rearrange("(c p) -> p c", p=P)).then_inc(taps_in, 16)
                sp.wait_ge(taps_in, 32)

            @block.tensor
            def _(pe):
                pe.wait_ge(rows_ok, 2)
                nc.tensor.matmul(peaks[:, 0:2], m.ones32[:, :], rows[:, :], start=True, stop=True).then_inc(total_ok, 1)
                pe.wait_ge(chain, 13)
                for n in range(4):
                    reach(pe, copied, n - 1)
                    for k in range(8):
                        q = (n % 2) * 8 + k
                        a, b = (q % HC, q // HC) if n < 2 else (q % DC, q // DC)
                        width = D if n < 2 else HID
                        last = nc.tensor.transpose(turn[n % 2][:, k * P:(k + 1) * P],
                                                   tern[n // 2][:, a * width + b * P:a * width + (b + 1) * P], m.ident16[:, :])
                    last.then_inc(turned, 1)

            @block.vector
            def _(dve):
                step = [0]

                def then(instruction):
                    step[0] += 1
                    instruction.then_inc(chain, 1)
                    dve.wait_ge(chain, step[0])

                dve.wait_ge(w1_in, 16)
                nc.vector.tensor_reduce(rows[:, 0:1], raw[0][:], AX.X, ALU.add, apply_absolute_value=True).then_inc(rows_ok, 1)
                dve.wait_ge(w_in, 16)
                nc.vector.tensor_reduce(rows[:, 1:2], raw[1][:], AX.X, ALU.add, apply_absolute_value=True).then_inc(rows_ok, 1)
                dve.wait_ge(total_ok, 1)
                then(nc.vector.tensor_scalar(weight_mean[:], peaks[:, 0:2], 1.0 / (HID * D), 1e-5, ALU.mult, ALU.max))
                then(nc.vector.reciprocal(inverse[:], weight_mean[:]))
                for n in range(2):
                    then(nc.vector.tensor_scalar(scaled[n][:], raw[n][:], inverse[:, n:n + 1], MAGIC, ALU.mult, ALU.add))
                    then(nc.vector.tensor_scalar(scaled[n][:], scaled[n][:], MAGIC, 1.0, ALU.subtract, ALU.min))
                    then(nc.vector.tensor_scalar(tern[n][:], scaled[n][:], -1.0, None, ALU.max))
                dve.wait_ge(taps_in, 32)
                then(nc.vector.tensor_scalar(taps[:], taps[:], 1.0 / XS, None, ALU.mult))
                then(nc.vector.tensor_scalar(in_back[:], weight_mean[:, 0:1], XS / 127.0, None, ALU.mult))
                then(nc.vector.tensor_scalar(out_back[:], weight_mean[:, 1:2], 1.0 / 127.0, m.tanh_gates[:, 2:3], ALU.mult, ALU.mult))
                then(nc.vector.memset(rows[:], 0.0))
                then(nc.vector.memset(inverse[:], 0.0))
                for n in range(4):
                    dve.wait_ge(turned, n + 1)
                    dst = w1t[:, n % 2, :] if n < 2 else w2t[:, 4 * (n % 2):4 * (n % 2) + 4, :].rearrange("p c d -> p (c d)")
                    nc.vector.tensor_copy(dst, turn[n % 2][:, :]).then_inc(copied, 1)
                dve.wait_ge(copied, 4)

        normed = sb("normed", [P, GT, D])
        x_parts = sb("x_parts", [P, 2, GT, D], F16)
        x_turned = sb("x_turned", [P, DC, 2, GT, P], F16)
        peak_in, scale_in, back_in = sb("peak_in", [P, GT]), sb("scale_in", [P, GT]), sb("back_in", [P, GT])
        peak_mid, scale_mid, back_mid = sb("peak_mid", [P, GT]), sb("scale_mid", [P, GT]), sb("back_mid", [P, 2, GT])
        shifted = sb("shifted", [P, 2, GW])
        hidden = sb("hidden", [P, 2, HC, GW])
        peak_t, peak_half = sb("peak_t", [P, 2, GW]), sb("peak_half", [P, GW])
        diagonal = sb("diagonal", [P, GT, P])
        ints = sb("ints", [P, HC, GW], F16)

        (norm_ok, in_ok, deq_ok, hi_ok, lo_ok, t_turn, t_copied, hid_ok, tap_r, tap_l, conv_ok, hidden_ok,
         peak_ok, peak_turn, mid_ok, diag_ok, spread_ok, mult_ok, ints_ok, out_ok, fin_ok) = (sem(n) for n in (
             "norm_ok", "in_ok", "deq_ok", "hi_ok", "lo_ok", "t_turn", "t_copied", "hid_ok", "tap_r", "tap_l", "conv_ok",
             "hidden_ok", "peak_ok", "peak_turn", "mid_ok", "diag_ok", "spread_ok", "mult_ok", "ints_ok", "out_ok", "fin_ok"))

        with nc.Block() as block:

            @block.tensor
            def _(pe):
                def first_product(t, u, c):
                    if c == 0:
                        reach(pe, t_copied, 2 * t + 2)
                    reach(pe, tap_r, t * HC + (c - 1))
                    for d in range(DC):
                        for part in range(2):
                            last = nc.tensor.matmul(hid[c % 2][:, :], w1t[:, d, c * P:(c + 1) * P],
                                                    x_turned[:, d, part, :, :].rearrange("p t k -> p (t k)"),
                                                    start=(d == 0 and part == 0), stop=(d == DC - 1 and part == 1))
                    last.then_inc(hid_ok, 1)

                def step(j, u):
                    if inside(j - 2, GROUPS):
                        reach(pe, peak_ok, (j - 2) * 3 + 3)
                        for k in range(GT):
                            last = nc.tensor.transpose(peaks[:, k * P:(k + 1) * P], peak_t[:, u % 2, k * P:(k + 1) * P], m.ident32[:, :])
                        last.then_inc(peak_turn, 1)
                    if inside(j - 1, GROUPS):
                        first_product(j - 1, u - 1, 0)
                        first_product(j - 1, u - 1, 1)
                    if inside(j - 2, GROUPS):
                        reach(pe, diag_ok, j - 1)
                        nc.tensor.matmul(spread_ps[:, :], m.ones32[:, :], diagonal[:].rearrange("p t k -> p (t k)"),
                                         start=True, stop=True).then_inc(spread_ok, 1)
                    if inside(j - 1, GROUPS):
                        for c in range(2, HC):
                            first_product(j - 1, u - 1, c)
                    if inside(j, GROUPS):
                        reach(pe, hi_ok, j + 1)
                        reach(pe, lo_ok, j + 1)
                        for d in range(DC):
                            reach(pe, t_copied, 2 * j + (d - 1))
                            for part in range(2):
                                for k in range(GT):
                                    n = part * GT + k
                                    last = nc.tensor.transpose(turn[d][:, n * P:(n + 1) * P], x_parts[:, part, k, d * P:(d + 1) * P], m.ident16[:, :])
                            last.then_inc(t_turn, 1)
                    if inside(j - 2, GROUPS):
                        reach(pe, ints_ok, (j - 2) * HC + HC)
                        reach(pe, fin_ok, j - 2)
                        for k in range(GT):
                            dst = out[k // 2][:, (k % 2) * D:(k % 2 + 1) * D]
                            for c in range(HC):
                                last = nc.tensor.matmul(dst, ints[:, c, k * P:(k + 1) * P], w2t[:, c, :], start=(c == 0), stop=(c == HC - 1))
                        last.then_inc(out_ok, 1)

                run_steps(pe, step, 2, head, GROUPS, lag)

            @block.vector
            def _(dve):
                def convolve(t, u, c):
                    reach(dve, tap_l, t * HC + (c + 1))
                    dst = hidden[:, u % 2, c, :].rearrange("p (t k) -> p t k", k=P)[:, :, 0:P - 1]
                    nc.vector.scalar_tensor_tensor(out=dst, in0=hid[c % 2][:, :].rearrange("p (t k) -> p t k", k=P)[:, :, 1:P],
                                                   scalar=taps[:, c, 2:3], in1=dst, op0=ALU.mult, op1=ALU.add).then_inc(tap_r, 1)

                def largest(t, u, half):
                    last = half == 1
                    reach(dve, hidden_ok, t * HC + (HC if last else HC // 2))
                    dst = peak_half if last else peak_t[:, u % 2, :]
                    src = hidden[:, u % 2, half * HC // 2:(half + 1) * HC // 2, :].rearrange("p c k -> p k c")
                    nc.vector.tensor_reduce(dst[:, :] if last else dst, src, AX.X, ALU.max, apply_absolute_value=True).then_inc(peak_ok, 1)
                    if last:
                        reach(dve, peak_ok, t * 3 + 2)
                        nc.vector.tensor_tensor(peak_t[:, u % 2, :], peak_t[:, u % 2, :], peak_half[:, :], ALU.max).then_inc(peak_ok, 1)

                def requantise(t, u, c):
                    if c == 0:
                        reach(dve, spread_ok, t + 1)
                        reach(dve, out_ok, t)
                    nc.vector.tensor_tensor(hidden[:, u % 2, c, :], hidden[:, u % 2, c, :], spread_ps[:, :], ALU.mult).then_inc(mult_ok, 1)
                    reach(dve, mult_ok, t * HC + (c + 1))
                    nc.vector.tensor_scalar(ints[:, c, :], hidden[:, u % 2, c, :], MAGIC, MAGIC, ALU.add, ALU.subtract).then_inc(ints_ok, 1)

                def step(j, u):
                    if inside(j - 3, GROUPS):
                        t = j - 3
                        reach(dve, out_ok, t + 1)
                        for k in range(GT):
                            x = m.x[:, t * GT + k, :]
                            last = nc.vector.scalar_tensor_tensor(out=x, in0=out[k // 2][:, (k % 2) * D:(k % 2 + 1) * D],
                                                                  scalar=back_mid[:, (u - 3) % 2, k:k + 1], in1=x, op0=ALU.mult, op1=ALU.add)
                        last.then_inc(fin_ok, 1)
                        reach(dve, fin_ok, t + 1)
                    if inside(j - 2, GROUPS):
                        t = j - 2
                        reach(dve, peak_turn, t + 1)
                        nc.vector.tensor_reduce(peak_mid[:], peaks[:, :].rearrange("p (t k) -> p t k", k=P), AX.X, ALU.max).then_inc(mid_ok, 1)
                        reach(dve, mid_ok, t * 4 + 1)
                        nc.vector.tensor_scalar(peak_mid[:], peak_mid[:], 1e-5, None, ALU.max).then_inc(mid_ok, 1)
                        reach(dve, mid_ok, t * 4 + 2)
                        nc.vector.reciprocal(scale_mid[:], peak_mid[:]).then_inc(mid_ok, 1)
                        nc.vector.tensor_scalar(back_mid[:, u % 2, :], peak_mid[:], out_back[:, 0:1], None, ALU.mult)
                        reach(dve, mid_ok, t * 4 + 3)
                        nc.vector.tensor_scalar(scale_mid[:], scale_mid[:], 127.0, None, ALU.mult).then_inc(mid_ok, 1)
                        reach(dve, mid_ok, t * 4 + 4)
                        for k in range(GT):
                            last = nc.vector.tensor_scalar(diagonal[:, k, :], m.ident32[:, :], scale_mid[:, k:k + 1], None, ALU.mult)
                        last.then_inc(diag_ok, 1)
                    if inside(j, GROUPS):
                        reach(dve, lo_ok, j)
                        for k in range(GT):
                            last = nc.vector.tensor_scalar(normed[:, k, :], m.x[:, j * GT + k, :], m.mean[:, j, k:k + 1],
                                                           m.rstd[:, j, k:k + 1], ALU.subtract, ALU.mult)
                        last.then_inc(norm_ok, 1)
                    if inside(j - 3, GROUPS):
                        for k in range(GT):
                            nc.vector.bn_stats(m.stats[:, (j - 3) * GT + k, :], m.x[:, (j - 3) * GT + k, :])
                    if inside(j, GROUPS):
                        reach(dve, norm_ok, j + 1)
                        nc.vector.tensor_reduce(peak_in[:], normed[:], AX.X, ALU.max, apply_absolute_value=True).then_inc(in_ok, 1)
                        reach(dve, in_ok, j * 4 + 1)
                        nc.vector.tensor_scalar(peak_in[:], peak_in[:], 1e-5, None, ALU.max).then_inc(in_ok, 1)
                        reach(dve, in_ok, j * 4 + 2)
                        nc.vector.reciprocal(scale_in[:], peak_in[:]).then_inc(in_ok, 1)
                        nc.vector.tensor_scalar(back_in[:], peak_in[:], in_back[:, 0:1], None, ALU.mult)
                        reach(dve, in_ok, j * 4 + 3)
                        nc.vector.tensor_scalar(scale_in[:], scale_in[:], 127.0, None, ALU.mult).then_inc(in_ok, 1)
                        reach(dve, in_ok, j * 4 + 4)
                        for k in range(GT):
                            last = nc.vector.tensor_scalar(normed[:, k, :], normed[:, k, :], scale_in[:, k:k + 1], MAGIC, ALU.mult, ALU.add)
                        last.then_inc(deq_ok, 1)
                        reach(dve, deq_ok, j * 2 + 1)
                        for k in range(GT):
                            last = nc.vector.tensor_scalar(normed[:, k, :], normed[:, k, :], MAGIC, back_in[:, k:k + 1], ALU.subtract, ALU.mult)
                        last.then_inc(deq_ok, 1)
                    for c in range(HC + 2):
                        if c < HC and inside(j - 1, GROUPS):
                            convolve(j - 1, u - 1, c)
                        if c < HC and inside(j - 2, GROUPS):
                            requantise(j - 2, u - 2, c)
                        if c in (HC - 1, HC + 1) and inside(j - 1, GROUPS):
                            largest(j - 1, u - 1, int(c > HC))
                    if inside(j, GROUPS):
                        for d in range(DC):
                            reach(dve, t_turn, 2 * j + (d + 1))
                            nc.vector.tensor_copy(x_turned[:, d, :, :, :],
                                                  turn[d][:, :].rearrange("p (a t k) -> p a t k", a=2, t=GT)).then_inc(t_copied, 1)

                run_steps(dve, step, 2, head, GROUPS, lag)

            @block.scalar
            def _(act):
                nc.scalar.preload_act_table(ACT.Silu)

                def split(j):
                    reach(act, deq_ok, j * 2 + 2)
                    reach(act, t_turn, 2 * j)
                    nc.scalar.activation(x_parts[:, 0, :, :], normed[:], ACT.Copy).then_inc(hi_ok, 1)

                def step(j, u):
                    for c in range(HC + 2):
                        if c < HC and inside(j - 1, GROUPS):
                            n = (j - 1) * HC + c
                            reach(act, hid_ok, n + 1)
                            if c == 0:
                                reach(act, ints_ok, (j - 2) * HC)
                            reach(act, conv_ok, n - 1)
                            nc.scalar.activation(hidden[:, (u - 1) % 2, c, :], hid[c % 2][:, :], ACT.Identity, scale=taps[:, c, 1:2],
                                                 bias=conv_b[:, c:c + 1])
                            nc.scalar.activation(shifted[:, c % 2, :], hid[c % 2][:, :], ACT.Copy, scale=taps[:, c, 0:1]).then_inc(tap_l, 1)
                        if c == 3 and inside(j, GROUPS):
                            split(j)
                        if c >= 2 and inside(j - 1, GROUPS):
                            n = (j - 1) * HC + c - 2
                            reach(act, conv_ok, n + 1)
                            nc.scalar.activation(hidden[:, (u - 1) % 2, c - 2, :], hidden[:, (u - 1) % 2, c - 2, :], ACT.Silu).then_inc(hidden_ok, 1)

                run_steps(act, step, 2, head, GROUPS, lag)

            @block.gpsimd
            def _(pool):
                def step(j, u):
                    for c in range(HC):
                        if inside(j - 1, GROUPS):
                            n = (j - 1) * HC + c
                            reach(pool, tap_l, n + 1)
                            reach(pool, tap_r, n + 1)
                            dst = hidden[:, (u - 1) % 2, c, :].rearrange("p (t k) -> p t k", k=P)[:, :, 1:P]
                            nc.gpsimd.tensor_tensor(dst, dst, shifted[:, c % 2, :].rearrange("p (t k) -> p t k", k=P)[:, :, 0:P - 1],
                                                    ALU.add).then_inc(conv_ok, 1)
                        if c == 3 and inside(j, GROUPS):
                            reach(pool, hi_ok, j + 1)
                            nc.gpsimd.tensor_tensor(x_parts[:, 1, :, :], normed[:], x_parts[:, 0, :, :], ALU.subtract).then_inc(lo_ok, 1)

                run_steps(pool, step, 2, head, GROUPS, lag)


def expert_stage(nc, io, m):
    lag, head = 2, 2
    with ExitStack() as ctx:
        def sem(name):
            return ctx.enter_context(nc.semaphore(f"e_{name}"))

        def sb(name, shape, dt=F32):
            return ctx.enter_context(nc.sbuf_tensor(f"e_{name}", shape, dt))

        def bank(name, dt=F32):
            return ctx.enter_context(nc.psum_tensor(f"e_{name}", [P, 2048 // (4 if dt == F32 else 2)], dt))

        turn = [bank("turn0", F16), bank("turn1", F16)]
        gate_ps, up_ps, weight_ps, route_ps = (bank(n) for n in ("gate_ps", "up_ps", "weight_ps", "route_ps"))
        out = [bank("out0"), bank("out1")]
        wt = {name: sb(f"{name}_t", [P, 2, DC, EXPERTS * P], F16) for name in ("gate", "up")}
        down_t = sb("down_t", [P, 2, EXPERTS, D], F16)
        router = sb("router", [P, 2, DC, EXPERTS], F16)
        bias = sb("bias", [P, EXPERTS])
        select = sb("select", [4 * EXPERTS, EXPERTS, P], F16)
        before4 = sb("before4", [P, EGROUPS, EGROUPS])
        before8 = sb("before8", [P, EXPERTS, EXPERTS])
        res_gate = sb("res_gate", [P, 1])

        with ExitStack() as prep:
            raw = [prep.enter_context(nc.sbuf_tensor(f"e_raw{n}", [P, EXPERTS, D], F32)) for n in range(3)]
            hi = prep.enter_context(nc.sbuf_tensor("e_hi", [P, EXPERTS, D], F16))
            lo = prep.enter_context(nc.sbuf_tensor("e_lo", [P, EXPERTS, D], F16))
            raw_r = prep.enter_context(nc.sbuf_tensor("e_raw_r", [P, DC, EXPERTS], F32))
            loaded = [sem(f"loaded{n}") for n in range(4)]
            chain, turned, copied, const_ok, part_ok, scaled_ok, route_ok = (sem(n) for n in (
                "chain", "turned", "copied", "const_ok", "part_ok", "scaled_ok", "route_ok"))
            block = prep.enter_context(nc.Block())

            @block.sync
            def _(sp):
                for n, name in enumerate(("L1_ffn_gate_proj", "L1_ffn_up_proj")):
                    sp.dma_start(raw[n][:], io[name].rearrange("e i d -> i e d")).then_inc(loaded[n], 16)
                down = io["L1_ffn_down_proj"].rearrange("e (c p) i -> c p e i", p=P)
                for c in range(DC):
                    sp.dma_start(raw[2][:, :, c * P:(c + 1) * P], down[c]).then_inc(loaded[2], 16)
                with nc.allow_non_contiguous_dma(reason="small"):
                    for c in range(DC):
                        sp.dma_start(raw_r[:, c, :], io["L1_ffn_gate_weight"][:, c * P:(c + 1) * P].rearrange("e p -> p e")).then_inc(loaded[3], 16)
                sp.dma_start(bias[:], io["L1_ffn_e_score_correction_bias"].rearrange("(a n) -> a n", a=1).broadcast_to([P, EXPERTS])).then_inc(loaded[3], 16)
                sp.wait_ge(loaded[3], 48)

            @block.gpsimd
            def _(pool):
                nc.gpsimd.memset(select[:], 1.0 / (WS * WS)).then_inc(const_ok, 1)
                nc.gpsimd.memset(before4[:], 1.0).then_inc(const_ok, 1)
                nc.gpsimd.memset(before8[:], 1.0).then_inc(const_ok, 1)
                pool.wait_ge(const_ok, 3)
                nc.gpsimd.affine_select(out=before4[:], in_=before4[:], pattern=[[1, EGROUPS], [-1, EGROUPS]], compare_op=ALU.is_gt,
                                        fill=0.0, base=0, channel_multiplier=0).then_inc(const_ok, 1)
                nc.gpsimd.affine_select(out=before8[:], in_=before8[:], pattern=[[1, EXPERTS], [-1, EXPERTS]], compare_op=ALU.is_gt,
                                        fill=0.0, base=0, channel_multiplier=0).then_inc(const_ok, 1)
                nc.gpsimd.affine_select(out=select[:], in_=select[:], pattern=[[-1, EXPERTS], [0, P]], compare_op=ALU.is_equal,
                                        fill=0.0, base=0, channel_multiplier=1).then_inc(const_ok, 1)
                pool.wait_ge(const_ok, 6)
                nc.gpsimd.affine_select(out=select[:], in_=select[:], pattern=[[-1, EXPERTS], [0, P]], compare_op=ALU.not_equal,
                                        fill=1.0 / (WS * WS), base=-EXPERTS, channel_multiplier=1).then_inc(const_ok, 1)
                pool.wait_ge(const_ok, 7)

            @block.scalar
            def _(act):
                for n in range(3):
                    act.wait_ge(scaled_ok, n + 1)
                    reach(act, turned, 4 * n)
                    nc.scalar.activation(hi[:], raw[n][:], ACT.Copy).then_inc(part_ok, 1)

            @block.vector
            def _(dve):
                for n in range(3):
                    dve.wait_ge(loaded[n], 16 if n < 2 else 32)
                    nc.vector.tensor_scalar(raw[n][:], raw[n][:], WS, None, ALU.mult).then_inc(scaled_ok, 1)
                dve.wait_ge(loaded[3], 48)
                nc.vector.tensor_copy(router[:, 0, :, :], raw_r[:]).then_inc(route_ok, 1)
                dve.wait_ge(route_ok, 1)
                nc.vector.tensor_tensor(router[:, 1, :, :], raw_r[:], router[:, 0, :, :], ALU.subtract).then_inc(route_ok, 1)
                nc.vector.tensor_scalar(res_gate[:], m.tanh_gates[:, 3:4], 1.0 / WS, None, ALU.mult).then_inc(route_ok, 1)
                for n in range(3):
                    dve.wait_ge(part_ok, n + 1)
                    reach(dve, turned, 4 * n)
                    nc.vector.tensor_tensor(lo[:], raw[n][:], hi[:], ALU.subtract).then_inc(chain, 1)
                    for k in range(4):
                        dve.wait_ge(turned, 4 * n + k + 1)
                        part, c = k // 2, k % 2
                        if n < 2:
                            dst = wt[("gate", "up")[n]][:, part, c, :]
                        else:
                            dst = down_t[:, part, :, c * P:(c + 1) * P]
                        src = turn[k % 2][:, :] if n < 2 else turn[k % 2][:, :].rearrange("p (e k) -> p e k", k=P)
                        nc.vector.tensor_copy(dst, src).then_inc(copied, 1)
                dve.wait_ge(copied, 12)
                dve.wait_ge(route_ok, 3)

            @block.tensor
            def _(pe):
                for n in range(3):
                    pe.wait_ge(chain, n + 1)
                    for k in range(4):
                        part, c = k // 2, k % 2
                        reach(pe, copied, 4 * n + k - 1)
                        for e in range(EXPERTS):
                            last = nc.tensor.transpose(turn[k % 2][:, e * P:(e + 1) * P], (hi, lo)[part][:, e, c * P:(c + 1) * P], m.ident16[:, :])
                        last.then_inc(turned, 1)

        normed = sb("normed", [P, GT, D])
        n_parts = sb("n_parts", [P, 2, GT, D], F16)
        n_turned = sb("n_turned", [P, 2, DC, 2, GT, P], F16)
        score = sb("score", [P, GT, EXPERTS])
        choice = sb("choice", [P, GT, EXPERTS])
        group = sb("group", [P, GT, EGROUPS])
        above4, equal4 = sb("above4", [P, GT, EGROUPS, EGROUPS]), sb("equal4", [P, GT, EGROUPS, EGROUPS])
        above8, equal8 = sb("above8", [P, GT, EXPERTS, EXPERTS]), sb("equal8", [P, GT, EXPERTS, EXPERTS])
        rank4, rank8 = sb("rank4", [P, GT, EGROUPS]), sb("rank8", [P, GT, EXPERTS])
        total = sb("total", [P, GT])
        weight = sb("weight", [P, GT, EXPERTS])
        w_parts = sb("w_parts", [P, GT, 2, EXPERTS], F16)
        w_turned = sb("w_turned", [4 * EXPERTS, 2, GW], F16)
        sig = sb("sig", [P, 2, GW])
        act1, act2, act3 = sb("act1", [P, 2, GW]), sb("act2", [P, 2, GW]), sb("act3", [P, 2, GW])
        a_parts = sb("a_parts", [P, 2, 2, GW], F16)

        (norm_ok, hi_ok, lo_ok, t_turn, t_copied, logits_ok, score_ok, chain, w_ok, w_turn, w_copied, gate_ok, up_ok, weight_ok,
         sig_ok, act1_ok, act2_ok, act3_ok, ahi_ok, alo_ok, down_ok, out_ok, fin_ok, stored, w_zero) = (sem(n) for n in (
             "norm_ok", "hi_ok", "lo_ok", "t_turn", "t_copied", "logits_ok", "score_ok", "route_chain", "w_ok", "w_turn", "w_copied",
             "gate_ok", "up_ok", "weight_ok", "sig_ok", "act1_ok", "act2_ok", "act3_ok", "ahi_ok", "alo_ok", "down_ok", "out_ok",
             "fin_ok", "stored", "w_zero"))
        CH = 19

        with nc.Block() as block:

            @block.sync
            def _(sp):
                view = io["out"].rearrange("b s d -> s b d")

                def step(j, u):
                    if inside(j - 2, GROUPS):
                        t = j - 2
                        reach(sp, fin_ok, t + 1)
                        sp.dma_start(view[:, (t * GT):(t * GT) + GT, :] if isinstance(t, int) else view[:, bass.ds(t * GT, GT), :],
                                     m.x[:, (t * GT):(t * GT) + GT, :] if isinstance(t, int) else m.x[:, bass.ds(t * GT, GT), :]).then_inc(stored, 16)

                run_steps(sp, step, 2, head, GROUPS, lag)
                sp.wait_ge(stored, 16 * GROUPS)

            @block.tensor
            def _(pe):
                terms = ((0, 0), (0, 1), (1, 0))

                def product(dst, w, u, e):
                    for n, (part, wpart) in enumerate(terms):
                        for d in range(DC):
                            last = nc.tensor.matmul(dst[:, :], w[:, wpart, d, e * P:(e + 1) * P],
                                                    n_turned[:, u % 2, d, part, :, :].rearrange("p t k -> p (t k)"),
                                                    start=(n == 0 and d == 0), stop=(n == 2 and d == DC - 1))
                    return last

                def down(t, u, e):
                    n = t * EXPERTS + e
                    reach(pe, alo_ok, n + 1)
                    if e == 0:
                        reach(pe, fin_ok, t)
                    for k in range(GT):
                        dst = out[k // 2][:, (k % 2) * D:(k % 2 + 1) * D]
                        for s, (part, wpart) in enumerate(terms):
                            last = nc.tensor.matmul(dst, a_parts[:, e % 2, part, k * P:(k + 1) * P], down_t[:, wpart, e, :],
                                                    start=(e == 0 and s == 0 and k % 2 == 0), stop=(e == EXPERTS - 1 and s == 2),
                                                    skip_group_check=True)
                    last.then_inc(down_ok, 1)
                    return last

                def step(j, u):
                    if inside(j, GROUPS):
                        reach(pe, lo_ok, j + 1)
                        for d in range(DC):
                            reach(pe, t_copied, 2 * j + (d - 1))
                            for part in range(2):
                                for k in range(GT):
                                    n = part * GT + k
                                    last = nc.tensor.transpose(turn[d][:, n * P:(n + 1) * P], n_parts[:, part, k, d * P:(d + 1) * P], m.ident16[:, :])
                            last.then_inc(t_turn, 1)
                    for e in range(EXPERTS + 1):
                        if e < EXPERTS and inside(j - 1, GROUPS):
                            n = (j - 1) * EXPERTS + e
                            if e == 0:
                                reach(pe, w_copied, j)
                            reach(pe, act1_ok, n)
                            product(gate_ps, wt["gate"], u - 1, e).then_inc(gate_ok, 1)
                            reach(pe, act2_ok, n)
                            product(up_ps, wt["up"], u - 1, e).then_inc(up_ok, 1)
                            reach(pe, act3_ok, n)
                            nc.tensor.matmul(weight_ps[:, :], select[:, e, :], w_turned[:, (u - 1) % 2, :], start=True, stop=True).then_inc(weight_ok, 1)
                        if e == 1 and inside(j, GROUPS):
                            reach(pe, t_copied, 2 * j + 2)
                            reach(pe, w_copied, j)
                            for k in range(GT):
                                for s, (part, wpart) in enumerate(((0, 0), (0, 1), (1, 0), (1, 1))):
                                    for d in range(DC):
                                        last = nc.tensor.matmul(route_ps[:, k * EXPERTS:(k + 1) * EXPERTS], n_turned[:, u % 2, d, part, k, :],
                                                                router[:, wpart, d, :], start=(s == 0 and d == 0), stop=(s == 3 and d == DC - 1))
                            last.then_inc(logits_ok, 1)
                        if e == 5 and inside(j, GROUPS):
                            reach(pe, w_ok, j + 1)
                            for k in range(GT):
                                last = nc.tensor.transpose(route_ps[0:2 * EXPERTS, :].bitcast(F16)[:, k * P:(k + 1) * P],
                                                           w_parts[:, k, :, :].rearrange("p a e -> p (a e)"), m.ident16[:, :])
                            last.then_inc(w_turn, 1)
                        if e >= 1 and inside(j - 1, GROUPS):
                            down(j - 1, u - 1, e - 1)

                run_steps(pe, step, 2, head, GROUPS, lag)

            @block.vector
            def _(dve):
                nc.vector.memset(w_turned[:], 0.0).then_inc(w_zero, 1)
                dve.wait_ge(w_zero, 1)

                def expert(t, u, e):
                    n = t * EXPERTS + e
                    p = e % 2
                    reach(dve, sig_ok, n + 1)
                    nc.vector.tensor_tensor(act1[:, p, :], sig[:, p, :], gate_ps[:, :], ALU.mult).then_inc(act1_ok, 1)
                    reach(dve, up_ok, n + 1)
                    reach(dve, act1_ok, n + 1)
                    nc.vector.tensor_tensor(act2[:, p, :], act1[:, p, :], up_ps[:, :], ALU.mult).then_inc(act2_ok, 1)
                    reach(dve, weight_ok, n + 1)
                    reach(dve, act2_ok, n + 1)
                    reach(dve, alo_ok, n - 1)
                    nc.vector.tensor_tensor(act3[:, p, :], act2[:, p, :], weight_ps[:, :], ALU.mult).then_inc(act3_ok, 1)

                def route(j, u):
                    step = [0]

                    def then(instruction):
                        step[0] += 1
                        instruction.then_inc(chain, 1)
                        reach(dve, chain, j * CH + step[0])

                    def ranks(values, count, above, equal, before, rank):
                        theirs = values[:, :, None, :].broadcast_to([P, GT, count, count])
                        own = values[:, :, :, None].broadcast_to([P, GT, count, count])
                        first = before[:, None, :, :].broadcast_to([P, GT, count, count])
                        then(nc.vector.tensor_tensor(above[:], theirs, own, ALU.is_gt))
                        then(nc.vector.tensor_tensor(equal[:], theirs, own, ALU.is_equal))
                        then(nc.vector.tensor_tensor(equal[:], equal[:], first, ALU.mult))
                        then(nc.vector.tensor_tensor(above[:], above[:], equal[:], ALU.add))
                        then(nc.vector.tensor_reduce(rank[:], above[:], AX.X, ALU.add))

                    reach(dve, score_ok, j + 1)
                    then(nc.vector.tensor_tensor(choice[:], score[:], bias[:, None, :].broadcast_to([P, GT, EXPERTS]), ALU.add))
                    then(nc.vector.tensor_tensor(group[:], choice[:, :, 0::2], choice[:, :, 1::2], ALU.add))
                    ranks(group, EGROUPS, above4, equal4, before4, rank4)
                    then(nc.vector.tensor_scalar(rank4[:], rank4[:], float(TOP), None, ALU.is_lt))
                    then(nc.vector.tensor_tensor(choice[:].rearrange("p t (g s) -> p t g s", s=2), choice[:].rearrange("p t (g s) -> p t g s", s=2),
                                                 rank4[:, :, :, None].broadcast_to([P, GT, EGROUPS, 2]), ALU.mult))
                    ranks(choice, EXPERTS, above8, equal8, before8, rank8)
                    then(nc.vector.scalar_tensor_tensor(out=weight[:], in0=rank8[:], scalar=float(TOP), in1=score[:], op0=ALU.is_lt, op1=ALU.mult))
                    then(nc.vector.tensor_reduce(total[:], weight[:], AX.X, ALU.add))
                    then(nc.vector.tensor_scalar(total[:], total[:], 1e-20, None, ALU.add))
                    then(nc.vector.reciprocal(total[:], total[:]))
                    then(nc.vector.tensor_tensor(weight[:], weight[:], total[:, :, None].broadcast_to([P, GT, EXPERTS]), ALU.mult))
                    nc.vector.tensor_copy(w_parts[:, :, 0, :], weight[:]).then_inc(w_ok_hi, 1)
                    reach(dve, w_ok_hi, j + 1)
                    nc.vector.tensor_tensor(w_parts[:, :, 1, :], weight[:], w_parts[:, :, 0, :], ALU.subtract).then_inc(w_ok, 1)
                    assert step[0] == CH

                w_ok_hi = sem("w_ok_hi")

                def step(j, u):
                    if inside(j - 2, GROUPS):
                        t = j - 2
                        reach(dve, out_ok_sem, t * EXPERTS + EXPERTS)
                        for k in range(GT):
                            x = m.x[:, t * GT + k, :]
                            last = nc.vector.scalar_tensor_tensor(out=x, in0=out[k // 2][:, (k % 2) * D:(k % 2 + 1) * D],
                                                                  scalar=res_gate[:, 0:1], in1=x, op0=ALU.mult, op1=ALU.add)
                        last.then_inc(fin_ok, 1)
                    if inside(j, GROUPS):
                        reach(dve, lo_ok, j)
                        for k in range(GT):
                            last = nc.vector.tensor_scalar(normed[:, k, :], m.x[:, j * GT + k, :], m.mean[:, j, k:k + 1],
                                                           m.rstd[:, j, k:k + 1], ALU.subtract, ALU.mult)
                        last.then_inc(norm_ok, 1)
                    for e in range(EXPERTS):
                        if inside(j - 1, GROUPS):
                            expert(j - 1, u - 1, e)
                        if e == 0 and inside(j, GROUPS):
                            for d in range(DC):
                                reach(dve, t_turn, 2 * j + (d + 1))
                                nc.vector.tensor_copy(n_turned[:, u % 2, d, :, :, :],
                                                      turn[d][:, :].rearrange("p (a t k) -> p a t k", a=2, t=GT)).then_inc(t_copied, 1)
                        if e == 2 and inside(j, GROUPS):
                            route(j, u)
                        if e == 6 and inside(j, GROUPS):
                            reach(dve, w_turn, j + 1)
                            nc.vector.tensor_copy(w_turned[0:2 * EXPERTS, u % 2, :], route_ps[0:2 * EXPERTS, :].bitcast(F16)[:, 0:GW]).then_inc(w_copied, 1)

                out_ok_sem = down_ok
                run_steps(dve, step, 2, head, GROUPS, lag)

            @block.scalar
            def _(act):
                nc.scalar.preload_act_table(ACT.Sigmoid)

                def step(j, u):
                    if inside(j, GROUPS):
                        reach(act, norm_ok, j + 1)
                        reach(act, t_turn, 2 * j)
                        nc.scalar.activation(n_parts[:, 0, :, :], normed[:], ACT.Copy).then_inc(hi_ok, 1)
                    for e in range(EXPERTS):
                        if inside(j - 1, GROUPS):
                            n = (j - 1) * EXPERTS + e
                            reach(act, gate_ok, n + 1)
                            reach(act, act1_ok, n - 1)
                            nc.scalar.activation(sig[:, e % 2, :], gate_ps[:, :], ACT.Sigmoid, scale=1.0 / WS).then_inc(sig_ok, 1)
                        if e == 1 and inside(j, GROUPS):
                            reach(act, logits_ok, j + 1)
                            reach(act, w_ok, j)
                            nc.scalar.activation(score[:].rearrange("p t e -> p (t e)"), route_ps[:, 0:GT * EXPERTS], ACT.Sigmoid).then_inc(score_ok, 1)
                        if inside(j - 1, GROUPS):
                            reach(act, act3_ok, n + 1)
                            reach(act, down_ok, n - 1)
                            nc.scalar.activation(a_parts[:, e % 2, 0, :], act3[:, e % 2, :], ACT.Copy).then_inc(ahi_ok, 1)

                run_steps(act, step, 2, head, GROUPS, lag)

            @block.gpsimd
            def _(pool):
                def step(j, u):
                    if inside(j, GROUPS):
                        reach(pool, hi_ok, j + 1)
                        nc.gpsimd.tensor_tensor(n_parts[:, 1, :, :], normed[:], n_parts[:, 0, :, :], ALU.subtract).then_inc(lo_ok, 1)
                    for e in range(EXPERTS):
                        if inside(j - 1, GROUPS):
                            reach(pool, ahi_ok, (j - 1) * EXPERTS + (e + 1))
                            nc.gpsimd.tensor_tensor(a_parts[:, e % 2, 1, :], act3[:, e % 2, :], a_parts[:, e % 2, 0, :],
                                                    ALU.subtract).then_inc(alo_ok, 1)

                run_steps(pool, step, 2, head, GROUPS, lag)


def build_program(nc, io):
    with ExitStack() as ctx:
        m = Shared()

        def sb(name, shape, dt=F32):
            return ctx.enter_context(nc.sbuf_tensor(name, shape, dt))

        def sem(name):
            return ctx.enter_context(nc.semaphore(name))

        m.x = sb("x", [P, TILES, D])
        m.gates, m.tanh_gates = sb("gates", [P, 4]), sb("tanh_gates", [P, 4])
        m.ident32, m.ident16 = sb("ident32", [P, P]), sb("ident16", [P, P], F16)
        m.ones32 = sb("ones32", [P, P])
        m.stats = sb("stats", [P, TILES, 6])
        m.mean2 = sb("mean", [P, TILES])
        m.root = sb("root", [P, TILES])
        m.rstd2 = sb("rstd", [P, TILES])
        m.rstd, m.mean = m.rstd2[:, :], m.mean2[:, :]
        with ExitStack() as held:
            m.ctx = held.enter_context(nc.sbuf_tensor("ctx", [P, TILES, D], F32))
            load_stage(nc, io, m, sem)
            deviation_stage(nc, m, sem, "dev0")
            attention_stage(nc, io, m, 0, sem)
            deviation_stage(nc, m, sem, "dev1")
            m.rstd, m.mean = (v[:, :].rearrange("p (j k) -> p j k", k=GT) for v in (m.rstd2, m.mean2))
            bitnet_stage(nc, io, m)
            m.rstd, m.mean = m.rstd2[:, :], m.mean2[:, :]
            deviation_stage(nc, m, sem, "dev2")
            attention_stage(nc, io, m, 1, sem)
            deviation_stage(nc, m, sem, "dev3")
        m.rstd, m.mean = (v[:, :].rearrange("p (j k) -> p j k", k=GT) for v in (m.rstd2, m.mean2))
        expert_stage(nc, io, m)


_INS = ["x", "ctx_1024", "g_xattn", "g_ffn", "L0_ffn_w1", "L0_ffn_conv_w", "L0_ffn_conv_b", "L0_ffn_w2",
        "L1_xattn_Wq", "L1_xattn_Wk", "L1_xattn_Wv", "L1_ffn_gate_weight", "L1_ffn_e_score_correction_bias",
        "L1_ffn_gate_proj", "L1_ffn_up_proj", "L1_ffn_down_proj"]


def kernel(**inputs):
    import numpy as np
    import concourse.bacc as bacc
    from concourse import mybir as mb
    from concourse.bass_utils import run_bass_kernel_spmd

    nc = bacc.Bacc("TRN2", target_bir_lowering=False, num_devices=1)
    arrays, io = {}, {}
    for name in _INS:
        a = np.ascontiguousarray(inputs[name])
        arrays[f"in_{name}"] = a
        io[name] = nc.dram_tensor(f"in_{name}", a.shape, mb.dt.from_np(a.dtype), kind="ExternalInput").ap()
    io["out"] = nc.dram_tensor("out", (TILES, P, D), mb.dt.float32, kind="ExternalOutput").ap()
    build_program(nc, io)
    result = run_bass_kernel_spmd(nc, [arrays], core_ids=[0])
    return result.results[0]["out"]
```

```python
from contextlib import ExitStack

import concourse.bass as bass
from concourse import mybir

F32 = mybir.dt.float32
F16 = mybir.dt.float16
ALU = mybir.AluOpType
ACT = mybir.ActivationFunctionType
AX = mybir.AxisListType

P = 128
TILES = 64
D = 256
DC = D // P
HEADS = 16
DH = D // HEADS
SLOT = 4 * DH
HG = 4
NG = HEADS // HG
PAIRS = HEADS // 2
UNROLL = 8
HID = 1024
HC = HID // P
GT = 4
GROUPS = TILES // GT
GW = GT * P
EXPERTS = 8
EGROUPS = 4
TOP = 2
WS = 32.0
XS = 64.0
LN_EPS = 1e-5
MAGIC = 12582912.0


def reach(engine, semaphore, value):
    if isinstance(value, int) and value <= 0:
        return
    engine.wait_ge(semaphore, value)


def run_steps(engine, step, period, head, count, tail):
    for i in range(head):
        step(i, i % period)
    with engine.Fori(head // period, count // period) as j:
        for u in range(period):
            step(j * period + u, u)
    for i in range(count, count + tail):
        step(i, i % period)


def head_of(g, k):
    return 8 * (g // 2) + 2 * k + g % 2, g % 2


def inside(t, count):
    return not isinstance(t, int) or 0 <= t < count


class Shared:
    pass


def load_stage(nc, io, m, sem):
    chunks = 4
    per = TILES // chunks
    x_in = [sem(f"x_loaded{c}") for c in range(chunks)]
    ctx_in = [sem(f"ctx_loaded{c}") for c in range(chunks)]
    gates_in = sem("gates_loaded")
    const_made = sem("constants_made")
    tanh_made = sem("tanh_made")
    x_view = io["x"].rearrange("b s d -> s b d")
    ctx_view = io["ctx_1024"].rearrange("b s d -> s b d")
    with nc.Block() as block:

        @block.sync
        def _(sp):
            for c in range(chunks):
                sp.dma_start(m.x[:, c * per:(c + 1) * per, :], x_view[:, c * per:(c + 1) * per, :]).then_inc(x_in[c], 16)
            for c in range(chunks):
                sp.wait_ge(ctx_in[c], 16)

        @block.scalar
        def _(act):
            act.dma_start(m.gates[:, 0:2], io["g_xattn"].rearrange("(a n) -> a n", a=1).broadcast_to([P, 2])).then_inc(gates_in, 16)
            act.dma_start(m.gates[:, 2:4], io["g_ffn"].rearrange("(a n) -> a n", a=1).broadcast_to([P, 2])).then_inc(gates_in, 16)
            for c in range(chunks):
                act.dma_start(m.ctx[:, c * per:(c + 1) * per, :], ctx_view[:, c * per:(c + 1) * per, :]).then_inc(ctx_in[c], 16)
            act.wait_ge(gates_in, 32)
            nc.scalar.activation(m.tanh_gates[:, :], m.gates[:, :], ACT.Tanh).then_inc(tanh_made, 1)
            act.wait_ge(tanh_made, 1)

        @block.gpsimd
        def _(pool):
            nc.gpsimd.memset(m.ident32[:, :], 1.0).then_inc(const_made, 1)
            pool.wait_ge(const_made, 1)
            nc.gpsimd.affine_select(out=m.ident32[:, :], in_=m.ident32[:, :], pattern=[[-1, P]], compare_op=ALU.is_equal,
                                    fill=0.0, base=0, channel_multiplier=1).then_inc(const_made, 1)
            pool.wait_ge(const_made, 2)
            nc.gpsimd.tensor_copy(m.ident16[:, :], m.ident32[:, :]).then_inc(const_made, 1)
            nc.gpsimd.memset(m.ones32[:, :], 1.0).then_inc(const_made, 1)
            pool.wait_ge(const_made, 4)

        @block.vector
        def _(dve):
            for c in range(chunks):
                dve.wait_ge(x_in[c], 16)
                with dve.Fori(c * per // UNROLL, (c + 1) * per // UNROLL) as j:
                    for u in range(UNROLL):
                        nc.vector.bn_stats(m.stats[:, j * UNROLL + u, :], m.x[:, j * UNROLL + u, :])


def deviation_stage(nc, m, sem, name):
    joined = sem(f"{name}_joined")
    biased = sem(f"{name}_biased")
    rooted = sem(f"{name}_rooted")
    inverted = sem(f"{name}_inverted")
    with nc.Block() as block:

        @block.vector
        def _(dve):
            even_mean, even_dev, odd_mean, odd_dev = (m.stats[:, :, k] for k in (1, 2, 4, 5))
            nc.vector.tensor_tensor(m.mean[:, :], even_mean, odd_mean, ALU.add).then_inc(joined, 1)
            nc.vector.tensor_tensor(m.root[:, :], even_mean, odd_mean, ALU.subtract).then_inc(joined, 1)
            nc.vector.tensor_tensor(m.rstd[:, :], even_dev, odd_dev, ALU.add).then_inc(joined, 1)
            dve.wait_ge(joined, 3)
            nc.vector.tensor_scalar(m.mean[:, :], m.mean[:, :], 0.5, None, ALU.mult).then_inc(joined, 1)
            nc.vector.scalar_tensor_tensor(out=m.root[:, :], in0=m.root[:, :], scalar=D / 4.0, in1=m.root[:, :],
                                           op0=ALU.mult, op1=ALU.mult).then_inc(joined, 1)
            dve.wait_ge(joined, 5)
            nc.vector.tensor_tensor(m.rstd[:, :], m.rstd[:, :], m.root[:, :], ALU.add).then_inc(joined, 1)
            dve.wait_ge(joined, 6)
            nc.vector.tensor_scalar(m.rstd[:, :], m.rstd[:, :], 1.0 / D, LN_EPS, ALU.mult, ALU.add).then_inc(biased, 1)
            dve.wait_ge(rooted, 1)
            nc.vector.reciprocal(m.rstd[:, :], m.root[:, :]).then_inc(inverted, 1)
            dve.wait_ge(inverted, 1)

        @block.scalar
        def _(act):
            act.wait_ge(biased, 1)
            nc.scalar.activation(m.root[:, :], m.rstd[:, :], ACT.Sqrt).then_inc(rooted, 1)


def projection_weights(nc, io, m, w_hi, w_lo, psum, sem):
    with ExitStack() as ctx:
        raw = ctx.enter_context(nc.sbuf_tensor("proj_raw", [P, 3, DC, D], F32))
        scaled = ctx.enter_context(nc.sbuf_tensor("proj_scaled", [P, 3, DC, D], F32))
        hi = ctx.enter_context(nc.sbuf_tensor("proj_hi", [P, 3, DC, D], F16))
        lo = ctx.enter_context(nc.sbuf_tensor("proj_lo", [P, 3, DC, D], F16))
        loaded, scaled_ok, hi_ok, lo_ok, turned, copied = (sem(f"proj_{n}") for n in (
            "loaded", "scaled_ok", "hi_ok", "lo_ok", "turned", "copied"))
        block = ctx.enter_context(nc.Block())

        @block.sync
        def _(sp):
            for n, name in enumerate(("L1_xattn_Wq", "L1_xattn_Wk", "L1_xattn_Wv")):
                sp.dma_start(raw[:, n, :, :], io[name].rearrange("(c p) d -> p c d", p=P)).then_inc(loaded, 16)
            sp.wait_ge(loaded, 48)

        @block.vector
        def _(dve):
            dve.wait_ge(loaded, 48)
            nc.vector.tensor_scalar(scaled[:], raw[:], WS, None, ALU.mult).then_inc(scaled_ok, 1)
            dve.wait_ge(hi_ok, 1)
            nc.vector.tensor_tensor(lo[:], scaled[:], hi[:], ALU.subtract).then_inc(lo_ok, 1)
            for n in range(4):
                dve.wait_ge(turned, n + 1)
                dst = (w_hi, w_lo)[n // 2][:, n % 2, :]
                nc.vector.tensor_copy(dst, psum[n % 2][:, 0:6 * P]).then_inc(copied, 1)
            dve.wait_ge(copied, 4)

        @block.scalar
        def _(act):
            act.wait_ge(scaled_ok, 1)
            nc.scalar.activation(hi[:], scaled[:], ACT.Copy).then_inc(hi_ok, 1)

        @block.tensor
        def _(pe):
            for n in range(4):
                pe.wait_ge(lo_ok, 1)
                reach(pe, copied, n - 1)
                src = (hi, lo)[n // 2]
                for k in range(6):
                    last = nc.tensor.transpose(psum[n % 2][:, k * P:(k + 1) * P],
                                               src[:, k // 2, k % 2, (n % 2) * P:(n % 2 + 1) * P], m.ident16[:, :])
                last.then_inc(turned, 1)


def attention_stage(nc, io, m, layer, sem_scope):
    L = layer
    scale = WS if layer else 1.0
    TL, SL, EL, VL = (n + L for n in (1, 2, 3, 4))
    last_lag = 1 + VL
    head = UNROLL * (-(-last_lag // UNROLL))
    with ExitStack() as ctx:
        def sem(name):
            return ctx.enter_context(nc.semaphore(f"a{layer}_{name}"))

        def sb(name, shape, dt):
            return ctx.enter_context(nc.sbuf_tensor(f"a{layer}_{name}", shape, dt))

        def bank(name, dt=F32):
            return ctx.enter_context(nc.psum_tensor(f"a{layer}_{name}", [P, 2048 // (4 if dt == F32 else 2)], dt))

        turn = [bank("turn0", F16), bank("turn1", F16)]
        if layer:
            w_hi, w_lo = sb("w_hi", [P, DC, 3 * D], F16), sb("w_lo", [P, DC, 3 * D], F16)
            projection_weights(nc, io, m, w_hi, w_lo, turn, sem)
        score = [bank(f"score{n}") for n in range(1 if layer else 2)]
        score_t = [bank("score_t0"), bank("score_t1")]
        out = [bank(f"out{n}") for n in range(1 if layer else 2)]
        if layer:
            q_ps, kv_ps = bank("q_ps"), bank("kv_ps")

        KR, NR = (2, 1) if layer else (UNROLL, 2)
        q_stack = sb("q_stack", [P, 2, HEADS, 4, DH], F16)
        k_stack = sb("k_stack", [P, KR, HEADS, 4, DH], F16)
        q_turned = sb("q_turned", [P, 4, HEADS // 2, P], F16)
        k_turned = sb("k_turned", [P, 4, HEADS // 2, P], F16)
        normed = sb("normed", [P, NR, D], F32)
        exp32 = sb("exp32", [P, NG, HG * P], F32)
        exp_hi = sb("exp_hi", [P, 2, NG, HG, P], F16)
        exp_lo = sb("exp_lo", [P, 2, NG, HG, P], F16)
        maxes = sb("maxes", [P, HEADS], F32)
        neg_max = sb("neg_max", [P, 2, 2, SLOT], F16)
        neg_max_t = sb("neg_max_t", [P, 2, P], F16)
        spread = sb("spread", [P, PAIRS, P], F16)
        rsum = sb("rsum", [P, HEADS], F32)
        mixed = sb("mixed", [P, HEADS, DH], F32)
        gate = sb("gate", [P, 1], F32)
        if layer:
            split = sb("split", [P, 2, 4, D], F16)
            split_t = sb("split_t", [P, 2, 4 * DC, P], F16)
            v_hi = sb("v_hi", [P, UNROLL, HEADS, DH + 1], F16)
            v_lo = sb("v_lo", [P, UNROLL, HEADS, DH], F16)

        made, nf_ok, qh_ok, ql_ok, kh_ok, kl_ok = (sem(n) for n in ("made", "nf_ok", "qh_ok", "ql_ok", "kh_ok", "kl_ok"))
        q_turn, k_turn, m_turn = sem("q_turn"), sem("k_turn"), sem("m_turn")
        q_copied, k_copied, m_copied = sem("q_copied"), sem("k_copied"), sem("m_copied")
        scores_ok, max_ok, neg_ok = sem("scores_ok"), sem("max_ok"), sem("neg_ok")
        scores_t_ok, exp_ok, exp_lo_ok = sem("scores_t_ok"), sem("exp_ok"), sem("exp_lo_ok")
        values_ok, out_read, fin_ok = sem("values_ok"), sem("out_read"), sem("fin_ok")
        if layer:
            nh_ok, nl_ok, ch_ok, cl_ok = sem("nh_ok"), sem("nl_ok"), sem("ch_ok"), sem("cl_ok")
            s_turn, s_copied, q_proj, kv_proj, vl_ok = sem("s_turn"), sem("s_copied"), sem("q_proj"), sem("kv_proj"), sem("vl_ok")

        with nc.Block() as block:

            @block.vector
            def _(dve):
                nc.vector.memset(q_stack[:], 0.0).then_inc(made, 1)
                nc.vector.memset(neg_max[:], 0.0).then_inc(made, 1)
                nc.vector.memset(k_stack[:], 0.0).then_inc(made, 1)
                dve.wait_ge(made, 3)
                nc.vector.memset(k_stack[:, :, :, 3, 0:1], 1.0).then_inc(made, 1)
                nc.vector.tensor_scalar(gate[:], m.tanh_gates[:, layer:layer + 1], 1.0 / scale, None, ALU.mult).then_inc(made, 1)
                if layer:
                    nc.vector.memset(v_hi[:, :, :, DH:DH + 1], 1.0).then_inc(made, 1)
                dve.wait_ge(made, 5 + L)

            @block.gpsimd
            def _(pool):
                nc.gpsimd.memset(spread[:], scale * scale).then_inc(kl_ok, 1)
                pool.wait_ge(kl_ok, 1)
                nc.gpsimd.affine_select(out=spread[:], in_=spread[:], pattern=[[-1, PAIRS], [0, P]],
                                        compare_op=ALU.is_equal, fill=0.0, base=0, channel_multiplier=1).then_inc(kl_ok, 1)
                pool.wait_ge(kl_ok, 2)
                nc.gpsimd.affine_select(out=spread[:], in_=spread[:], pattern=[[-1, PAIRS], [0, P]],
                                        compare_op=ALU.not_equal, fill=scale * scale, base=-SLOT, channel_multiplier=1).then_inc(kl_ok, 1)
                pool.wait_ge(kl_ok, 3)
        KL0 = 3

        with nc.Block() as block:

            heads = lambda ap: ap.rearrange("p (h d) -> p h d", h=HEADS)
            twice = lambda ap: ap.rearrange("p (h a d) -> p h a d", h=HEADS, a=1).broadcast_to([P, HEADS, 2, DH])

            @block.tensor
            def _(pe):
                def turn_maxima(t, u):
                    reach(pe, neg_ok, t + 1)
                    nc.tensor.transpose(score[-1][:, :].bitcast(F16)[:, 0:P], neg_max[:, u % 2, :, :].rearrange("p r n -> p (r n)"),
                                        m.ident16[:, :]).then_inc(m_turn, 1)

                def do_scores(t, u, g, after_turn):
                    if g == 0:
                        reach(pe, k_copied, t + 1)
                    reach(pe, max_ok, t * NG + (g + 1 - len(score)))
                    if g == len(score) - 1 and after_turn:
                        reach(pe, m_copied, t)
                    for k in range(HG):
                        h, half = head_of(g, k)
                        r = SLOT * half
                        last = nc.tensor.matmul(score[g % len(score)][:, k * P:(k + 1) * P], q_turned[r:r + SLOT, u % 4, h // 2, :],
                                                k_turned[r:r + SLOT, u % 4, h // 2, :], start=True, stop=True)
                    last.then_inc(scores_ok, 1)

                def do_scores_t(t, u, g):
                    if g == 0:
                        reach(pe, m_copied, t + 1)
                    reach(pe, exp_ok, t * NG + (g - 1))
                    for k in range(HG):
                        h, half = head_of(g, k)
                        r = SLOT * half
                        dst = score_t[g % 2][:, k * P:(k + 1) * P]
                        nc.tensor.matmul(dst, k_turned[r:r + SLOT, u % 4, h // 2, :], q_turned[r:r + SLOT, u % 4, h // 2, :],
                                         start=True, stop=False)
                        last = nc.tensor.matmul(dst, spread[r:r + SLOT, h // 2, :], neg_max_t[r:r + SLOT, u % 2, :], start=False, stop=True)
                    last.then_inc(scores_t_ok, 1)

                def do_values(t, u, g):
                    reach(pe, exp_lo_ok, t * NG + (g + 1))
                    if g == 0:
                        reach(pe, out_read, t + (1 - len(out)))
                    for k in range(HG):
                        h, _ = head_of(g, k)
                        c = h * (DH + 1)
                        dst = out[u % len(out)]
                        if layer:
                            vh, vl = v_hi[:, u, h, :], v_lo[:, u, h, :]
                        else:
                            one = k_stack[:, u, h, :, :].rearrange("p a d -> p (a d)")
                            vh, vl = one[:, 2 * DH:3 * DH + 1], one[:, DH:2 * DH]
                        nc.tensor.matmul(dst[:, c:c + DH + 1], exp_hi[:, u % 2, g, k, :], vh, start=True, stop=False)
                        nc.tensor.matmul(dst[:, c:c + DH], exp_hi[:, u % 2, g, k, :], vl, start=False, stop=False)
                        last = nc.tensor.matmul(dst[:, c:c + DH + 1], exp_lo[:, u % 2, g, k, :], vh, start=False, stop=True)
                    if g == NG - 1:
                        last.then_inc(values_ok, 1)

                def turn_stack(dst, stack, signal):
                    for n in range(PAIRS):
                        last = nc.tensor.transpose(dst[:, n * P:(n + 1) * P], stack[:, 2 * n:2 * n + 2, :, :].rearrange("p h a d -> p (h a d)"),
                                                   m.ident16[:, :])
                    last.then_inc(signal, 1)

                def turn_q(i, t, u):
                    reach(pe, ql_ok, t + 1)
                    if layer and inside(i - 1, TILES):
                        reach(pe, s_copied, i)
                    else:
                        reach(pe, q_copied, t)
                    turn_stack(turn[0], q_stack[:, u % 2, :, :, :], q_turn)

                def turn_k(t, u):
                    reach(pe, kl_ok, t + (1 + KL0))
                    reach(pe, k_copied, t)
                    turn_stack(turn[1], k_stack[:, u % KR, :, :, :], k_turn)

                if layer:
                    parts = ((0, w_hi), (0, w_lo), (2, w_hi))

                    def project(dst, first, cols, u, source, signal):
                        for n, (part, w) in enumerate(parts):
                            for c in range(DC):
                                last = nc.tensor.matmul(dst[:, 0:cols], split_t[:, u % 2, (part + source) * DC + c, :],
                                                        w[:, c, first:first + cols], start=(n == 0 and c == 0), stop=(n == 2 and c == DC - 1))
                        last.then_inc(signal, 1)

                def step(i, u):
                    run_turn, run_scores, run_exps, run_values = (inside(i - lag, TILES) for lag in (TL, SL, EL, VL))
                    run_project = layer and inside(i - 1, TILES)
                    uT, uS, uE, uV = ((u - lag) % UNROLL for lag in (TL, SL, EL, VL))
                    if run_exps:
                        turn_maxima(i - EL, uE)
                    if run_project:
                        reach(pe, s_copied, i)
                        reach(pe, ql_ok, i - 1)
                        project(q_ps, 0, D, (u - 1) % UNROLL, 0, q_proj)
                    for g in range(NG):
                        if run_values and layer and g == 0:
                            do_values(i - VL, uV, g)
                        if run_scores:
                            do_scores(i - SL, uS, g, run_exps)
                        if g == 1 and run_turn:
                            turn_q(i, i - TL, uT)
                        if g == 2 and run_project:
                            reach(pe, vl_ok, i - 1)
                            project(kv_ps, D, 2 * D, (u - 1) % UNROLL, 1, kv_proj)
                        if run_values and not (layer and g == 0):
                            do_values(i - VL, uV, g)
                        if g == 3 and layer and inside(i, TILES):
                            reach(pe, nl_ok, i + 1)
                            reach(pe, cl_ok, i + 1)
                            if run_turn:
                                reach(pe, q_copied, i - (TL - 1))
                            else:
                                reach(pe, s_copied, i)
                            for n in range(4 * DC):
                                last = nc.tensor.transpose(turn[0][:, n * P:(n + 1) * P],
                                                           split[:, u % 2, n // DC, (n % DC) * P:(n % DC + 1) * P], m.ident16[:, :])
                            last.then_inc(s_turn, 1)
                        if run_exps:
                            do_scores_t(i - EL, uE, g)
                        if g == (1 if layer else 2) and run_turn:
                            turn_k(i - TL, uT)

                run_steps(pe, step, UNROLL, head, TILES, last_lag)

            @block.vector
            def _(dve):
                def take_max(t, g):
                    reach(dve, scores_ok, t * NG + (g + 1))
                    nc.vector.tensor_reduce(maxes[:, g * HG:(g + 1) * HG],
                                            score[g % len(score)][:, :].rearrange("p (h k) -> p h k", h=HG),
                                            AX.X, ALU.max).then_inc(max_ok, 1)

                def step(i, u):
                    run_stats = inside(i - 1 - VL, TILES)
                    run_front, run_project = inside(i, TILES), layer and inside(i - 1, TILES)
                    run_turn, run_scores, run_exps, run_values = (inside(i - lag, TILES) for lag in (TL, SL, EL, VL))
                    uT, uS, uE, uV = ((u - lag) % UNROLL for lag in (TL, SL, EL, VL))
                    if run_exps:
                        reach(dve, m_turn, i - (EL - 1))
                        nc.vector.tensor_copy(neg_max_t[:, uE % 2, :], score[-1][:, :].bitcast(F16)[:, 0:P]).then_inc(m_copied, 1)
                    if run_stats:
                        t = i - (1 + VL)
                        reach(dve, out_read, t + 1)
                        nc.vector.scalar_tensor_tensor(out=m.x[:, t, :], in0=mixed[:].rearrange("p h d -> p (h d)"), scalar=gate[:, 0:1],
                                                       in1=m.x[:, t, :], op0=ALU.mult, op1=ALU.add).then_inc(fin_ok, 1)
                    if run_front:
                        if layer:
                            reach(dve, nh_ok, i)
                            reach(dve, nl_ok, i)
                        else:
                            reach(dve, qh_ok, i - 1)
                            reach(dve, ql_ok, i - 1)
                        nc.vector.tensor_scalar(normed[:, u % NR, :], m.x[:, i, :], m.mean[:, bass.ds(i, 1)], m.rstd[:, bass.ds(i, 1)],
                                                ALU.subtract, ALU.mult).then_inc(nf_ok, 1)
                    if run_stats:
                        reach(dve, fin_ok, t * 3 + 2)
                    if run_scores:
                        reach(dve, neg_ok, i - SL)
                        take_max(i - SL, 0)
                    if layer and inside(i - 2, TILES):
                        reach(dve, kh_ok, i - 1)
                        nc.vector.scalar_tensor_tensor(out=k_stack[:, (u - 2) % 2, :, 1, :], in0=heads(kv_ps[:, 0:D]), scalar=0.0,
                                                       in1=k_stack[:, (u - 2) % 2, :, 0, :], op0=ALU.max, op1=ALU.subtract).then_inc(kl_ok, 1)
                        nc.vector.scalar_tensor_tensor(out=v_lo[:, (u - 2) % UNROLL, :, :], in0=heads(kv_ps[:, D:2 * D]), scalar=0.0,
                                                       in1=v_hi[:, (u - 2) % UNROLL, :, 0:DH], op0=ALU.max, op1=ALU.subtract).then_inc(vl_ok, 1)
                    if run_project:
                        reach(dve, qh_ok, i)
                        nc.vector.scalar_tensor_tensor(out=q_stack[:, (u - 1) % 2, :, 2, :], in0=heads(q_ps[:, 0:D]), scalar=0.0,
                                                       in1=q_stack[:, (u - 1) % 2, :, 0, :], op0=ALU.max, op1=ALU.subtract).then_inc(ql_ok, 1)
                    if run_scores:
                        take_max(i - SL, 1)
                    if run_stats:
                        nc.vector.bn_stats(m.stats[:, t, :], m.x[:, t, :]).then_inc(fin_ok, 1)
                    if run_turn:
                        reach(dve, q_turn, i - (TL - 1))
                        nc.vector.tensor_copy(q_turned[:, uT % 4, :, :], turn[0][:, :].rearrange("p (n k) -> p n k", k=P)).then_inc(q_copied, 1)
                    if run_front:
                        if layer:
                            reach(dve, nh_ok, i + 1)
                            nc.vector.tensor_tensor(split[:, u % 2, 2, :], normed[:, u % NR, :], split[:, u % 2, 0, :],
                                                    ALU.subtract).then_inc(nl_ok, 1)
                        else:
                            reach(dve, qh_ok, i + 1)
                            nc.vector.tensor_tensor(q_stack[:, u % 2, :, 2, :], heads(normed[:, u % NR, :]), q_stack[:, u % 2, :, 0, :],
                                                    ALU.subtract).then_inc(ql_ok, 1)
                    if run_scores:
                        take_max(i - SL, 2)
                    if run_turn:
                        reach(dve, k_turn, i - (TL - 1))
                        nc.vector.tensor_copy(k_turned[:, uT % 4, :, :], turn[1][:, :].rearrange("p (n k) -> p n k", k=P)).then_inc(k_copied, 1)
                    if run_scores:
                        take_max(i - SL, 3)
                        reach(dve, max_ok, (i - SL) * NG + NG)
                        nc.vector.tensor_scalar(neg_max[:, uS % 2, :, 0:PAIRS].rearrange("p r (a k) -> p r a k", k=HG),
                                                maxes[:, :].rearrange("p (a r k) -> p r a k", r=2, k=HG), -1.0 / (scale * scale), None,
                                                ALU.mult).then_inc(neg_ok, 1)
                    if layer and run_front:
                        reach(dve, s_turn, i + 1)
                        nc.vector.tensor_copy(split_t[:, u % 2, :, :], turn[0][:, :].rearrange("p (n k) -> p n k", k=P)).then_inc(s_copied, 1)
                    if run_values:
                        t = i - VL
                        reach(dve, values_ok, t + 1)
                        sums = out[uV % len(out)][:, 0:HEADS * (DH + 1)].rearrange("p (h d) -> p h d", h=HEADS)
                        nc.vector.reciprocal(rsum[:, :], sums[:, :, DH]).then_inc(fin_ok, 1)
                        reach(dve, fin_ok, t * 3 + 1)
                        nc.vector.tensor_tensor(mixed[:], sums[:, :, 0:DH], rsum[:, :, None].broadcast_to([P, HEADS, DH]),
                                                ALU.mult).then_inc(out_read, 1)

                run_steps(dve, step, UNROLL, head, TILES, last_lag)

            @block.scalar
            def _(act):
                nc.scalar.preload_act_table(ACT.Exp)

                def do_exp(t, u, g):
                    reach(act, scores_t_ok, t * NG + (g + 1))
                    if g == 0:
                        reach(act, values_ok, t - 1)
                    reach(act, exp_lo_ok, t * NG + (g - NG + 1))
                    nc.scalar.activation(exp32[:, g, :], score_t[g % 2][:, :], ACT.Exp, scale=DH ** -0.5 / (scale * scale))
                    nc.scalar.activation(exp_hi[:, u % 2, g, :, :].rearrange("p h q -> p (h q)"), score_t[g % 2][:, :],
                                         ACT.Exp, scale=DH ** -0.5 / (scale * scale)).then_inc(exp_ok, 1)

                def step(i, u):
                    run_exps = inside(i - EL, TILES)
                    uE = (u - EL) % UNROLL
                    if inside(i, TILES):
                        if layer:
                            reach(act, s_turn, i - 1)
                            nc.scalar.activation(split[:, u % 2, 1, :], m.ctx[:, i, :], ACT.Copy).then_inc(ch_ok, 1)
                        else:
                            reach(act, values_ok, i - 7)
                            nc.scalar.activation(k_stack[:, u, :, 0:3:2, :], twice(m.ctx[:, i, :]), ACT.Copy).then_inc(kh_ok, 1)
                    if layer and inside(i - 1, TILES):
                        reach(act, q_proj, i)
                        reach(act, k_turn, i - 2)
                        nc.scalar.activation(q_stack[:, (u - 1) % 2, :, 0:2, :], twice(q_ps[:, 0:D]), ACT.Relu).then_inc(qh_ok, 1)
                    if run_exps:
                        do_exp(i - EL, uE, 0)
                    if inside(i, TILES):
                        reach(act, nf_ok, i + 1)
                        if layer:
                            nc.scalar.activation(split[:, u % 2, 0, :], normed[:, u % NR, :], ACT.Copy).then_inc(nh_ok, 1)
                        else:
                            reach(act, q_turn, i - 1)
                            nc.scalar.activation(q_stack[:, u % 2, :, 0:2, :], twice(normed[:, u % NR, :]), ACT.Copy).then_inc(qh_ok, 1)
                    if run_exps:
                        do_exp(i - EL, uE, 1)
                        do_exp(i - EL, uE, 2)
                    if layer and inside(i - 1, TILES):
                        reach(act, kv_proj, i)
                        nc.scalar.activation(k_stack[:, (u - 1) % 2, :, 0:3:2, :], twice(kv_ps[:, 0:D]), ACT.Relu)
                        reach(act, values_ok, i - 7)
                        nc.scalar.activation(v_hi[:, (u - 1) % UNROLL, :, 0:DH], heads(kv_ps[:, D:2 * D]), ACT.Relu).then_inc(kh_ok, 1)
                    if run_exps:
                        do_exp(i - EL, uE, 3)

                run_steps(act, step, UNROLL, head, TILES, last_lag)

            @block.gpsimd
            def _(pool):
                def step(i, u):
                    uE = (u - EL) % UNROLL
                    if inside(i, TILES):
                        if layer:
                            reach(pool, ch_ok, i + 1)
                            nc.gpsimd.tensor_tensor(split[:, u % 2, 3, :], m.ctx[:, i, :], split[:, u % 2, 1, :],
                                                    ALU.subtract).then_inc(cl_ok, 1)
                        else:
                            reach(pool, kh_ok, i + 1)
                            nc.gpsimd.tensor_tensor(k_stack[:, u, :, 1, :], heads(m.ctx[:, i, :]), k_stack[:, u, :, 0, :],
                                                    ALU.subtract).then_inc(kl_ok, 1)
                    if inside(i - EL, TILES):
                        for g in range(NG):
                            reach(pool, exp_ok, (i - EL) * NG + (g + 1))
                            nc.gpsimd.tensor_tensor(exp_lo[:, uE % 2, g, :, :].rearrange("p h q -> p (h q)"), exp32[:, g, :],
                                                    exp_hi[:, uE % 2, g, :, :].rearrange("p h q -> p (h q)"),
                                                    ALU.subtract).then_inc(exp_lo_ok, 1)

                run_steps(pool, step, UNROLL, head, TILES, last_lag)


def bitnet_stage(nc, io, m):
    lag, head = 3, 4
    with ExitStack() as ctx:
        def sem(name):
            return ctx.enter_context(nc.semaphore(f"b_{name}"))

        def sb(name, shape, dt=F32):
            return ctx.enter_context(nc.sbuf_tensor(f"b_{name}", shape, dt))

        def bank(name, dt=F32):
            return ctx.enter_context(nc.psum_tensor(f"b_{name}", [P, 2048 // (4 if dt == F32 else 2)], dt))

        turn = [bank("turn0", F16), bank("turn1", F16)]
        hid = [bank("hid0"), bank("hid1")]
        out = [bank("out0"), bank("out1")]
        peaks, spread_ps = bank("peaks"), bank("spread_ps")
        w1t = sb("w1t", [P, DC, HID], F16)
        w2t = sb("w2t", [P, HC, D], F16)
        taps = sb("taps", [P, HC, 3])
        conv_b = sb("conv_b", [P, HC])
        weight_mean = sb("weight_mean", [P, 2])
        in_back = sb("in_back", [P, 1])
        out_back = sb("out_back", [P, 1])

        with ExitStack() as prep:
            raw = [prep.enter_context(nc.sbuf_tensor(f"b_raw{n}", [P, 2048], F32)) for n in range(2)]
            scaled = [prep.enter_context(nc.sbuf_tensor(f"b_scaled{n}", [P, 2048], F32)) for n in range(2)]
            tern = [prep.enter_context(nc.sbuf_tensor(f"b_tern{n}", [P, 2048], F16)) for n in range(2)]
            rows = prep.enter_context(nc.sbuf_tensor("b_rows", [P, 2], F32))
            inverse = prep.enter_context(nc.sbuf_tensor("b_inverse", [P, 2], F32))
            w_in, taps_in, rows_ok, total_ok, chain, turned, copied, w1_in = (sem(n) for n in (
                "w_in", "taps_in", "rows_ok", "total_ok", "chain", "turned", "copied", "w1_in"))
            block = prep.enter_context(nc.Block())

            @block.sync
            def _(sp):
                sp.dma_start(raw[0][:].rearrange("p (c d) -> p c d", c=HC), io["L0_ffn_w1"].rearrange("(c p) d -> p c d", p=P)).then_inc(w1_in, 16)
                sp.dma_start(raw[1][:].rearrange("p (c d) -> p c d", c=DC), io["L0_ffn_w2"].rearrange("(c p) d -> p c d", p=P)).then_inc(w_in, 16)
                with nc.allow_non_contiguous_dma(reason="small"):
                    sp.dma_start(taps[:], io["L0_ffn_conv_w"].rearrange("(c p) a k -> p c (a k)", p=P)).then_inc(taps_in, 16)
                    sp.dma_start(conv_b[:], io["L0_ffn_conv_b"].rearrange("(c p) -> p c", p=P)).then_inc(taps_in, 16)
                sp.wait_ge(taps_in, 32)

            @block.tensor
            def _(pe):
                pe.wait_ge(rows_ok, 2)
                nc.tensor.matmul(peaks[:, 0:2], m.ones32[:, :], rows[:, :], start=True, stop=True).then_inc(total_ok, 1)
                pe.wait_ge(chain, 13)
                for n in range(4):
                    reach(pe, copied, n - 1)
                    for k in range(8):
                        q = (n % 2) * 8 + k
                        a, b = (q % HC, q // HC) if n < 2 else (q % DC, q // DC)
                        width = D if n < 2 else HID
                        last = nc.tensor.transpose(turn[n % 2][:, k * P:(k + 1) * P],
                                                   tern[n // 2][:, a * width + b * P:a * width + (b + 1) * P], m.ident16[:, :])
                    last.then_inc(turned, 1)

            @block.vector
            def _(dve):
                step = [0]

                def then(instruction):
                    step[0] += 1
                    instruction.then_inc(chain, 1)
                    dve.wait_ge(chain, step[0])

                dve.wait_ge(w1_in, 16)
                nc.vector.tensor_reduce(rows[:, 0:1], raw[0][:], AX.X, ALU.add, apply_absolute_value=True).then_inc(rows_ok, 1)
                dve.wait_ge(w_in, 16)
                nc.vector.tensor_reduce(rows[:, 1:2], raw[1][:], AX.X, ALU.add, apply_absolute_value=True).then_inc(rows_ok, 1)
                dve.wait_ge(total_ok, 1)
                then(nc.vector.tensor_scalar(weight_mean[:], peaks[:, 0:2], 1.0 / (HID * D), 1e-5, ALU.mult, ALU.max))
                then(nc.vector.reciprocal(inverse[:], weight_mean[:]))
                for n in range(2):
                    then(nc.vector.tensor_scalar(scaled[n][:], raw[n][:], inverse[:, n:n + 1], MAGIC, ALU.mult, ALU.add))
                    then(nc.vector.tensor_scalar(scaled[n][:], scaled[n][:], MAGIC, 1.0, ALU.subtract, ALU.min))
                    then(nc.vector.tensor_scalar(tern[n][:], scaled[n][:], -1.0, None, ALU.max))
                dve.wait_ge(taps_in, 32)
                then(nc.vector.tensor_scalar(taps[:], taps[:], 1.0 / XS, None, ALU.mult))
                then(nc.vector.tensor_scalar(in_back[:], weight_mean[:, 0:1], XS / 127.0, None, ALU.mult))
                then(nc.vector.tensor_scalar(out_back[:], weight_mean[:, 1:2], 1.0 / 127.0, m.tanh_gates[:, 2:3], ALU.mult, ALU.mult))
                then(nc.vector.memset(rows[:], 0.0))
                then(nc.vector.memset(inverse[:], 0.0))
                for n in range(4):
                    dve.wait_ge(turned, n + 1)
                    dst = w1t[:, n % 2, :] if n < 2 else w2t[:, 4 * (n % 2):4 * (n % 2) + 4, :].rearrange("p c d -> p (c d)")
                    nc.vector.tensor_copy(dst, turn[n % 2][:, :]).then_inc(copied, 1)
                dve.wait_ge(copied, 4)

        normed = sb("normed", [P, GT, D])
        x_parts = sb("x_parts", [P, 2, GT, D], F16)
        x_turned = sb("x_turned", [P, DC, 2, GT, P], F16)
        peak_in, scale_in, back_in = sb("peak_in", [P, GT]), sb("scale_in", [P, GT]), sb("back_in", [P, GT])
        peak_mid, scale_mid, back_mid = sb("peak_mid", [P, GT]), sb("scale_mid", [P, GT]), sb("back_mid", [P, 2, GT])
        shifted = sb("shifted", [P, 2, GW])
        hidden = sb("hidden", [P, 2, HC, GW])
        peak_t, peak_half = sb("peak_t", [P, 2, GW]), sb("peak_half", [P, GW])
        diagonal = sb("diagonal", [P, GT, P])
        ints = sb("ints", [P, HC, GW], F16)

        (norm_ok, in_ok, deq_ok, hi_ok, lo_ok, t_turn, t_copied, hid_ok, tap_r, tap_l, conv_ok, hidden_ok,
         peak_ok, peak_turn, mid_ok, diag_ok, spread_ok, mult_ok, ints_ok, out_ok, fin_ok) = (sem(n) for n in (
             "norm_ok", "in_ok", "deq_ok", "hi_ok", "lo_ok", "t_turn", "t_copied", "hid_ok", "tap_r", "tap_l", "conv_ok",
             "hidden_ok", "peak_ok", "peak_turn", "mid_ok", "diag_ok", "spread_ok", "mult_ok", "ints_ok", "out_ok", "fin_ok"))

        with nc.Block() as block:

            @block.tensor
            def _(pe):
                def first_product(t, u, c):
                    if c == 0:
                        reach(pe, t_copied, 2 * t + 2)
                    reach(pe, tap_r, t * HC + (c - 1))
                    for d in range(DC):
                        for part in range(2):
                            last = nc.tensor.matmul(hid[c % 2][:, :], w1t[:, d, c * P:(c + 1) * P],
                                                    x_turned[:, d, part, :, :].rearrange("p t k -> p (t k)"),
                                                    start=(d == 0 and part == 0), stop=(d == DC - 1 and part == 1))
                    last.then_inc(hid_ok, 1)

                def step(j, u):
                    if inside(j - 2, GROUPS):
                        reach(pe, peak_ok, (j - 2) * 3 + 3)
                        for k in range(GT):
                            last = nc.tensor.transpose(peaks[:, k * P:(k + 1) * P], peak_t[:, u % 2, k * P:(k + 1) * P], m.ident32[:, :])
                        last.then_inc(peak_turn, 1)
                    if inside(j - 1, GROUPS):
                        first_product(j - 1, u - 1, 0)
                        first_product(j - 1, u - 1, 1)
                    if inside(j - 2, GROUPS):
                        reach(pe, diag_ok, j - 1)
                        nc.tensor.matmul(spread_ps[:, :], m.ones32[:, :], diagonal[:].rearrange("p t k -> p (t k)"),
                                         start=True, stop=True).then_inc(spread_ok, 1)
                    if inside(j - 1, GROUPS):
                        for c in range(2, HC):
                            first_product(j - 1, u - 1, c)
                    if inside(j, GROUPS):
                        reach(pe, hi_ok, j + 1)
                        reach(pe, lo_ok, j + 1)
                        for d in range(DC):
                            reach(pe, t_copied, 2 * j + (d - 1))
                            for part in range(2):
                                for k in range(GT):
                                    n = part * GT + k
                                    last = nc.tensor.transpose(turn[d][:, n * P:(n + 1) * P], x_parts[:, part, k, d * P:(d + 1) * P], m.ident16[:, :])
                            last.then_inc(t_turn, 1)
                    if inside(j - 2, GROUPS):
                        reach(pe, ints_ok, (j - 2) * HC + HC)
                        reach(pe, fin_ok, j - 2)
                        for k in range(GT):
                            dst = out[k // 2][:, (k % 2) * D:(k % 2 + 1) * D]
                            for c in range(HC):
                                last = nc.tensor.matmul(dst, ints[:, c, k * P:(k + 1) * P], w2t[:, c, :], start=(c == 0), stop=(c == HC - 1))
                        last.then_inc(out_ok, 1)

                run_steps(pe, step, 2, head, GROUPS, lag)

            @block.vector
            def _(dve):
                def convolve(t, u, c):
                    reach(dve, tap_l, t * HC + (c + 1))
                    dst = hidden[:, u % 2, c, :].rearrange("p (t k) -> p t k", k=P)[:, :, 0:P - 1]
                    nc.vector.scalar_tensor_tensor(out=dst, in0=hid[c % 2][:, :].rearrange("p (t k) -> p t k", k=P)[:, :, 1:P],
                                                   scalar=taps[:, c, 2:3], in1=dst, op0=ALU.mult, op1=ALU.add).then_inc(tap_r, 1)

                def largest(t, u, half):
                    last = half == 1
                    reach(dve, hidden_ok, t * HC + (HC if last else HC // 2))
                    dst = peak_half if last else peak_t[:, u % 2, :]
                    src = hidden[:, u % 2, half * HC // 2:(half + 1) * HC // 2, :].rearrange("p c k -> p k c")
                    nc.vector.tensor_reduce(dst[:, :] if last else dst, src, AX.X, ALU.max, apply_absolute_value=True).then_inc(peak_ok, 1)
                    if last:
                        reach(dve, peak_ok, t * 3 + 2)
                        nc.vector.tensor_tensor(peak_t[:, u % 2, :], peak_t[:, u % 2, :], peak_half[:, :], ALU.max).then_inc(peak_ok, 1)

                def requantise(t, u, c):
                    if c == 0:
                        reach(dve, spread_ok, t + 1)
                        reach(dve, out_ok, t)
                    nc.vector.tensor_tensor(hidden[:, u % 2, c, :], hidden[:, u % 2, c, :], spread_ps[:, :], ALU.mult).then_inc(mult_ok, 1)
                    reach(dve, mult_ok, t * HC + (c + 1))
                    nc.vector.tensor_scalar(ints[:, c, :], hidden[:, u % 2, c, :], MAGIC, MAGIC, ALU.add, ALU.subtract).then_inc(ints_ok, 1)

                def step(j, u):
                    if inside(j - 3, GROUPS):
                        t = j - 3
                        reach(dve, out_ok, t + 1)
                        for k in range(GT):
                            x = m.x[:, t * GT + k, :]
                            last = nc.vector.scalar_tensor_tensor(out=x, in0=out[k // 2][:, (k % 2) * D:(k % 2 + 1) * D],
                                                                  scalar=back_mid[:, (u - 3) % 2, k:k + 1], in1=x, op0=ALU.mult, op1=ALU.add)
                        last.then_inc(fin_ok, 1)
                        reach(dve, fin_ok, t + 1)
                    if inside(j - 2, GROUPS):
                        t = j - 2
                        reach(dve, peak_turn, t + 1)
                        nc.vector.tensor_reduce(peak_mid[:], peaks[:, :].rearrange("p (t k) -> p t k", k=P), AX.X, ALU.max).then_inc(mid_ok, 1)
                        reach(dve, mid_ok, t * 4 + 1)
                        nc.vector.tensor_scalar(peak_mid[:], peak_mid[:], 1e-5, None, ALU.max).then_inc(mid_ok, 1)
                        reach(dve, mid_ok, t * 4 + 2)
                        nc.vector.reciprocal(scale_mid[:], peak_mid[:]).then_inc(mid_ok, 1)
                        nc.vector.tensor_scalar(back_mid[:, u % 2, :], peak_mid[:], out_back[:, 0:1], None, ALU.mult)
                        reach(dve, mid_ok, t * 4 + 3)
                        nc.vector.tensor_scalar(scale_mid[:], scale_mid[:], 127.0, None, ALU.mult).then_inc(mid_ok, 1)
                        reach(dve, mid_ok, t * 4 + 4)
                        for k in range(GT):
                            last = nc.vector.tensor_scalar(diagonal[:, k, :], m.ident32[:, :], scale_mid[:, k:k + 1], None, ALU.mult)
                        last.then_inc(diag_ok, 1)
                    if inside(j, GROUPS):
                        reach(dve, lo_ok, j)
                        for k in range(GT):
                            last = nc.vector.tensor_scalar(normed[:, k, :], m.x[:, j * GT + k, :], m.mean[:, j, k:k + 1],
                                                           m.rstd[:, j, k:k + 1], ALU.subtract, ALU.mult)
                        last.then_inc(norm_ok, 1)
                    if inside(j - 3, GROUPS):
                        for k in range(GT):
                            nc.vector.bn_stats(m.stats[:, (j - 3) * GT + k, :], m.x[:, (j - 3) * GT + k, :])
                    if inside(j, GROUPS):
                        reach(dve, norm_ok, j + 1)
                        nc.vector.tensor_reduce(peak_in[:], normed[:], AX.X, ALU.max, apply_absolute_value=True).then_inc(in_ok, 1)
                        reach(dve, in_ok, j * 4 + 1)
                        nc.vector.tensor_scalar(peak_in[:], peak_in[:], 1e-5, None, ALU.max).then_inc(in_ok, 1)
                        reach(dve, in_ok, j * 4 + 2)
                        nc.vector.reciprocal(scale_in[:], peak_in[:]).then_inc(in_ok, 1)
                        nc.vector.tensor_scalar(back_in[:], peak_in[:], in_back[:, 0:1], None, ALU.mult)
                        reach(dve, in_ok, j * 4 + 3)
                        nc.vector.tensor_scalar(scale_in[:], scale_in[:], 127.0, None, ALU.mult).then_inc(in_ok, 1)
                        reach(dve, in_ok, j * 4 + 4)
                        for k in range(GT):
                            last = nc.vector.tensor_scalar(normed[:, k, :], normed[:, k, :], scale_in[:, k:k + 1], MAGIC, ALU.mult, ALU.add)
                        last.then_inc(deq_ok, 1)
                        reach(dve, deq_ok, j * 2 + 1)
                        for k in range(GT):
                            last = nc.vector.tensor_scalar(normed[:, k, :], normed[:, k, :], MAGIC, back_in[:, k:k + 1], ALU.subtract, ALU.mult)
                        last.then_inc(deq_ok, 1)
                    for c in range(HC + 2):
                        if c < HC and inside(j - 1, GROUPS):
                            convolve(j - 1, u - 1, c)
                        if c < HC and inside(j - 2, GROUPS):
                            requantise(j - 2, u - 2, c)
                        if c in (HC - 1, HC + 1) and inside(j - 1, GROUPS):
                            largest(j - 1, u - 1, int(c > HC))
                    if inside(j, GROUPS):
                        for d in range(DC):
                            reach(dve, t_turn, 2 * j + (d + 1))
                            nc.vector.tensor_copy(x_turned[:, d, :, :, :],
                                                  turn[d][:, :].rearrange("p (a t k) -> p a t k", a=2, t=GT)).then_inc(t_copied, 1)

                run_steps(dve, step, 2, head, GROUPS, lag)

            @block.scalar
            def _(act):
                nc.scalar.preload_act_table(ACT.Silu)

                def split(j):
                    reach(act, deq_ok, j * 2 + 2)
                    reach(act, t_turn, 2 * j)
                    nc.scalar.activation(x_parts[:, 0, :, :], normed[:], ACT.Copy).then_inc(hi_ok, 1)

                def step(j, u):
                    for c in range(HC + 2):
                        if c < HC and inside(j - 1, GROUPS):
                            n = (j - 1) * HC + c
                            reach(act, hid_ok, n + 1)
                            if c == 0:
                                reach(act, ints_ok, (j - 2) * HC)
                            reach(act, conv_ok, n - 1)
                            nc.scalar.activation(hidden[:, (u - 1) % 2, c, :], hid[c % 2][:, :], ACT.Identity, scale=taps[:, c, 1:2],
                                                 bias=conv_b[:, c:c + 1])
                            nc.scalar.activation(shifted[:, c % 2, :], hid[c % 2][:, :], ACT.Copy, scale=taps[:, c, 0:1]).then_inc(tap_l, 1)
                        if c == 3 and inside(j, GROUPS):
                            split(j)
                        if c >= 2 and inside(j - 1, GROUPS):
                            n = (j - 1) * HC + c - 2
                            reach(act, conv_ok, n + 1)
                            nc.scalar.activation(hidden[:, (u - 1) % 2, c - 2, :], hidden[:, (u - 1) % 2, c - 2, :], ACT.Silu).then_inc(hidden_ok, 1)

                run_steps(act, step, 2, head, GROUPS, lag)

            @block.gpsimd
            def _(pool):
                def step(j, u):
                    for c in range(HC):
                        if inside(j - 1, GROUPS):
                            n = (j - 1) * HC + c
                            reach(pool, tap_l, n + 1)
                            reach(pool, tap_r, n + 1)
                            dst = hidden[:, (u - 1) % 2, c, :].rearrange("p (t k) -> p t k", k=P)[:, :, 1:P]
                            nc.gpsimd.tensor_tensor(dst, dst, shifted[:, c % 2, :].rearrange("p (t k) -> p t k", k=P)[:, :, 0:P - 1],
                                                    ALU.add).then_inc(conv_ok, 1)
                        if c == 3 and inside(j, GROUPS):
                            reach(pool, hi_ok, j + 1)
                            nc.gpsimd.tensor_tensor(x_parts[:, 1, :, :], normed[:], x_parts[:, 0, :, :], ALU.subtract).then_inc(lo_ok, 1)

                run_steps(pool, step, 2, head, GROUPS, lag)


def expert_stage(nc, io, m):
    lag, head = 2, 2
    with ExitStack() as ctx:
        def sem(name):
            return ctx.enter_context(nc.semaphore(f"e_{name}"))

        def sb(name, shape, dt=F32):
            return ctx.enter_context(nc.sbuf_tensor(f"e_{name}", shape, dt))

        def bank(name, dt=F32):
            return ctx.enter_context(nc.psum_tensor(f"e_{name}", [P, 2048 // (4 if dt == F32 else 2)], dt))

        turn = [bank("turn0", F16), bank("turn1", F16)]
        gate_ps, up_ps, weight_ps, route_ps = (bank(n) for n in ("gate_ps", "up_ps", "weight_ps", "route_ps"))
        out = [bank("out0"), bank("out1")]
        wt = {name: sb(f"{name}_t", [P, 2, DC, EXPERTS * P], F16) for name in ("gate", "up")}
        down_t = sb("down_t", [P, 2, EXPERTS, D], F16)
        router = sb("router", [P, 2, DC, EXPERTS], F16)
        bias = sb("bias", [P, EXPERTS])
        select = sb("select", [4 * EXPERTS, EXPERTS, P], F16)
        before4 = sb("before4", [P, EGROUPS, EGROUPS])
        before8 = sb("before8", [P, EXPERTS, EXPERTS])
        res_gate = sb("res_gate", [P, 1])

        with ExitStack() as prep:
            raw = [prep.enter_context(nc.sbuf_tensor(f"e_raw{n}", [P, EXPERTS, D], F32)) for n in range(3)]
            hi = prep.enter_context(nc.sbuf_tensor("e_hi", [P, EXPERTS, D], F16))
            lo = prep.enter_context(nc.sbuf_tensor("e_lo", [P, EXPERTS, D], F16))
            raw_r = prep.enter_context(nc.sbuf_tensor("e_raw_r", [P, DC, EXPERTS], F32))
            loaded = [sem(f"loaded{n}") for n in range(4)]
            chain, turned, copied, const_ok, part_ok, scaled_ok, route_ok = (sem(n) for n in (
                "chain", "turned", "copied", "const_ok", "part_ok", "scaled_ok", "route_ok"))
            block = prep.enter_context(nc.Block())

            @block.sync
            def _(sp):
                for n, name in enumerate(("L1_ffn_gate_proj", "L1_ffn_up_proj")):
                    sp.dma_start(raw[n][:], io[name].rearrange("e i d -> i e d")).then_inc(loaded[n], 16)
                down = io["L1_ffn_down_proj"].rearrange("e (c p) i -> c p e i", p=P)
                for c in range(DC):
                    sp.dma_start(raw[2][:, :, c * P:(c + 1) * P], down[c]).then_inc(loaded[2], 16)
                with nc.allow_non_contiguous_dma(reason="small"):
                    for c in range(DC):
                        sp.dma_start(raw_r[:, c, :], io["L1_ffn_gate_weight"][:, c * P:(c + 1) * P].rearrange("e p -> p e")).then_inc(loaded[3], 16)
                sp.dma_start(bias[:], io["L1_ffn_e_score_correction_bias"].rearrange("(a n) -> a n", a=1).broadcast_to([P, EXPERTS])).then_inc(loaded[3], 16)
                sp.wait_ge(loaded[3], 48)

            @block.gpsimd
            def _(pool):
                nc.gpsimd.memset(select[:], 1.0 / (WS * WS)).then_inc(const_ok, 1)
                nc.gpsimd.memset(before4[:], 1.0).then_inc(const_ok, 1)
                nc.gpsimd.memset(before8[:], 1.0).then_inc(const_ok, 1)
                pool.wait_ge(const_ok, 3)
                nc.gpsimd.affine_select(out=before4[:], in_=before4[:], pattern=[[1, EGROUPS], [-1, EGROUPS]], compare_op=ALU.is_gt,
                                        fill=0.0, base=0, channel_multiplier=0).then_inc(const_ok, 1)
                nc.gpsimd.affine_select(out=before8[:], in_=before8[:], pattern=[[1, EXPERTS], [-1, EXPERTS]], compare_op=ALU.is_gt,
                                        fill=0.0, base=0, channel_multiplier=0).then_inc(const_ok, 1)
                nc.gpsimd.affine_select(out=select[:], in_=select[:], pattern=[[-1, EXPERTS], [0, P]], compare_op=ALU.is_equal,
                                        fill=0.0, base=0, channel_multiplier=1).then_inc(const_ok, 1)
                pool.wait_ge(const_ok, 6)
                nc.gpsimd.affine_select(out=select[:], in_=select[:], pattern=[[-1, EXPERTS], [0, P]], compare_op=ALU.not_equal,
                                        fill=1.0 / (WS * WS), base=-EXPERTS, channel_multiplier=1).then_inc(const_ok, 1)
                pool.wait_ge(const_ok, 7)

            @block.scalar
            def _(act):
                for n in range(3):
                    act.wait_ge(scaled_ok, n + 1)
                    reach(act, turned, 4 * n)
                    nc.scalar.activation(hi[:], raw[n][:], ACT.Copy).then_inc(part_ok, 1)

            @block.vector
            def _(dve):
                for n in range(3):
                    dve.wait_ge(loaded[n], 16 if n < 2 else 32)
                    nc.vector.tensor_scalar(raw[n][:], raw[n][:], WS, None, ALU.mult).then_inc(scaled_ok, 1)
                dve.wait_ge(loaded[3], 48)
                nc.vector.tensor_copy(router[:, 0, :, :], raw_r[:]).then_inc(route_ok, 1)
                dve.wait_ge(route_ok, 1)
                nc.vector.tensor_tensor(router[:, 1, :, :], raw_r[:], router[:, 0, :, :], ALU.subtract).then_inc(route_ok, 1)
                nc.vector.tensor_scalar(res_gate[:], m.tanh_gates[:, 3:4], 1.0 / WS, None, ALU.mult).then_inc(route_ok, 1)
                for n in range(3):
                    dve.wait_ge(part_ok, n + 1)
                    reach(dve, turned, 4 * n)
                    nc.vector.tensor_tensor(lo[:], raw[n][:], hi[:], ALU.subtract).then_inc(chain, 1)
                    for k in range(4):
                        dve.wait_ge(turned, 4 * n + k + 1)
                        part, c = k // 2, k % 2
                        if n < 2:
                            dst = wt[("gate", "up")[n]][:, part, c, :]
                        else:
                            dst = down_t[:, part, :, c * P:(c + 1) * P]
                        src = turn[k % 2][:, :] if n < 2 else turn[k % 2][:, :].rearrange("p (e k) -> p e k", k=P)
                        nc.vector.tensor_copy(dst, src).then_inc(copied, 1)
                dve.wait_ge(copied, 12)
                dve.wait_ge(route_ok, 3)

            @block.tensor
            def _(pe):
                for n in range(3):
                    pe.wait_ge(chain, n + 1)
                    for k in range(4):
                        part, c = k // 2, k % 2
                        reach(pe, copied, 4 * n + k - 1)
                        for e in range(EXPERTS):
                            last = nc.tensor.transpose(turn[k % 2][:, e * P:(e + 1) * P], (hi, lo)[part][:, e, c * P:(c + 1) * P], m.ident16[:, :])
                        last.then_inc(turned, 1)

        normed = sb("normed", [P, GT, D])
        n_parts = sb("n_parts", [P, 2, GT, D], F16)
        n_turned = sb("n_turned", [P, 2, DC, 2, GT, P], F16)
        score = sb("score", [P, GT, EXPERTS])
        choice = sb("choice", [P, GT, EXPERTS])
        group = sb("group", [P, GT, EGROUPS])
        above4, equal4 = sb("above4", [P, GT, EGROUPS, EGROUPS]), sb("equal4", [P, GT, EGROUPS, EGROUPS])
        above8, equal8 = sb("above8", [P, GT, EXPERTS, EXPERTS]), sb("equal8", [P, GT, EXPERTS, EXPERTS])
        rank4, rank8 = sb("rank4", [P, GT, EGROUPS]), sb("rank8", [P, GT, EXPERTS])
        total = sb("total", [P, GT])
        weight = sb("weight", [P, GT, EXPERTS])
        w_parts = sb("w_parts", [P, GT, 2, EXPERTS], F16)
        w_turned = sb("w_turned", [4 * EXPERTS, 2, GW], F16)
        sig = sb("sig", [P, 2, GW])
        act1, act2, act3 = sb("act1", [P, 2, GW]), sb("act2", [P, 2, GW]), sb("act3", [P, 2, GW])
        a_parts = sb("a_parts", [P, 2, 2, GW], F16)

        (norm_ok, hi_ok, lo_ok, t_turn, t_copied, logits_ok, score_ok, chain, w_ok, w_turn, w_copied, gate_ok, up_ok, weight_ok,
         sig_ok, act1_ok, act2_ok, act3_ok, ahi_ok, alo_ok, down_ok, out_ok, fin_ok, stored, w_zero) = (sem(n) for n in (
             "norm_ok", "hi_ok", "lo_ok", "t_turn", "t_copied", "logits_ok", "score_ok", "route_chain", "w_ok", "w_turn", "w_copied",
             "gate_ok", "up_ok", "weight_ok", "sig_ok", "act1_ok", "act2_ok", "act3_ok", "ahi_ok", "alo_ok", "down_ok", "out_ok",
             "fin_ok", "stored", "w_zero"))
        CH = 18

        with nc.Block() as block:

            @block.sync
            def _(sp):
                view = io["out"].rearrange("b s d -> s b d")

                def step(j, u):
                    if inside(j - 2, GROUPS):
                        t = j - 2
                        reach(sp, fin_ok, t + 1)
                        sp.dma_start(view[:, (t * GT):(t * GT) + GT, :] if isinstance(t, int) else view[:, bass.ds(t * GT, GT), :],
                                     m.x[:, (t * GT):(t * GT) + GT, :] if isinstance(t, int) else m.x[:, bass.ds(t * GT, GT), :]).then_inc(stored, 16)

                run_steps(sp, step, 2, head, GROUPS, lag)
                sp.wait_ge(stored, 16 * GROUPS)

            @block.tensor
            def _(pe):
                terms = ((0, 0), (0, 1), (1, 0))

                def product(dst, w, u, e):
                    for n, (part, wpart) in enumerate(terms):
                        for d in range(DC):
                            last = nc.tensor.matmul(dst[:, :], w[:, wpart, d, e * P:(e + 1) * P],
                                                    n_turned[:, u % 2, d, part, :, :].rearrange("p t k -> p (t k)"),
                                                    start=(n == 0 and d == 0), stop=(n == 2 and d == DC - 1))
                    return last

                def down(t, e):
                    n = t * EXPERTS + e
                    reach(pe, alo_ok, n + 1)
                    if e == 0:
                        reach(pe, fin_ok, t)
                    for k in range(GT):
                        dst = out[k // 2][:, (k % 2) * D:(k % 2 + 1) * D]
                        for s, (part, wpart) in enumerate(terms):
                            last = nc.tensor.matmul(dst, a_parts[:, e % 2, part, k * P:(k + 1) * P], down_t[:, wpart, e, :],
                                                    start=(e == 0 and s == 0 and k % 2 == 0), stop=(e == EXPERTS - 1 and s == 2),
                                                    skip_group_check=True)
                    last.then_inc(down_ok, 1)
                    return last

                def turn_tokens(j):
                    reach(pe, lo_ok, j + 1)
                    for d in range(DC):
                        reach(pe, t_copied, 2 * j + (d - 1))
                        for part in range(2):
                            for k in range(GT):
                                n = part * GT + k
                                last = nc.tensor.transpose(turn[d][:, n * P:(n + 1) * P], n_parts[:, part, k, d * P:(d + 1) * P], m.ident16[:, :])
                        last.then_inc(t_turn, 1)

                def logits(j, u):
                    reach(pe, t_copied, 2 * j + 2)
                    reach(pe, w_copied, j)
                    for k in range(GT):
                        for s, (part, wpart) in enumerate(((0, 0), (0, 1), (1, 0), (1, 1))):
                            for d in range(DC):
                                last = nc.tensor.matmul(route_ps[:, k * EXPERTS:(k + 1) * EXPERTS], n_turned[:, u % 2, d, part, k, :],
                                                        router[:, wpart, d, :], start=(s == 0 and d == 0), stop=(s == 3 and d == DC - 1))
                    last.then_inc(logits_ok, 1)

                def turn_weights(j):
                    reach(pe, w_ok, j + 1)
                    for k in range(GT):
                        last = nc.tensor.transpose(route_ps[0:2 * EXPERTS, :].bitcast(F16)[:, k * P:(k + 1) * P],
                                                   w_parts[:, k, :, :].rearrange("p a e -> p (a e)"), m.ident16[:, :])
                    last.then_inc(w_turn, 1)

                def step(j, u):
                    for e in range(EXPERTS):
                        if inside(j - 1, GROUPS):
                            n = (j - 1) * EXPERTS + e
                            if e == 0:
                                reach(pe, t_copied, 2 * j)
                            reach(pe, act1_ok, n)
                            product(gate_ps, wt["gate"], u - 1, e).then_inc(gate_ok, 1)
                            reach(pe, act2_ok, n)
                            product(up_ps, wt["up"], u - 1, e).then_inc(up_ok, 1)
                            if e == 0:
                                reach(pe, w_copied, j)
                            reach(pe, act3_ok, n)
                            nc.tensor.matmul(weight_ps[:, :], select[:, e, :], w_turned[:, (u - 1) % 2, :], start=True, stop=True).then_inc(weight_ok, 1)
                        if inside(j, GROUPS):
                            if e == 1:
                                turn_tokens(j)
                            if e == 2:
                                logits(j, u)
                            if e == 6:
                                turn_weights(j)
                        if e == 0 and inside(j - 2, GROUPS):
                            down(j - 2, EXPERTS - 1)
                        if e >= 1 and inside(j - 1, GROUPS):
                            down(j - 1, e - 1)

                run_steps(pe, step, 2, head, GROUPS, lag)

            @block.vector
            def _(dve):
                nc.vector.memset(w_turned[:], 0.0).then_inc(w_zero, 1)
                dve.wait_ge(w_zero, 1)

                def expert(t, u, e):
                    n = t * EXPERTS + e
                    p = e % 2
                    reach(dve, sig_ok, n + 1)
                    nc.vector.tensor_tensor(act1[:, p, :], sig[:, p, :], gate_ps[:, :], ALU.mult).then_inc(act1_ok, 1)
                    reach(dve, up_ok, n + 1)
                    reach(dve, act1_ok, n + 1)
                    nc.vector.tensor_tensor(act2[:, p, :], act1[:, p, :], up_ps[:, :], ALU.mult).then_inc(act2_ok, 1)
                    reach(dve, weight_ok, n + 1)
                    reach(dve, act2_ok, n + 1)
                    reach(dve, alo_ok, n - 1)
                    nc.vector.tensor_tensor(act3[:, p, :], act2[:, p, :], weight_ps[:, :], ALU.mult).then_inc(act3_ok, 1)

                def route(j, piece):
                    step = [(0, 7, 13)[piece]]

                    def then(instruction):
                        step[0] += 1
                        instruction.then_inc(chain, 1)
                        reach(dve, chain, j * CH + step[0])

                    def ranks(values, count, above, equal, before, rank):
                        theirs = values[:, :, None, :].broadcast_to([P, GT, count, count])
                        own = values[:, :, :, None].broadcast_to([P, GT, count, count])
                        first = before[:, None, :, :].broadcast_to([P, GT, count, count])
                        then(nc.vector.tensor_tensor(above[:], theirs, own, ALU.is_gt))
                        then(nc.vector.tensor_tensor(equal[:], theirs, own, ALU.is_equal))
                        then(nc.vector.tensor_tensor(equal[:], equal[:], first, ALU.mult))
                        then(nc.vector.tensor_tensor(above[:], above[:], equal[:], ALU.add))
                        then(nc.vector.tensor_reduce(rank[:], above[:], AX.X, ALU.add))

                    if piece == 0:
                        reach(dve, score_ok, j + 1)
                        then(nc.vector.tensor_tensor(choice[:], score[:], bias[:, None, :].broadcast_to([P, GT, EXPERTS]), ALU.add))
                        then(nc.vector.tensor_tensor(group[:], choice[:, :, 0::2], choice[:, :, 1::2], ALU.add))
                        ranks(group, EGROUPS, above4, equal4, before4, rank4)
                        assert step[0] == 7
                    if piece == 1:
                        then(nc.vector.scalar_tensor_tensor(out=choice[:].rearrange("p t (g s) -> p t g s", s=2),
                                                            in0=rank4[:, :, :, None].broadcast_to([P, GT, EGROUPS, 2]), scalar=float(TOP),
                                                            in1=choice[:].rearrange("p t (g s) -> p t g s", s=2), op0=ALU.is_lt, op1=ALU.mult))
                        ranks(choice, EXPERTS, above8, equal8, before8, rank8)
                        assert step[0] == 13
                    if piece == 2:
                        then(nc.vector.scalar_tensor_tensor(out=weight[:], in0=rank8[:], scalar=float(TOP), in1=score[:], op0=ALU.is_lt, op1=ALU.mult))
                        then(nc.vector.tensor_reduce(total[:], weight[:], AX.X, ALU.add))
                        then(nc.vector.tensor_scalar(total[:], total[:], 1e-20, None, ALU.add))
                        then(nc.vector.reciprocal(total[:], total[:]))
                        then(nc.vector.tensor_tensor(weight[:], weight[:], total[:, :, None].broadcast_to([P, GT, EXPERTS]), ALU.mult))
                        nc.vector.tensor_copy(w_parts[:, :, 0, :], weight[:]).then_inc(w_ok_hi, 1)
                        reach(dve, w_ok_hi, j + 1)
                        nc.vector.tensor_tensor(w_parts[:, :, 1, :], weight[:], w_parts[:, :, 0, :], ALU.subtract).then_inc(w_ok, 1)
                        assert step[0] == CH

                w_ok_hi = sem("w_ok_hi")

                def step(j, u):
                    if inside(j, GROUPS):
                        reach(dve, lo_ok, j)
                        for k in range(GT):
                            last = nc.vector.tensor_scalar(normed[:, k, :], m.x[:, j * GT + k, :], m.mean[:, j, k:k + 1],
                                                           m.rstd[:, j, k:k + 1], ALU.subtract, ALU.mult)
                        last.then_inc(norm_ok, 1)
                    for e in range(EXPERTS):
                        if inside(j - 1, GROUPS):
                            expert(j - 1, u - 1, e)
                        if e == 0 and inside(j - 2, GROUPS):
                            t = j - 2
                            reach(dve, down_ok, t * EXPERTS + EXPERTS)
                            for k in range(GT):
                                x = m.x[:, t * GT + k, :]
                                last = nc.vector.scalar_tensor_tensor(out=x, in0=out[k // 2][:, (k % 2) * D:(k % 2 + 1) * D],
                                                                      scalar=res_gate[:, 0:1], in1=x, op0=ALU.mult, op1=ALU.add)
                            last.then_inc(fin_ok, 1)
                        if e == 1 and inside(j, GROUPS):
                            for d in range(DC):
                                reach(dve, t_turn, 2 * j + (d + 1))
                                nc.vector.tensor_copy(n_turned[:, u % 2, d, :, :, :],
                                                      turn[d][:, :].rearrange("p (a t k) -> p a t k", a=2, t=GT)).then_inc(t_copied, 1)
                        if e in (3, 4, 5) and inside(j, GROUPS):
                            route(j, e - 3)
                        if e == EXPERTS - 1 and inside(j, GROUPS):
                            reach(dve, w_turn, j + 1)
                            nc.vector.tensor_copy(w_turned[0:2 * EXPERTS, u % 2, :], route_ps[0:2 * EXPERTS, :].bitcast(F16)[:, 0:GW]).then_inc(w_copied, 1)

                run_steps(dve, step, 2, head, GROUPS, lag)

            @block.scalar
            def _(act):
                nc.scalar.preload_act_table(ACT.Sigmoid)

                def step(j, u):
                    if inside(j, GROUPS):
                        reach(act, norm_ok, j + 1)
                        reach(act, t_turn, 2 * j)
                        nc.scalar.activation(n_parts[:, 0, :, :], normed[:], ACT.Copy).then_inc(hi_ok, 1)
                    for e in range(EXPERTS):
                        if inside(j - 1, GROUPS):
                            n = (j - 1) * EXPERTS + e
                            reach(act, gate_ok, n + 1)
                            reach(act, act1_ok, n - 1)
                            nc.scalar.activation(sig[:, e % 2, :], gate_ps[:, :], ACT.Sigmoid, scale=1.0 / WS).then_inc(sig_ok, 1)
                        if inside(j - 1, GROUPS):
                            reach(act, act3_ok, n + 1)
                            reach(act, down_ok, n - 1)
                            nc.scalar.activation(a_parts[:, e % 2, 0, :], act3[:, e % 2, :], ACT.Copy).then_inc(ahi_ok, 1)
                        if e == 2 and inside(j, GROUPS):
                            reach(act, logits_ok, j + 1)
                            reach(act, w_ok, j)
                            nc.scalar.activation(score[:].rearrange("p t e -> p (t e)"), route_ps[:, 0:GT * EXPERTS], ACT.Sigmoid).then_inc(score_ok, 1)

                run_steps(act, step, 2, head, GROUPS, lag)

            @block.gpsimd
            def _(pool):
                def step(j, u):
                    if inside(j, GROUPS):
                        reach(pool, hi_ok, j + 1)
                        nc.gpsimd.tensor_tensor(n_parts[:, 1, :, :], normed[:], n_parts[:, 0, :, :], ALU.subtract).then_inc(lo_ok, 1)
                    for e in range(EXPERTS):
                        if inside(j - 1, GROUPS):
                            reach(pool, ahi_ok, (j - 1) * EXPERTS + (e + 1))
                            nc.gpsimd.tensor_tensor(a_parts[:, e % 2, 1, :], act3[:, e % 2, :], a_parts[:, e % 2, 0, :],
                                                    ALU.subtract).then_inc(alo_ok, 1)

                run_steps(pool, step, 2, head, GROUPS, lag)


def build_program(nc, io):
    with ExitStack() as ctx:
        m = Shared()

        def sb(name, shape, dt=F32):
            return ctx.enter_context(nc.sbuf_tensor(name, shape, dt))

        def sem(name):
            return ctx.enter_context(nc.semaphore(name))

        m.x = sb("x", [P, TILES, D])
        m.gates, m.tanh_gates = sb("gates", [P, 4]), sb("tanh_gates", [P, 4])
        m.ident32, m.ident16 = sb("ident32", [P, P]), sb("ident16", [P, P], F16)
        m.ones32 = sb("ones32", [P, P])
        m.stats = sb("stats", [P, TILES, 6])
        m.mean2 = sb("mean", [P, TILES])
        m.root = sb("root", [P, TILES])
        m.rstd2 = sb("rstd", [P, TILES])
        m.rstd, m.mean = m.rstd2[:, :], m.mean2[:, :]
        with ExitStack() as held:
            m.ctx = held.enter_context(nc.sbuf_tensor("ctx", [P, TILES, D], F32))
            load_stage(nc, io, m, sem)
            deviation_stage(nc, m, sem, "dev0")
            attention_stage(nc, io, m, 0, sem)
            deviation_stage(nc, m, sem, "dev1")
            m.rstd, m.mean = (v[:, :].rearrange("p (j k) -> p j k", k=GT) for v in (m.rstd2, m.mean2))
            bitnet_stage(nc, io, m)
            m.rstd, m.mean = m.rstd2[:, :], m.mean2[:, :]
            deviation_stage(nc, m, sem, "dev2")
            attention_stage(nc, io, m, 1, sem)
            deviation_stage(nc, m, sem, "dev3")
        m.rstd, m.mean = (v[:, :].rearrange("p (j k) -> p j k", k=GT) for v in (m.rstd2, m.mean2))
        expert_stage(nc, io, m)


_INS = ["x", "ctx_1024", "g_xattn", "g_ffn", "L0_ffn_w1", "L0_ffn_conv_w", "L0_ffn_conv_b", "L0_ffn_w2",
        "L1_xattn_Wq", "L1_xattn_Wk", "L1_xattn_Wv", "L1_ffn_gate_weight", "L1_ffn_e_score_correction_bias",
        "L1_ffn_gate_proj", "L1_ffn_up_proj", "L1_ffn_down_proj"]


def kernel(**inputs):
    import numpy as np
    import concourse.bacc as bacc
    from concourse import mybir as mb
    from concourse.bass_utils import run_bass_kernel_spmd

    nc = bacc.Bacc("TRN2", target_bir_lowering=False, num_devices=1)
    arrays, io = {}, {}
    for name in _INS:
        a = np.ascontiguousarray(inputs[name])
        arrays[f"in_{name}"] = a
        io[name] = nc.dram_tensor(f"in_{name}", a.shape, mb.dt.from_np(a.dtype), kind="ExternalInput").ap()
    io["out"] = nc.dram_tensor("out", (TILES, P, D), mb.dt.float32, kind="ExternalOutput").ap()
    build_program(nc, io)
    result = run_bass_kernel_spmd(nc, [arrays], core_ids=[0])
    return result.results[0]["out"]
```

```python
from contextlib import ExitStack

import concourse.bass as bass
from concourse import mybir

F32 = mybir.dt.float32
F16 = mybir.dt.float16
ALU = mybir.AluOpType
ACT = mybir.ActivationFunctionType
AX = mybir.AxisListType

P = 128
TILES = 64
D = 256
DC = D // P
HEADS = 16
DH = D // HEADS
SLOT = 4 * DH
HG = 4
NG = HEADS // HG
PAIRS = HEADS // 2
UNROLL = 8
HID = 1024
HC = HID // P
GT = 4
GROUPS = TILES // GT
GW = GT * P
EXPERTS = 8
EGROUPS = 4
TOP = 2
WS = 32.0
XS = 64.0
LN_EPS = 1e-5
MAGIC = 12582912.0


def reach(engine, semaphore, value):
    if isinstance(value, int) and value <= 0:
        return
    engine.wait_ge(semaphore, value)


def run_steps(engine, step, period, head, count, tail):
    for i in range(head):
        step(i, i % period)
    with engine.Fori(head // period, count // period) as j:
        for u in range(period):
            step(j * period + u, u)
    for i in range(count, count + tail):
        step(i, i % period)


def head_of(g, k):
    return 8 * (g // 2) + 2 * k + g % 2, g % 2


def inside(t, count):
    return not isinstance(t, int) or 0 <= t < count


class Shared:
    pass


def load_stage(nc, io, m, sem):
    chunks = 4
    per = TILES // chunks
    x_in = [sem(f"x_loaded{c}") for c in range(chunks)]
    ctx_in = m.ctx_in = [sem(f"ctx_loaded{c}") for c in range(chunks)]
    gates_in = sem("gates_loaded")
    const_made = sem("constants_made")
    tanh_made = sem("tanh_made")
    x_view = io["x"].rearrange("b s d -> s b d")
    ctx_view = io["ctx_1024"].rearrange("b s d -> s b d")
    with nc.Block() as block:

        @block.sync
        def _(sp):
            for c in range(chunks):
                sp.dma_start(m.x[:, c * per:(c + 1) * per, :], x_view[:, c * per:(c + 1) * per, :]).then_inc(x_in[c], 16)
            for c in range(chunks):
                sp.dma_start(m.ctx[:, c * per:(c + 1) * per, :], ctx_view[:, c * per:(c + 1) * per, :]).then_inc(ctx_in[c], 16)
            sp.wait_ge(ctx_in[0], 16)

        @block.scalar
        def _(act):
            act.dma_start(m.gates[:, 0:2], io["g_xattn"].rearrange("(a n) -> a n", a=1).broadcast_to([P, 2])).then_inc(gates_in, 16)
            act.dma_start(m.gates[:, 2:4], io["g_ffn"].rearrange("(a n) -> a n", a=1).broadcast_to([P, 2])).then_inc(gates_in, 16)
            act.wait_ge(gates_in, 32)
            nc.scalar.activation(m.tanh_gates[:, :], m.gates[:, :], ACT.Tanh).then_inc(tanh_made, 1)
            act.wait_ge(tanh_made, 1)

        @block.gpsimd
        def _(pool):
            nc.gpsimd.memset(m.ident32[:, :], 1.0).then_inc(const_made, 1)
            pool.wait_ge(const_made, 1)
            nc.gpsimd.affine_select(out=m.ident32[:, :], in_=m.ident32[:, :], pattern=[[-1, P]], compare_op=ALU.is_equal,
                                    fill=0.0, base=0, channel_multiplier=1).then_inc(const_made, 1)
            pool.wait_ge(const_made, 2)
            nc.gpsimd.tensor_copy(m.ident16[:, :], m.ident32[:, :]).then_inc(const_made, 1)
            nc.gpsimd.memset(m.ones32[:, :], 1.0).then_inc(const_made, 1)
            pool.wait_ge(const_made, 4)

        @block.vector
        def _(dve):
            for c in range(chunks):
                dve.wait_ge(x_in[c], 16)
                with dve.Fori(c * per // UNROLL, (c + 1) * per // UNROLL) as j:
                    for u in range(UNROLL):
                        nc.vector.bn_stats(m.stats[:, j * UNROLL + u, :], m.x[:, j * UNROLL + u, :])


def deviation_stage(nc, m, sem, name, start_loads=None):
    joined = sem(f"{name}_joined")
    biased = sem(f"{name}_biased")
    rooted = sem(f"{name}_rooted")
    inverted = sem(f"{name}_inverted")
    with nc.Block() as block:
        if start_loads is not None:

            @block.sync
            def _(sp):
                start_loads(sp)

        @block.vector
        def _(dve):
            even_mean, even_dev, odd_mean, odd_dev = (m.stats[:, :, k] for k in (1, 2, 4, 5))
            nc.vector.tensor_tensor(m.mean2[:, :], even_mean, odd_mean, ALU.add).then_inc(joined, 1)
            nc.vector.tensor_tensor(m.root[:, :], even_mean, odd_mean, ALU.subtract).then_inc(joined, 1)
            nc.vector.tensor_tensor(m.rstd2[:, :], even_dev, odd_dev, ALU.add).then_inc(joined, 1)
            dve.wait_ge(joined, 3)
            nc.vector.tensor_scalar(m.mean2[:, :], m.mean2[:, :], 0.5, None, ALU.mult).then_inc(joined, 1)
            nc.vector.scalar_tensor_tensor(out=m.root[:, :], in0=m.root[:, :], scalar=D / 4.0, in1=m.root[:, :],
                                           op0=ALU.mult, op1=ALU.mult).then_inc(joined, 1)
            dve.wait_ge(joined, 5)
            nc.vector.tensor_tensor(m.rstd2[:, :], m.rstd2[:, :], m.root[:, :], ALU.add).then_inc(joined, 1)
            dve.wait_ge(joined, 6)
            nc.vector.tensor_scalar(m.rstd2[:, :], m.rstd2[:, :], 1.0 / D, LN_EPS, ALU.mult, ALU.add).then_inc(biased, 1)
            dve.wait_ge(rooted, 1)
            nc.vector.reciprocal(m.rstd2[:, :], m.root[:, :]).then_inc(inverted, 1)
            dve.wait_ge(inverted, 1)

        @block.scalar
        def _(act):
            act.wait_ge(biased, 1)
            nc.scalar.activation(m.root[:, :], m.rstd2[:, :], ACT.Sqrt).then_inc(rooted, 1)


def projection_weights(nc, io, m, w_hi, w_lo, psum, make_spread, sem):
    with ExitStack() as ctx:
        raw = ctx.enter_context(nc.sbuf_tensor("proj_raw", [P, 3, DC, D], F32))
        hi = ctx.enter_context(nc.sbuf_tensor("proj_hi", [P, 3, DC, D], F16))
        lo = ctx.enter_context(nc.sbuf_tensor("proj_lo", [P, 3, DC, D], F16))
        loaded, hi_ok, lo_ok, turned, copied = (sem(f"proj_{n}") for n in ("loaded", "hi_ok", "lo_ok", "turned", "copied"))

        def start_loads(sp):
            for n, name in enumerate(("L1_xattn_Wq", "L1_xattn_Wk", "L1_xattn_Wv")):
                sp.dma_start(raw[:, n, :, :], io[name].rearrange("(c p) d -> p c d", p=P)).then_inc(loaded, 16)

        deviation_stage(nc, m, sem, "deviation", start_loads)
        block = ctx.enter_context(nc.Block())

        @block.vector
        def _(dve):
            dve.wait_ge(loaded, 48)
            dve.wait_ge(hi_ok, 1)
            nc.vector.scalar_tensor_tensor(out=lo[:], in0=raw[:], scalar=WS, in1=hi[:], op0=ALU.mult, op1=ALU.subtract).then_inc(lo_ok, 1)
            for n in range(4):
                dve.wait_ge(turned, n + 1)
                dst = (w_hi, w_lo)[n // 2][:, n % 2, :]
                nc.vector.tensor_copy(dst, psum[n % 2][:, 0:6 * P]).then_inc(copied, 1)
            dve.wait_ge(copied, 4)

        @block.scalar
        def _(act):
            act.wait_ge(loaded, 48)
            nc.scalar.activation(hi[:], raw[:], ACT.Copy, scale=WS).then_inc(hi_ok, 1)

        @block.gpsimd
        def _(pool):
            make_spread(pool)

        @block.tensor
        def _(pe):
            for n in range(4):
                pe.wait_ge((hi_ok, lo_ok)[n // 2], 1)
                reach(pe, copied, n - 1)
                src = (hi, lo)[n // 2]
                for k in range(6):
                    last = nc.tensor.transpose(psum[n % 2][:, k * P:(k + 1) * P],
                                               src[:, k // 2, k % 2, (n % 2) * P:(n % 2 + 1) * P], m.ident16[:, :])
                last.then_inc(turned, 1)


def attention_stage(nc, io, m, layer, sem_scope):
    L = layer
    scale = WS if layer else 1.0
    TL, SL, EL, VL = (n + L for n in (1, 2, 3, 4))
    last_lag = 1 + VL
    head = UNROLL * (-(-last_lag // UNROLL))
    with ExitStack() as ctx:
        def sem(name):
            return ctx.enter_context(nc.semaphore(f"a{layer}_{name}"))

        def sb(name, shape, dt):
            return ctx.enter_context(nc.sbuf_tensor(f"a{layer}_{name}", shape, dt))

        def bank(name, dt=F32):
            return ctx.enter_context(nc.psum_tensor(f"a{layer}_{name}", [P, 2048 // (4 if dt == F32 else 2)], dt))

        turn = [bank("turn0", F16), bank("turn1", F16)]
        spread = sb("spread", [P, PAIRS, P], F16)
        spread_made = sem("spread_made")

        def make_spread(pool):
            nc.gpsimd.memset(spread[:], scale * scale).then_inc(spread_made, 1)
            pool.wait_ge(spread_made, 1)
            nc.gpsimd.affine_select(out=spread[:], in_=spread[:], pattern=[[-1, PAIRS], [0, P]],
                                    compare_op=ALU.is_equal, fill=0.0, base=0, channel_multiplier=1).then_inc(spread_made, 1)
            pool.wait_ge(spread_made, 2)
            nc.gpsimd.affine_select(out=spread[:], in_=spread[:], pattern=[[-1, PAIRS], [0, P]],
                                    compare_op=ALU.not_equal, fill=scale * scale, base=-SLOT, channel_multiplier=1).then_inc(spread_made, 1)
            pool.wait_ge(spread_made, 3)

        if layer:
            w_hi, w_lo = sb("w_hi", [P, DC, 3 * D], F16), sb("w_lo", [P, DC, 3 * D], F16)
            projection_weights(nc, io, m, w_hi, w_lo, turn, make_spread, sem)
        else:
            deviation_stage(nc, m, sem, "deviation")
        score = [bank(f"score{n}") for n in range(1 if layer else 2)]
        score_t = [bank("score_t0"), bank("score_t1")]
        out = bank("out")
        if layer:
            q_ps, kv_ps = bank("q_ps"), bank("kv_ps")
        else:
            unread = bank("unread")

        KR, NR = (2, 1) if layer else (UNROLL, 2)
        q_stack = sb("q_stack", [P, 2, HEADS, 4, DH], F16)
        k_stack = sb("k_stack", [P, KR, HEADS, 4, DH], F16)
        q_turned = sb("q_turned", [P, 4, HEADS // 2, P], F16)
        k_turned = sb("k_turned", [P, 4, HEADS // 2, P], F16)
        normed = sb("normed", [P, NR, D], F32)
        exp32 = sb("exp32", [P, NG, HG * P], F32)
        exp_hi = sb("exp_hi", [P, 2, NG, HG, P], F16)
        exp_lo = sb("exp_lo", [P, 2, NG, HG, P], F16)
        maxes = sb("maxes", [P, HEADS], F32)
        neg_max = sb("neg_max", [P, 2, 2, SLOT], F16)
        neg_max_t = sb("neg_max_t", [P, 2, P], F16)
        rsum = sb("rsum", [P, HEADS], F32)
        mixed = sb("mixed", [P, HEADS, DH], F32)
        gate = sb("gate", [P, 1], F32)
        if layer:
            split = sb("split", [P, 2, 4, D], F16)
            split_t = sb("split_t", [P, 2, 4 * DC, P], F16)
            v_hi = sb("v_hi", [P, UNROLL, HEADS, DH + 1], F16)
            v_lo = sb("v_lo", [P, UNROLL, HEADS, DH], F16)

        made, nf_ok, qh_ok, ql_ok, kh_ok, kl_ok = (sem(n) for n in ("made", "nf_ok", "qh_ok", "ql_ok", "kh_ok", "kl_ok"))
        q_turn, k_turn, m_turn = sem("q_turn"), sem("k_turn"), sem("m_turn")
        q_copied, k_copied, m_copied = sem("q_copied"), sem("k_copied"), sem("m_copied")
        scores_ok, max_ok, neg_ok = sem("scores_ok"), sem("max_ok"), sem("neg_ok")
        scores_t_ok, exp_ok, exp_lo_ok = sem("scores_t_ok"), sem("exp_ok"), sem("exp_lo_ok")
        values_ok, out_read, fin_ok = sem("values_ok"), sem("out_read"), sem("fin_ok")
        if layer:
            nh_ok, nl_ok, ch_ok, cl_ok = sem("nh_ok"), sem("nl_ok"), sem("ch_ok"), sem("cl_ok")
            s_turn, s_copied, q_proj, kv_proj, vl_ok = sem("s_turn"), sem("s_copied"), sem("q_proj"), sem("kv_proj"), sem("vl_ok")

        with nc.Block() as block:

            @block.vector
            def _(dve):
                nc.vector.memset(q_stack[:, :, :, 3, :], 0.0).then_inc(made, 1)
                nc.vector.memset(neg_max[:], 0.0).then_inc(made, 1)
                nc.vector.memset(k_stack[:, :, :, 3, :], 0.0).then_inc(made, 1)
                dve.wait_ge(made, 3)
                nc.vector.memset(k_stack[:, :, :, 3, 0:1], 1.0).then_inc(made, 1)
                nc.vector.tensor_scalar(gate[:], m.tanh_gates[:, layer:layer + 1], 1.0 / scale, None, ALU.mult).then_inc(made, 1)
                if layer:
                    nc.vector.memset(v_hi[:, :, :, DH:DH + 1], 1.0).then_inc(made, 1)
                dve.wait_ge(made, 5 + L)

            if not layer:

                @block.gpsimd
                def _(pool):
                    make_spread(pool)

        with nc.Block() as block:

            if layer:

                @block.sync
                def _(sp):
                    sp.wait_ge(cl_ok, 3 * EXPERTS)
                    load_experts(nc, sp, io, m)

            heads = lambda ap: ap.rearrange("p (h d) -> p h d", h=HEADS)
            twice = lambda ap: ap.rearrange("p (h a d) -> p h a d", h=HEADS, a=1).broadcast_to([P, HEADS, 2, DH])

            @block.tensor
            def _(pe):
                def turn_maxima(t, u):
                    reach(pe, neg_ok, t + 1)
                    nc.tensor.transpose(score[-1][:, :].bitcast(F16)[:, 0:P], neg_max[:, u % 2, :, :].rearrange("p r n -> p (r n)"),
                                        m.ident16[:, :]).then_inc(m_turn, 1)

                def do_scores(t, u, g, after_turn):
                    if g == 0:
                        reach(pe, q_copied, t + 1)
                        reach(pe, k_copied, t + 1)
                    reach(pe, max_ok, t * NG + (g + 1 - len(score)))
                    if g == len(score) - 1 and after_turn:
                        reach(pe, m_copied, t)
                    for k in range(HG):
                        h, half = head_of(g, k)
                        r = SLOT * half
                        last = nc.tensor.matmul(score[g % len(score)][:, k * P:(k + 1) * P], q_turned[r:r + SLOT, u % 4, h // 2, :],
                                                k_turned[r:r + SLOT, u % 4, h // 2, :], start=True, stop=True)
                    last.then_inc(scores_ok, 1)

                def do_scores_t(t, u, g):
                    if g == 0:
                        reach(pe, m_copied, t + 1)
                    reach(pe, exp_ok, t * NG + (g - 1))
                    for k in range(HG):
                        h, half = head_of(g, k)
                        r = SLOT * half
                        dst = score_t[g % 2][:, k * P:(k + 1) * P]
                        nc.tensor.matmul(dst, k_turned[r:r + SLOT, u % 4, h // 2, :], q_turned[r:r + SLOT, u % 4, h // 2, :],
                                         start=True, stop=False)
                        last = nc.tensor.matmul(dst, spread[r:r + SLOT, h // 2, :], neg_max_t[r:r + SLOT, u % 2, :], start=False, stop=True)
                    last.then_inc(scores_t_ok, 1)

                def do_values(t, u, g):
                    reach(pe, exp_lo_ok, t * NG + (g + 1))
                    if g == 0:
                        reach(pe, out_read, t)
                    for k in range(HG):
                        h, _ = head_of(g, k)
                        c = h * (DH + 1)
                        dst = out
                        if layer:
                            vh, vl = v_hi[:, u, h, :], v_lo[:, u, h, :]
                        else:
                            one = k_stack[:, u, h, :, :].rearrange("p a d -> p (a d)")
                            vh, vl = one[:, 2 * DH:3 * DH + 1], one[:, DH:2 * DH]
                        nc.tensor.matmul(dst[:, c:c + DH + 1], exp_hi[:, u % 2, g, k, :], vh, start=True, stop=False)
                        nc.tensor.matmul(dst[:, c:c + DH], exp_hi[:, u % 2, g, k, :], vl, start=False, stop=False)
                        last = nc.tensor.matmul(dst[:, c:c + DH + 1], exp_lo[:, u % 2, g, k, :], vh, start=False, stop=True)
                    if g == NG - 1:
                        last.then_inc(values_ok, 1)

                def turn_stack(dst, stack, signal):
                    for n in range(PAIRS):
                        last = nc.tensor.transpose(dst[:, n * P:(n + 1) * P], stack[:, 2 * n:2 * n + 2, :, :].rearrange("p h a d -> p (h a d)"),
                                                   m.ident16[:, :])
                    last.then_inc(signal, 1)

                def turn_q(i, t, u):
                    reach(pe, ql_ok, t + 1)
                    if layer and inside(i - 1, TILES):
                        reach(pe, s_copied, i)
                    else:
                        reach(pe, q_copied, t)
                    turn_stack(turn[0], q_stack[:, u % 2, :, :, :], q_turn)

                def turn_k(t, u):
                    reach(pe, kl_ok, t + 1)
                    reach(pe, k_copied, t)
                    turn_stack(turn[1], k_stack[:, u % KR, :, :, :], k_turn)

                if layer:
                    parts = ((0, w_hi), (0, w_lo), (2, w_hi))

                    def project(dst, first, cols, u, source, signal):
                        for n, (part, w) in enumerate(parts):
                            for c in range(DC):
                                last = nc.tensor.matmul(dst[:, 0:cols], split_t[:, u % 2, (part + source) * DC + c, :],
                                                        w[:, c, first:first + cols], start=(n == 0 and c == 0), stop=(n == 2 and c == DC - 1))
                        last.then_inc(signal, 1)

                def keep_busy():
                    for n in range(2):
                        nc.tensor.matmul(unread[:, :], m.ident16[:, :], spread[:, 0:HG, :].rearrange("p n k -> p (n k)"), start=True, stop=True)

                def step(i, u):
                    run_turn, run_scores, run_exps, run_values = (inside(i - lag, TILES) for lag in (TL, SL, EL, VL))
                    run_project = layer and inside(i - 1, TILES)
                    uT, uS, uE, uV = ((u - lag) % UNROLL for lag in (TL, SL, EL, VL))
                    if run_exps:
                        turn_maxima(i - EL, uE)
                    if run_project:
                        reach(pe, s_copied, i)
                        reach(pe, ql_ok, i - 1)
                        project(q_ps, 0, D, (u - 1) % UNROLL, 0, q_proj)
                    for g in range(NG):
                        if not layer and g % 2 == 0:
                            keep_busy()
                        if run_scores:
                            do_scores(i - SL, uS, g, run_exps)
                        if g == 1 and run_turn:
                            turn_q(i, i - TL, uT)
                        if g == 2 and run_project:
                            reach(pe, vl_ok, i - 1)
                            project(kv_ps, D, 2 * D, (u - 1) % UNROLL, 1, kv_proj)
                        if g == 3 and layer and inside(i, TILES):
                            reach(pe, nl_ok, i + 1)
                            reach(pe, cl_ok, i + 1)
                            if run_turn:
                                reach(pe, q_copied, i - (TL - 1))
                            else:
                                reach(pe, s_copied, i)
                            for n in range(4 * DC):
                                last = nc.tensor.transpose(turn[0][:, n * P:(n + 1) * P],
                                                           split[:, u % 2, n // DC, (n % DC) * P:(n % DC + 1) * P], m.ident16[:, :])
                            last.then_inc(s_turn, 1)
                        if run_values and g == 3:
                            for values_g in range(NG):
                                do_values(i - VL, uV, values_g)
                        if run_exps:
                            do_scores_t(i - EL, uE, g)
                        if g == (1 if layer else 2) and run_turn:
                            turn_k(i - TL, uT)

                run_steps(pe, step, UNROLL, head, TILES, last_lag)

            @block.vector
            def _(dve):
                def take_max(t, g):
                    reach(dve, scores_ok, t * NG + (g + 1))
                    nc.vector.tensor_reduce(maxes[:, g * HG:(g + 1) * HG],
                                            score[g % len(score)][:, :].rearrange("p (h k) -> p h k", h=HG),
                                            AX.X, ALU.max).then_inc(max_ok, 1)

                def step(i, u):
                    run_stats = inside(i - 1 - VL, TILES)
                    run_front, run_project = inside(i, TILES), layer and inside(i - 1, TILES)
                    run_turn, run_scores, run_exps, run_values = (inside(i - lag, TILES) for lag in (TL, SL, EL, VL))
                    uT, uS, uE, uV = ((u - lag) % UNROLL for lag in (TL, SL, EL, VL))
                    if run_exps:
                        reach(dve, m_turn, i - (EL - 1))
                        nc.vector.tensor_copy(neg_max_t[:, uE % 2, :], score[-1][:, :].bitcast(F16)[:, 0:P]).then_inc(m_copied, 1)
                    if run_stats:
                        t = i - (1 + VL)
                        reach(dve, out_read, t + 1)
                        nc.vector.scalar_tensor_tensor(out=m.x[:, t, :], in0=mixed[:].rearrange("p h d -> p (h d)"), scalar=gate[:, 0:1],
                                                       in1=m.x[:, t, :], op0=ALU.mult, op1=ALU.add).then_inc(fin_ok, 1)
                    if run_front:
                        if layer:
                            reach(dve, nh_ok, i)
                            reach(dve, nl_ok, i)
                        else:
                            reach(dve, qh_ok, i - 1)
                            reach(dve, ql_ok, i - 1)
                        nc.vector.tensor_scalar(normed[:, u % NR, :], m.x[:, i, :], m.mean[:, bass.ds(i, 1)], m.rstd[:, bass.ds(i, 1)],
                                                ALU.subtract, ALU.mult).then_inc(nf_ok, 1)
                    if run_stats:
                        reach(dve, fin_ok, t * 3 + 2)
                    if run_scores:
                        reach(dve, neg_ok, i - SL)
                        take_max(i - SL, 0)
                    if layer and inside(i - 2, TILES):
                        reach(dve, kh_ok, i - 1)
                        nc.vector.scalar_tensor_tensor(out=k_stack[:, (u - 2) % 2, :, 1, :], in0=heads(kv_ps[:, 0:D]), scalar=0.0,
                                                       in1=k_stack[:, (u - 2) % 2, :, 0, :], op0=ALU.max, op1=ALU.subtract).then_inc(kl_ok, 1)
                        nc.vector.scalar_tensor_tensor(out=v_lo[:, (u - 2) % UNROLL, :, :], in0=heads(kv_ps[:, D:2 * D]), scalar=0.0,
                                                       in1=v_hi[:, (u - 2) % UNROLL, :, 0:DH], op0=ALU.max, op1=ALU.subtract).then_inc(vl_ok, 1)
                    if run_project:
                        reach(dve, qh_ok, i)
                        nc.vector.scalar_tensor_tensor(out=q_stack[:, (u - 1) % 2, :, 2, :], in0=heads(q_ps[:, 0:D]), scalar=0.0,
                                                       in1=q_stack[:, (u - 1) % 2, :, 0, :], op0=ALU.max, op1=ALU.subtract).then_inc(ql_ok, 1)
                    if run_scores:
                        take_max(i - SL, 1)
                    if run_stats:
                        nc.vector.bn_stats(m.stats[:, t, :], m.x[:, t, :]).then_inc(fin_ok, 1)
                    if run_turn:
                        reach(dve, q_turn, i - (TL - 1))
                        nc.vector.tensor_copy(q_turned[:, uT % 4, :, :], turn[0][:, :].rearrange("p (n k) -> p n k", k=P)).then_inc(q_copied, 1)
                    if run_front:
                        if layer:
                            reach(dve, nh_ok, i + 1)
                            nc.vector.tensor_tensor(split[:, u % 2, 2, :], normed[:, u % NR, :], split[:, u % 2, 0, :],
                                                    ALU.subtract).then_inc(nl_ok, 1)
                        else:
                            reach(dve, qh_ok, i + 1)
                            nc.vector.tensor_tensor(q_stack[:, u % 2, :, 2, :], heads(normed[:, u % NR, :]), q_stack[:, u % 2, :, 0, :],
                                                    ALU.subtract).then_inc(ql_ok, 1)
                    if run_scores:
                        take_max(i - SL, 2)
                    if run_scores:
                        take_max(i - SL, 3)
                        reach(dve, max_ok, (i - SL) * NG + NG)
                        nc.vector.tensor_scalar(neg_max[:, uS % 2, :, 0:PAIRS].rearrange("p r (a k) -> p r a k", k=HG),
                                                maxes[:, :].rearrange("p (a r k) -> p r a k", r=2, k=HG), -1.0 / (scale * scale), None,
                                                ALU.mult).then_inc(neg_ok, 1)
                    if layer and run_front:
                        reach(dve, s_turn, i + 1)
                        nc.vector.tensor_copy(split_t[:, u % 2, :, :], turn[0][:, :].rearrange("p (n k) -> p n k", k=P)).then_inc(s_copied, 1)
                    if run_values:
                        t = i - VL
                        reach(dve, values_ok, t + 1)
                        sums = out[:, 0:HEADS * (DH + 1)].rearrange("p (h d) -> p h d", h=HEADS)
                        nc.vector.reciprocal(rsum[:, :], sums[:, :, DH]).then_inc(fin_ok, 1)
                        reach(dve, fin_ok, t * 3 + 1)
                        nc.vector.tensor_tensor(mixed[:], sums[:, :, 0:DH], rsum[:, :, None].broadcast_to([P, HEADS, DH]),
                                                ALU.mult).then_inc(out_read, 1)

                run_steps(dve, step, UNROLL, head, TILES, last_lag)

            @block.scalar
            def _(act):
                nc.scalar.preload_act_table(ACT.Exp)

                def do_exp(t, u, g):
                    reach(act, scores_t_ok, t * NG + (g + 1))
                    if g == 0:
                        reach(act, values_ok, t - 1)
                    reach(act, exp_lo_ok, t * NG + (g - NG + 1))
                    nc.scalar.activation(exp32[:, g, :], score_t[g % 2][:, :], ACT.Exp, scale=DH ** -0.5 / (scale * scale))
                    nc.scalar.activation(exp_hi[:, u % 2, g, :, :].rearrange("p h q -> p (h q)"), score_t[g % 2][:, :],
                                         ACT.Exp, scale=DH ** -0.5 / (scale * scale)).then_inc(exp_ok, 1)

                def step(i, u):
                    run_exps = inside(i - EL, TILES)
                    uE = (u - EL) % UNROLL
                    if not layer and isinstance(i, int) and i == head - 1:
                        for loaded in m.ctx_in[1:]:
                            act.wait_ge(loaded, 16)
                    if inside(i, TILES):
                        if layer:
                            reach(act, s_turn, i - 1)
                            nc.scalar.activation(split[:, u % 2, 1, :], m.ctx[:, i, :], ACT.Copy).then_inc(ch_ok, 1)
                        else:
                            reach(act, values_ok, i - 7)
                            nc.scalar.activation(k_stack[:, u, :, 0:3:2, :], twice(m.ctx[:, i, :]), ACT.Copy).then_inc(kh_ok, 1)
                    if layer and inside(i - 1, TILES):
                        reach(act, q_proj, i)
                        reach(act, k_turn, i - 2)
                        nc.scalar.activation(q_stack[:, (u - 1) % 2, :, 0:2, :], twice(q_ps[:, 0:D]), ACT.Relu).then_inc(qh_ok, 1)
                    if run_exps:
                        do_exp(i - EL, uE, 0)
                    if inside(i, TILES):
                        reach(act, nf_ok, i + 1)
                        if layer:
                            nc.scalar.activation(split[:, u % 2, 0, :], normed[:, u % NR, :], ACT.Copy).then_inc(nh_ok, 1)
                        else:
                            reach(act, q_turn, i - 1)
                            nc.scalar.activation(q_stack[:, u % 2, :, 0:2, :], twice(normed[:, u % NR, :]), ACT.Copy).then_inc(qh_ok, 1)
                    if run_exps:
                        do_exp(i - EL, uE, 1)
                    if inside(i - TL, TILES):
                        reach(act, k_turn, i - (TL - 1))
                        nc.scalar.activation(k_turned[:, (u - TL) % 4, :, :], turn[1][:, :].rearrange("p (n k) -> p n k", k=P), ACT.Copy).then_inc(k_copied, 1)
                    if run_exps:
                        do_exp(i - EL, uE, 2)
                    if layer and inside(i - 1, TILES):
                        reach(act, kv_proj, i)
                        nc.scalar.activation(k_stack[:, (u - 1) % 2, :, 0:3:2, :], twice(kv_ps[:, 0:D]), ACT.Relu)
                        reach(act, values_ok, i - 7)
                        nc.scalar.activation(v_hi[:, (u - 1) % UNROLL, :, 0:DH], heads(kv_ps[:, D:2 * D]), ACT.Relu).then_inc(kh_ok, 1)
                    if run_exps:
                        do_exp(i - EL, uE, 3)

                run_steps(act, step, UNROLL, head, TILES, last_lag)

            @block.gpsimd
            def _(pool):
                def step(i, u):
                    uE = (u - EL) % UNROLL
                    if inside(i, TILES):
                        if layer:
                            reach(pool, ch_ok, i + 1)
                            nc.gpsimd.tensor_tensor(split[:, u % 2, 3, :], m.ctx[:, i, :], split[:, u % 2, 1, :],
                                                    ALU.subtract).then_inc(cl_ok, 1)
                        else:
                            reach(pool, kh_ok, i + 1)
                            nc.gpsimd.tensor_tensor(k_stack[:, u, :, 1, :], heads(m.ctx[:, i, :]), k_stack[:, u, :, 0, :],
                                                    ALU.subtract).then_inc(kl_ok, 1)
                    if inside(i - EL, TILES):
                        for g in range(NG):
                            reach(pool, exp_ok, (i - EL) * NG + (g + 1))
                            nc.gpsimd.tensor_tensor(exp_lo[:, uE % 2, g, :, :].rearrange("p h q -> p (h q)"), exp32[:, g, :],
                                                    exp_hi[:, uE % 2, g, :, :].rearrange("p h q -> p (h q)"),
                                                    ALU.subtract).then_inc(exp_lo_ok, 1)

                run_steps(pool, step, UNROLL, head, TILES, last_lag)


def bitnet_stage(nc, io, m):
    lag, head = 3, 4
    with ExitStack() as ctx:
        def sem(name):
            return ctx.enter_context(nc.semaphore(f"b_{name}"))

        def sb(name, shape, dt=F32):
            return ctx.enter_context(nc.sbuf_tensor(f"b_{name}", shape, dt))

        def bank(name, dt=F32):
            return ctx.enter_context(nc.psum_tensor(f"b_{name}", [P, 2048 // (4 if dt == F32 else 2)], dt))

        turn = [bank("turn0", F16), bank("turn1", F16)]
        hid = [bank("hid0"), bank("hid1")]
        out = [bank("out0"), bank("out1")]
        peaks, spread_ps = bank("peaks"), bank("spread_ps")
        w1t = sb("w1t", [P, DC, HID], F16)
        w2t = sb("w2t", [P, HC, D], F16)
        taps = sb("taps", [P, HC, 3])
        conv_b = sb("conv_b", [P, HC])
        weight_mean = sb("weight_mean", [P, 2])
        in_back = sb("in_back", [P, 1])
        out_back = sb("out_back", [P, 1])

        with ExitStack() as prep:
            raw = [prep.enter_context(nc.sbuf_tensor(f"b_raw{n}", [P, 2048], F32)) for n in range(2)]
            scaled = [prep.enter_context(nc.sbuf_tensor(f"b_scaled{n}", [P, 2048], F32)) for n in range(2)]
            tern = [prep.enter_context(nc.sbuf_tensor(f"b_tern{n}", [P, 2048], F16)) for n in range(2)]
            rows = prep.enter_context(nc.sbuf_tensor("b_rows", [P, 2], F32))
            inverse = prep.enter_context(nc.sbuf_tensor("b_inverse", [P, 2], F32))
            w_in, taps_in, rows_ok, total_ok, chain, turned, copied, w1_in = (sem(n) for n in (
                "w_in", "taps_in", "rows_ok", "total_ok", "chain", "turned", "copied", "w1_in"))

            def start_loads(sp):
                sp.dma_start(raw[0][:].rearrange("p (c d) -> p c d", c=HC), io["L0_ffn_w1"].rearrange("(c p) d -> p c d", p=P)).then_inc(w1_in, 16)
                sp.dma_start(raw[1][:].rearrange("p (c d) -> p c d", c=DC), io["L0_ffn_w2"].rearrange("(c p) d -> p c d", p=P)).then_inc(w_in, 16)
                with nc.allow_non_contiguous_dma(reason="small"):
                    sp.dma_start(taps[:], io["L0_ffn_conv_w"].rearrange("(c p) a k -> p c (a k)", p=P)).then_inc(taps_in, 16)
                    sp.dma_start(conv_b[:], io["L0_ffn_conv_b"].rearrange("(c p) -> p c", p=P)).then_inc(taps_in, 16)

            deviation_stage(nc, m, sem, "deviation", start_loads)
            block = prep.enter_context(nc.Block())

            @block.tensor
            def _(pe):
                pe.wait_ge(rows_ok, 2)
                nc.tensor.matmul(peaks[:, 0:2], m.ones32[:, :], rows[:, :], start=True, stop=True).then_inc(total_ok, 1)
                pe.wait_ge(chain, 13)
                for n in range(4):
                    reach(pe, copied, n - 1)
                    for k in range(8):
                        q = (n % 2) * 8 + k
                        a, b = (q % HC, q // HC) if n < 2 else (q % DC, q // DC)
                        width = D if n < 2 else HID
                        last = nc.tensor.transpose(turn[n % 2][:, k * P:(k + 1) * P],
                                                   tern[n // 2][:, a * width + b * P:a * width + (b + 1) * P], m.ident16[:, :])
                    last.then_inc(turned, 1)

            @block.vector
            def _(dve):
                step = [0]

                def then(instruction):
                    step[0] += 1
                    instruction.then_inc(chain, 1)
                    dve.wait_ge(chain, step[0])

                dve.wait_ge(w1_in, 16)
                nc.vector.tensor_reduce(rows[:, 0:1], raw[0][:], AX.X, ALU.add, apply_absolute_value=True).then_inc(rows_ok, 1)
                dve.wait_ge(w_in, 16)
                nc.vector.tensor_reduce(rows[:, 1:2], raw[1][:], AX.X, ALU.add, apply_absolute_value=True).then_inc(rows_ok, 1)
                dve.wait_ge(total_ok, 1)
                then(nc.vector.tensor_scalar(weight_mean[:], peaks[:, 0:2], 1.0 / (HID * D), 1e-5, ALU.mult, ALU.max))
                then(nc.vector.reciprocal(inverse[:], weight_mean[:]))
                for n in range(2):
                    then(nc.vector.tensor_scalar(scaled[n][:], raw[n][:], inverse[:, n:n + 1], MAGIC, ALU.mult, ALU.add))
                    then(nc.vector.tensor_scalar(scaled[n][:], scaled[n][:], MAGIC, 1.0, ALU.subtract, ALU.min))
                    then(nc.vector.tensor_scalar(tern[n][:], scaled[n][:], -1.0, None, ALU.max))
                dve.wait_ge(taps_in, 32)
                then(nc.vector.tensor_scalar(taps[:], taps[:], 1.0 / XS, None, ALU.mult))
                then(nc.vector.tensor_scalar(in_back[:], weight_mean[:, 0:1], XS / 127.0, None, ALU.mult))
                then(nc.vector.tensor_scalar(out_back[:], weight_mean[:, 1:2], 1.0 / 127.0, m.tanh_gates[:, 2:3], ALU.mult, ALU.mult))
                then(nc.vector.memset(rows[:], 0.0))
                then(nc.vector.memset(inverse[:], 0.0))
                for n in range(4):
                    dve.wait_ge(turned, n + 1)
                    dst = w1t[:, n % 2, :] if n < 2 else w2t[:, 4 * (n % 2):4 * (n % 2) + 4, :].rearrange("p c d -> p (c d)")
                    nc.vector.tensor_copy(dst, turn[n % 2][:, :]).then_inc(copied, 1)
                dve.wait_ge(copied, 4)

        normed = sb("normed", [P, GT, D])
        x_parts = sb("x_parts", [P, 2, GT, D], F16)
        x_turned = sb("x_turned", [P, DC, 2, GT, P], F16)
        peak_in, scale_in, back_in = sb("peak_in", [P, GT]), sb("scale_in", [P, GT]), sb("back_in", [P, GT])
        peak_mid, scale_mid, back_mid = sb("peak_mid", [P, GT]), sb("scale_mid", [P, GT]), sb("back_mid", [P, 2, GT])
        shifted = sb("shifted", [P, 2, GW])
        hidden = sb("hidden", [P, 2, HC, GW])
        peak_t, peak_half = sb("peak_t", [P, GW]), sb("peak_half", [P, GW])
        scales = sb("scales", [P, GW])
        diagonal = sb("diagonal", [P, GT, P])
        ints = sb("ints", [P, HC, GW], F16)

        POOL_CHUNKS = 4
        ROUND_ORDER = (4, 5, 0, 6, 1, 7, 2, 3)
        SPREAD_AT = 3
        scales_ok, pool_mult = sem("scales_ok"), sem("pool_mult")
        (norm_ok, in_ok, deq_ok, hi_ok, lo_ok, t_turn, t_copied, hid_ok, tap_r, tap_l, conv_ok, hidden_ok,
         peak_ok, peak_turn, mid_ok, diag_ok, spread_ok, mult_ok, ints_ok, out_ok, fin_ok) = (sem(n) for n in (
             "norm_ok", "in_ok", "deq_ok", "hi_ok", "lo_ok", "t_turn", "t_copied", "hid_ok", "tap_r", "tap_l", "conv_ok",
             "hidden_ok", "peak_ok", "peak_turn", "mid_ok", "diag_ok", "spread_ok", "mult_ok", "ints_ok", "out_ok", "fin_ok"))

        with nc.Block() as block:

            @block.tensor
            def _(pe):
                def first_product(t, u, c):
                    if c == 0:
                        reach(pe, t_copied, 2 * t + 2)
                    reach(pe, tap_r, t * HC + (c - 1))
                    for d in range(DC):
                        for part in range(2):
                            last = nc.tensor.matmul(hid[c % 2][:, :], w1t[:, d, c * P:(c + 1) * P],
                                                    x_turned[:, d, part, :, :].rearrange("p t k -> p (t k)"),
                                                    start=(d == 0 and part == 0), stop=(d == DC - 1 and part == 1))
                    last.then_inc(hid_ok, 1)

                def second_product(t, half):
                    reach(pe, ints_ok, t * HC + (half + 1) * HC // 2)
                    if half == 0:
                        reach(pe, fin_ok, t)
                    for n in range(half * HC // 2, (half + 1) * HC // 2):
                        c = ROUND_ORDER[n]
                        for k in range(GT):
                            last = nc.tensor.matmul(out[k // 2][:, (k % 2) * D:(k % 2 + 1) * D], ints[:, c, k * P:(k + 1) * P], w2t[:, c, :],
                                                    start=(n == 0 and k % 2 == 0), stop=(n == HC - 1), skip_group_check=True)
                    if half == 1:
                        last.then_inc(out_ok, 1)

                def step(j, u):
                    for c in range(HC):
                        if inside(j - 1, GROUPS):
                            first_product(j - 1, u - 1, c)
                        if c == 1 and inside(j - 2, GROUPS):
                            reach(pe, peak_ok, (j - 2) * 3 + 3)
                            for k in range(GT):
                                last = nc.tensor.transpose(peaks[:, k * P:(k + 1) * P], peak_t[:, k * P:(k + 1) * P], m.ident32[:, :])
                            last.then_inc(peak_turn, 1)
                        if c == 1 and inside(j - 3, GROUPS):
                            second_product(j - 3, 1)
                        if c == SPREAD_AT and inside(j - 2, GROUPS):
                            reach(pe, diag_ok, j - 1)
                            nc.tensor.matmul(spread_ps[:, :], m.ones32[:, :], diagonal[:].rearrange("p t k -> p (t k)"),
                                             start=True, stop=True).then_inc(spread_ok, 1)
                    if inside(j, GROUPS):
                        reach(pe, hi_ok, j + 1)
                        reach(pe, lo_ok, j + 1)
                        for d in range(DC):
                            reach(pe, t_copied, 2 * j + (d - 1))
                            for part in range(2):
                                for k in range(GT):
                                    n = part * GT + k
                                    last = nc.tensor.transpose(turn[d][:, n * P:(n + 1) * P], x_parts[:, part, k, d * P:(d + 1) * P], m.ident16[:, :])
                            last.then_inc(t_turn, 1)
                    if inside(j - 2, GROUPS):
                        second_product(j - 2, 0)

                run_steps(pe, step, 2, head, GROUPS, lag)

            @block.vector
            def _(dve):
                def convolve(t, u, c):
                    reach(dve, tap_l, t * HC + (c + 1))
                    dst = hidden[:, u % 2, c, :].rearrange("p (t k) -> p t k", k=P)[:, :, 0:P - 1]
                    nc.vector.scalar_tensor_tensor(out=dst, in0=hid[c % 2][:, :].rearrange("p (t k) -> p t k", k=P)[:, :, 1:P],
                                                   scalar=taps[:, c, 2:3], in1=dst, op0=ALU.mult, op1=ALU.add).then_inc(tap_r, 1)

                def largest(t, u, half):
                    last = half == 1
                    reach(dve, hidden_ok, t * HC + (HC if last else HC // 2))
                    dst = peak_half if last else peak_t
                    src = hidden[:, u % 2, half * HC // 2:(half + 1) * HC // 2, :].rearrange("p c k -> p k c")
                    nc.vector.tensor_reduce(dst[:, :], src, AX.X, ALU.max, apply_absolute_value=True).then_inc(peak_ok, 1)
                    if last:
                        reach(dve, peak_ok, t * 3 + 2)
                        nc.vector.tensor_tensor(peak_t[:, :], peak_t[:, :], peak_half[:, :], ALU.max).then_inc(peak_ok, 1)

                def rescale(t, u, c):
                    if c == POOL_CHUNKS:
                        reach(dve, scales_ok, t + 1)
                    nc.vector.tensor_tensor(hidden[:, u % 2, c, :], hidden[:, u % 2, c, :], scales[:, :], ALU.mult).then_inc(mult_ok, 1)

                def round_hidden(t, u, n):
                    c = ROUND_ORDER[n]
                    if c < POOL_CHUNKS:
                        reach(dve, pool_mult, t * POOL_CHUNKS + (c + 1))
                    else:
                        reach(dve, mult_ok, t * (HC - POOL_CHUNKS) + (c - POOL_CHUNKS + 1))
                    if n == 0:
                        reach(dve, out_ok, t)
                    nc.vector.tensor_scalar(ints[:, c, :], hidden[:, u % 2, c, :], MAGIC, MAGIC, ALU.add, ALU.subtract).then_inc(ints_ok, 1)

                def token_scales(t, u):
                    reach(dve, peak_turn, t + 1)
                    nc.vector.tensor_reduce(peak_mid[:], peaks[:, :].rearrange("p (t k) -> p t k", k=P), AX.X, ALU.max).then_inc(mid_ok, 1)
                    reach(dve, mid_ok, t * 4 + 1)
                    nc.vector.tensor_scalar(peak_mid[:], peak_mid[:], 1e-5, None, ALU.max).then_inc(mid_ok, 1)
                    reach(dve, mid_ok, t * 4 + 2)
                    nc.vector.reciprocal(scale_mid[:], peak_mid[:]).then_inc(mid_ok, 1)
                    nc.vector.tensor_scalar(back_mid[:, u % 2, :], peak_mid[:], out_back[:, 0:1], None, ALU.mult)
                    reach(dve, mid_ok, t * 4 + 3)
                    nc.vector.tensor_scalar(scale_mid[:], scale_mid[:], 127.0, None, ALU.mult).then_inc(mid_ok, 1)
                    reach(dve, mid_ok, t * 4 + 4)
                    for k in range(GT):
                        last = nc.vector.tensor_scalar(diagonal[:, k, :], m.ident32[:, :], scale_mid[:, k:k + 1], None, ALU.mult)
                    last.then_inc(diag_ok, 1)

                def quantise(j, part):
                    if part == 0:
                        reach(dve, lo_ok, j)
                        for k in range(GT):
                            last = nc.vector.tensor_scalar(normed[:, k, :], m.x[:, j * GT + k, :], m.mean[:, j, k:k + 1],
                                                           m.rstd[:, j, k:k + 1], ALU.subtract, ALU.mult)
                        last.then_inc(norm_ok, 1)
                    if part == 1:
                        reach(dve, norm_ok, j + 1)
                        nc.vector.tensor_reduce(peak_in[:], normed[:], AX.X, ALU.max, apply_absolute_value=True).then_inc(in_ok, 1)
                    if part == 2:
                        reach(dve, in_ok, j * 4 + 1)
                        nc.vector.tensor_scalar(peak_in[:], peak_in[:], 1e-5, None, ALU.max).then_inc(in_ok, 1)
                        reach(dve, in_ok, j * 4 + 2)
                        nc.vector.reciprocal(scale_in[:], peak_in[:]).then_inc(in_ok, 1)
                        nc.vector.tensor_scalar(back_in[:], peak_in[:], in_back[:, 0:1], None, ALU.mult)
                        reach(dve, in_ok, j * 4 + 3)
                        nc.vector.tensor_scalar(scale_in[:], scale_in[:], 127.0, None, ALU.mult).then_inc(in_ok, 1)
                    if part == 3:
                        reach(dve, in_ok, j * 4 + 4)
                        for k in range(GT):
                            last = nc.vector.tensor_scalar(normed[:, k, :], normed[:, k, :], scale_in[:, k:k + 1], MAGIC, ALU.mult, ALU.add)
                        last.then_inc(deq_ok, 1)
                    if part == 4:
                        reach(dve, deq_ok, j * 2 + 1)
                        for k in range(GT):
                            last = nc.vector.tensor_scalar(normed[:, k, :], normed[:, k, :], MAGIC, back_in[:, k:k + 1], ALU.subtract, ALU.mult)
                        last.then_inc(deq_ok, 1)

                def step(j, u):
                    for c in range(HC + 2):
                        if c < HC and inside(j - 1, GROUPS):
                            convolve(j - 1, u - 1, c)
                        if c == 1 and inside(j - 3, GROUPS):
                            t = j - 3
                            reach(dve, out_ok, t + 1)
                            for k in range(GT):
                                x = m.x[:, t * GT + k, :]
                                last = nc.vector.scalar_tensor_tensor(out=x, in0=out[k // 2][:, (k % 2) * D:(k % 2 + 1) * D],
                                                                      scalar=back_mid[:, (u - 3) % 2, k:k + 1], in1=x, op0=ALU.mult, op1=ALU.add)
                            last.then_inc(fin_ok, 1)
                        if c == 1 and inside(j - 2, GROUPS):
                            token_scales(j - 2, u)
                        if c == 2 and inside(j - 3, GROUPS):
                            reach(dve, fin_ok, j - 2)
                        if c in (0, 2, 3, 4, 5) and inside(j, GROUPS):
                            quantise(j, (0, 2, 3, 4, 5).index(c))
                        if c == 2 and inside(j - 3, GROUPS):
                            for k in range(GT):
                                nc.vector.bn_stats(m.stats[:, (j - 3) * GT + k, :], m.x[:, (j - 3) * GT + k, :])
                        if inside(j - 2, GROUPS):
                            if 5 <= c < 5 + HC - POOL_CHUNKS:
                                rescale(j - 2, u - 2, c - 5 + POOL_CHUNKS)
                            for n in {6: (0, 1), 7: (2, 3), 8: (4, 5), 9: (6, 7)}.get(c, ()):
                                round_hidden(j - 2, u - 2, n)
                        if c == 7 and inside(j, GROUPS):
                            reach(dve, hi_ok, j + 1)
                            nc.vector.tensor_tensor(x_parts[:, 1, :, :], normed[:], x_parts[:, 0, :, :], ALU.subtract).then_inc(lo_ok, 1)
                        if c in (HC - 1, HC + 1) and inside(j - 1, GROUPS):
                            largest(j - 1, u - 1, int(c > HC))

                run_steps(dve, step, 2, head, GROUPS, lag)

            @block.scalar
            def _(act):
                nc.scalar.preload_act_table(ACT.Silu)

                def split(j):
                    reach(act, deq_ok, j * 2 + 2)
                    reach(act, t_turn, 2 * j)
                    nc.scalar.activation(x_parts[:, 0, :, :], normed[:], ACT.Copy).then_inc(hi_ok, 1)

                def step(j, u):
                    for c in range(HC + 3):
                        if c < HC and inside(j - 1, GROUPS):
                            n = (j - 1) * HC + c
                            reach(act, hid_ok, n + 1)
                            if c == 0:
                                reach(act, ints_ok, (j - 2) * HC)
                            reach(act, conv_ok, n - 1)
                            nc.scalar.activation(hidden[:, (u - 1) % 2, c, :], hid[c % 2][:, :], ACT.Identity, scale=taps[:, c, 1:2],
                                                 bias=conv_b[:, c:c + 1])
                            nc.scalar.activation(shifted[:, c % 2, :], hid[c % 2][:, :], ACT.Copy, scale=taps[:, c, 0:1]).then_inc(tap_l, 1)
                        if c == SPREAD_AT and inside(j - 2, GROUPS):
                            reach(act, spread_ok, j - 1)
                            reach(act, ints_ok, (j - 2) * HC)
                            nc.scalar.activation(scales[:, :], spread_ps[:, :], ACT.Copy).then_inc(scales_ok, 1)
                        if c == 7 and inside(j, GROUPS):
                            split(j)
                        if c >= 3 and inside(j - 1, GROUPS):
                            n = (j - 1) * HC + c - 3
                            reach(act, conv_ok, n + 1)
                            nc.scalar.activation(hidden[:, (u - 1) % 2, c - 3, :], hidden[:, (u - 1) % 2, c - 3, :], ACT.Silu).then_inc(hidden_ok, 1)

                    if inside(j, GROUPS):
                        for d in range(DC):
                            reach(act, t_turn, 2 * j + (d + 1))
                            nc.scalar.activation(x_turned[:, d, :, :, :], turn[d][:, :].rearrange("p (a t k) -> p a t k", a=2, t=GT),
                                                 ACT.Copy).then_inc(t_copied, 1)

                run_steps(act, step, 2, head, GROUPS, lag)

            @block.gpsimd
            def _(pool):
                def step(j, u):
                    for c in range(HC):
                        if inside(j - 1, GROUPS):
                            n = (j - 1) * HC + c
                            reach(pool, tap_l, n + 1)
                            reach(pool, tap_r, n + 1)
                            dst = hidden[:, (u - 1) % 2, c, :].rearrange("p (t k) -> p t k", k=P)[:, :, 1:P]
                            nc.gpsimd.tensor_tensor(dst, dst, shifted[:, c % 2, :].rearrange("p (t k) -> p t k", k=P)[:, :, 0:P - 1],
                                                    ALU.add).then_inc(conv_ok, 1)
                        if 4 <= c < 4 + POOL_CHUNKS and inside(j - 2, GROUPS):
                            if c == 4:
                                reach(pool, scales_ok, j - 1)
                            nc.gpsimd.tensor_tensor(hidden[:, (u - 2) % 2, c - 4, :], hidden[:, (u - 2) % 2, c - 4, :], scales[:, :],
                                                    ALU.mult).then_inc(pool_mult, 1)

                run_steps(pool, step, 2, head, GROUPS, lag)


def load_experts(nc, sp, io, m):
    with nc.allow_non_contiguous_dma(reason="small"):
        for c in range(DC):
            sp.dma_start(m.router_raw[:, c, :], io["L1_ffn_gate_weight"][:, c * P:(c + 1) * P].rearrange("e p -> p e")).then_inc(m.expert_loaded[3], 16)
    sp.dma_start(m.router_bias[:], io["L1_ffn_e_score_correction_bias"].rearrange("(a n) -> a n", a=1).broadcast_to([P, EXPERTS])).then_inc(m.expert_loaded[3], 16)
    for n, name in enumerate(("L1_ffn_gate_proj", "L1_ffn_up_proj")):
        sp.dma_start(m.expert_raw[n], io[name].rearrange("e i d -> i e d")).then_inc(m.expert_loaded[n], 16)
    down = io["L1_ffn_down_proj"].rearrange("e (c p) i -> c p e i", p=P)
    for c in range(DC):
        sp.dma_start(m.expert_raw[2][:, :, c * P:(c + 1) * P], down[c]).then_inc(m.expert_loaded[2], 16)
    for n, count in enumerate((16, 16, 32, 48)):
        sp.wait_ge(m.expert_loaded[n], count)


def expert_stage(nc, io, m):
    lag, head = 2, 2
    with ExitStack() as ctx:
        def sem(name):
            return ctx.enter_context(nc.semaphore(f"e_{name}"))

        def sb(name, shape, dt=F32):
            return ctx.enter_context(nc.sbuf_tensor(f"e_{name}", shape, dt))

        def bank(name, dt=F32):
            return ctx.enter_context(nc.psum_tensor(f"e_{name}", [P, 2048 // (4 if dt == F32 else 2)], dt))

        turn = [bank("turn0", F16), bank("turn1", F16)]
        gate_ps, up_ps, weight_ps, route_ps = (bank(n) for n in ("gate_ps", "up_ps", "weight_ps", "route_ps"))
        out = [bank("out0"), bank("out1")]
        wt = {name: sb(f"{name}_t", [P, 2, DC, EXPERTS * P], F16) for name in ("gate", "up")}
        down_t = sb("down_t", [P, 2, EXPERTS, D], F16)
        router = sb("router", [P, 2, DC, EXPERTS], F16)
        bias = m.router_bias
        select = sb("select", [4 * EXPERTS, EXPERTS, P], F16)
        before4 = sb("before4", [P, EGROUPS, EGROUPS])
        before8 = sb("before8", [P, EXPERTS, EXPERTS])
        res_gate = sb("res_gate", [P, 1])

        with ExitStack() as prep:
            raw, raw_r, loaded = m.expert_raw, m.router_raw, m.expert_loaded
            hi = [prep.enter_context(nc.sbuf_tensor(f"e_hi{n}", [P, EXPERTS, D], F16)) for n in range(3)]
            lo = [prep.enter_context(nc.sbuf_tensor(f"e_lo{n}", [P, EXPERTS, D], F16)) for n in range(3)]
            turn_lo = [bank[:, :].bitcast(F16) for bank in out]
            hi_made, lo_made, hi_turned, lo_turned, hi_copied, lo_copied, const_ok, route_ok = (sem(n) for n in (
                "hi_made", "lo_made", "hi_turned", "lo_turned", "hi_copied", "lo_copied", "const_ok", "route_ok"))

            def turned_to(n, part, c):
                if n < 2:
                    return wt[("gate", "up")[n]][:, part, c, :], lambda ap: ap
                return down_t[:, part, :, c * P:(c + 1) * P], lambda ap: ap.rearrange("p (e k) -> p e k", k=P)
            block = prep.enter_context(nc.Block())

            @block.gpsimd
            def _(pool):
                nc.gpsimd.memset(select[:], 1.0 / (WS * WS)).then_inc(const_ok, 1)
                nc.gpsimd.memset(before4[:], 1.0).then_inc(const_ok, 1)
                nc.gpsimd.memset(before8[:], 1.0).then_inc(const_ok, 1)
                pool.wait_ge(const_ok, 3)
                nc.gpsimd.affine_select(out=before4[:], in_=before4[:], pattern=[[1, EGROUPS], [-1, EGROUPS]], compare_op=ALU.is_gt,
                                        fill=0.0, base=0, channel_multiplier=0).then_inc(const_ok, 1)
                nc.gpsimd.affine_select(out=before8[:], in_=before8[:], pattern=[[1, EXPERTS], [-1, EXPERTS]], compare_op=ALU.is_gt,
                                        fill=0.0, base=0, channel_multiplier=0).then_inc(const_ok, 1)
                nc.gpsimd.affine_select(out=select[:], in_=select[:], pattern=[[-1, EXPERTS], [0, P]], compare_op=ALU.is_equal,
                                        fill=0.0, base=0, channel_multiplier=1).then_inc(const_ok, 1)
                pool.wait_ge(const_ok, 6)
                nc.gpsimd.affine_select(out=select[:], in_=select[:], pattern=[[-1, EXPERTS], [0, P]], compare_op=ALU.not_equal,
                                        fill=1.0 / (WS * WS), base=-EXPERTS, channel_multiplier=1).then_inc(const_ok, 1)
                pool.wait_ge(const_ok, 7)

            @block.scalar
            def _(act):
                for n in range(4):
                    if n < 3:
                        act.wait_ge(loaded[n], 16 if n < 2 else 32)
                        nc.scalar.activation(hi[n][:], raw[n], ACT.Copy, scale=WS).then_inc(hi_made, 1)
                    for c in range(DC if n else 0):
                        act.wait_ge(hi_turned, 2 * (n - 1) + c + 1)
                        dst, blocks = turned_to(n - 1, 0, c)
                        nc.scalar.activation(dst, blocks(turn[c][:, :]), ACT.Copy).then_inc(hi_copied, 1)
                act.wait_ge(hi_copied, 6)

            @block.vector
            def _(dve):
                for n in range(4):
                    if n < 3:
                        dve.wait_ge(loaded[n], 16 if n < 2 else 32)
                        dve.wait_ge(hi_made, n + 1)
                        nc.vector.scalar_tensor_tensor(out=lo[n][:], in0=raw[n], scalar=WS, in1=hi[n][:],
                                                       op0=ALU.mult, op1=ALU.subtract).then_inc(lo_made, 1)
                    for c in range(DC if n else 0):
                        dve.wait_ge(lo_turned, 2 * (n - 1) + c + 1)
                        dst, blocks = turned_to(n - 1, 1, c)
                        nc.vector.tensor_copy(dst, blocks(turn_lo[c])).then_inc(lo_copied, 1)
                    if n == 0:
                        dve.wait_ge(loaded[3], 48)
                        nc.vector.tensor_copy(router[:, 0, :, :], raw_r[:]).then_inc(route_ok, 1)
                        dve.wait_ge(route_ok, 1)
                        nc.vector.tensor_tensor(router[:, 1, :, :], raw_r[:], router[:, 0, :, :], ALU.subtract).then_inc(route_ok, 1)
                        nc.vector.tensor_scalar(res_gate[:], m.tanh_gates[:, 3:4], 1.0 / WS, None, ALU.mult).then_inc(route_ok, 1)
                dve.wait_ge(lo_copied, 6)
                dve.wait_ge(route_ok, 3)

            @block.tensor
            def _(pe):
                for n in range(3):
                    for part, (made, turned, copied, dst, src) in enumerate((
                            (hi_made, hi_turned, hi_copied, turn, hi), (lo_made, lo_turned, lo_copied, turn_lo, lo))):
                        pe.wait_ge(made, n + 1)
                        for c in range(DC):
                            reach(pe, copied, 2 * n + c - 1)
                            for e in range(EXPERTS):
                                last = nc.tensor.transpose(dst[c][:, e * P:(e + 1) * P], src[n][:, e, c * P:(c + 1) * P], m.ident16[:, :])
                            last.then_inc(turned, 1)

        normed = sb("normed", [P, GT, D])
        n_parts = sb("n_parts", [P, 2, GT, D], F16)
        n_turned = sb("n_turned", [P, 2, DC, 2, GT, P], F16)
        score = sb("score", [P, GT, EXPERTS])
        choice = sb("choice", [P, GT, EXPERTS])
        group = sb("group", [P, GT, EGROUPS])
        above4, equal4 = sb("above4", [P, GT, EGROUPS, EGROUPS]), sb("equal4", [P, GT, EGROUPS, EGROUPS])
        above8, equal8 = sb("above8", [P, GT, EXPERTS, EXPERTS]), sb("equal8", [P, GT, EXPERTS, EXPERTS])
        rank4, rank8 = sb("rank4", [P, GT, EGROUPS]), sb("rank8", [P, GT, EXPERTS])
        total = sb("total", [P, GT])
        weight = sb("weight", [P, GT, EXPERTS])
        w_parts = sb("w_parts", [P, GT, 2, EXPERTS], F16)
        w_turned = sb("w_turned", [4 * EXPERTS, 2, GW], F16)
        sig = sb("sig", [P, 2, GW])
        act1, act2, act3 = sb("act1", [P, 2, GW]), sb("act2", [P, 2, GW]), sb("act3", [P, 2, GW])
        a_parts = sb("a_parts", [P, 2, 2, GW], F16)

        (norm_ok, hi_ok, lo_ok, t_turn, t_copied, logits_ok, score_ok, chain, w_ok, w_turn, w_copied, gate_ok, up_ok, weight_ok,
         sig_ok, act1_ok, act2_ok, act3_ok, ahi_ok, alo_ok, down_ok, out_ok, fin_ok, stored, w_zero) = (sem(n) for n in (
             "norm_ok", "hi_ok", "lo_ok", "t_turn", "t_copied", "logits_ok", "score_ok", "route_chain", "w_ok", "w_turn", "w_copied",
             "gate_ok", "up_ok", "weight_ok", "sig_ok", "act1_ok", "act2_ok", "act3_ok", "ahi_ok", "alo_ok", "down_ok", "out_ok",
             "fin_ok", "stored", "w_zero"))
        CH = 18

        with nc.Block() as block:

            @block.sync
            def _(sp):
                view = io["out"].rearrange("b s d -> s b d")

                def step(j, u):
                    if inside(j - 2, GROUPS):
                        t = j - 2
                        reach(sp, fin_ok, t + 1)
                        sp.dma_start(view[:, (t * GT):(t * GT) + GT, :] if isinstance(t, int) else view[:, bass.ds(t * GT, GT), :],
                                     m.x[:, (t * GT):(t * GT) + GT, :] if isinstance(t, int) else m.x[:, bass.ds(t * GT, GT), :]).then_inc(stored, 16)

                run_steps(sp, step, 2, head, GROUPS, lag)
                sp.wait_ge(stored, 16 * GROUPS)

            @block.tensor
            def _(pe):
                terms = ((0, 0), (0, 1), (1, 0))

                def product(dst, w, u, e):
                    for n, (part, wpart) in enumerate(terms):
                        for d in range(DC):
                            last = nc.tensor.matmul(dst[:, :], w[:, wpart, d, e * P:(e + 1) * P],
                                                    n_turned[:, u % 2, d, part, :, :].rearrange("p t k -> p (t k)"),
                                                    start=(n == 0 and d == 0), stop=(n == 2 and d == DC - 1))
                    return last

                def down(t, e):
                    n = t * EXPERTS + e
                    reach(pe, alo_ok, n + 1)
                    if e == 0:
                        reach(pe, fin_ok, t)
                    for k in range(GT):
                        dst = out[k // 2][:, (k % 2) * D:(k % 2 + 1) * D]
                        for s, (part, wpart) in enumerate(terms):
                            last = nc.tensor.matmul(dst, a_parts[:, e % 2, part, k * P:(k + 1) * P], down_t[:, wpart, e, :],
                                                    start=(e == 0 and s == 0 and k % 2 == 0), stop=(e == EXPERTS - 1 and s == 2),
                                                    skip_group_check=True)
                    last.then_inc(down_ok, 1)
                    return last

                def turn_tokens(j):
                    reach(pe, lo_ok, j + 1)
                    for d in range(DC):
                        reach(pe, t_copied, 2 * j + (d - 1))
                        for part in range(2):
                            for k in range(GT):
                                n = part * GT + k
                                last = nc.tensor.transpose(turn[d][:, n * P:(n + 1) * P], n_parts[:, part, k, d * P:(d + 1) * P], m.ident16[:, :])
                        last.then_inc(t_turn, 1)

                def logits(j, u):
                    reach(pe, t_copied, 2 * j + 2)
                    reach(pe, w_copied, j)
                    for k in range(GT):
                        for s, (part, wpart) in enumerate(((0, 0), (0, 1), (1, 0), (1, 1))):
                            for d in range(DC):
                                last = nc.tensor.matmul(route_ps[:, k * EXPERTS:(k + 1) * EXPERTS], n_turned[:, u % 2, d, part, k, :],
                                                        router[:, wpart, d, :], start=(s == 0 and d == 0), stop=(s == 3 and d == DC - 1))
                    last.then_inc(logits_ok, 1)

                def turn_weights(j):
                    reach(pe, w_ok, j + 1)
                    for k in range(GT):
                        last = nc.tensor.transpose(route_ps[0:2 * EXPERTS, :].bitcast(F16)[:, k * P:(k + 1) * P],
                                                   w_parts[:, k, :, :].rearrange("p a e -> p (a e)"), m.ident16[:, :])
                    last.then_inc(w_turn, 1)

                def step(j, u):
                    for e in range(EXPERTS):
                        if inside(j - 1, GROUPS):
                            n = (j - 1) * EXPERTS + e
                            if e == 0:
                                reach(pe, t_copied, 2 * j)
                            reach(pe, act1_ok, n)
                            product(gate_ps, wt["gate"], u - 1, e).then_inc(gate_ok, 1)
                            reach(pe, act2_ok, n)
                            product(up_ps, wt["up"], u - 1, e).then_inc(up_ok, 1)
                            if e == 0:
                                reach(pe, w_copied, j)
                            reach(pe, act3_ok, n)
                            nc.tensor.matmul(weight_ps[:, :], select[:, e, :], w_turned[:, (u - 1) % 2, :], start=True, stop=True).then_inc(weight_ok, 1)
                        if inside(j, GROUPS):
                            if e == 1:
                                turn_tokens(j)
                            if e == 2:
                                logits(j, u)
                            if e == 6:
                                turn_weights(j)
                        if e == 0 and inside(j - 2, GROUPS):
                            down(j - 2, EXPERTS - 1)
                        if e >= 1 and inside(j - 1, GROUPS):
                            down(j - 1, e - 1)

                run_steps(pe, step, 2, head, GROUPS, lag)

            @block.vector
            def _(dve):
                nc.vector.memset(w_turned[:], 0.0).then_inc(w_zero, 1)
                dve.wait_ge(w_zero, 1)

                def expert(t, u, e):
                    n = t * EXPERTS + e
                    p = e % 2
                    reach(dve, sig_ok, n + 1)
                    nc.vector.tensor_tensor(act1[:, p, :], sig[:, p, :], gate_ps[:, :], ALU.mult).then_inc(act1_ok, 1)
                    reach(dve, up_ok, n + 1)
                    reach(dve, act1_ok, n + 1)
                    nc.vector.tensor_tensor(act2[:, p, :], act1[:, p, :], up_ps[:, :], ALU.mult).then_inc(act2_ok, 1)
                    reach(dve, weight_ok, n + 1)
                    reach(dve, act2_ok, n + 1)
                    reach(dve, alo_ok, n - 1)
                    nc.vector.tensor_tensor(act3[:, p, :], act2[:, p, :], weight_ps[:, :], ALU.mult).then_inc(act3_ok, 1)

                def route(j, piece):
                    step = [(0, 7, 13)[piece]]

                    def then(instruction):
                        step[0] += 1
                        instruction.then_inc(chain, 1)
                        reach(dve, chain, j * CH + step[0])

                    def ranks(values, count, above, equal, before, rank):
                        theirs = values[:, :, None, :].broadcast_to([P, GT, count, count])
                        own = values[:, :, :, None].broadcast_to([P, GT, count, count])
                        first = before[:, None, :, :].broadcast_to([P, GT, count, count])
                        then(nc.vector.tensor_tensor(above[:], theirs, own, ALU.is_gt))
                        then(nc.vector.tensor_tensor(equal[:], theirs, own, ALU.is_equal))
                        then(nc.vector.tensor_tensor(equal[:], equal[:], first, ALU.mult))
                        then(nc.vector.tensor_tensor(above[:], above[:], equal[:], ALU.add))
                        then(nc.vector.tensor_reduce(rank[:], above[:], AX.X, ALU.add))

                    if piece == 0:
                        reach(dve, score_ok, j + 1)
                        then(nc.vector.tensor_tensor(choice[:], score[:], bias[:, None, :].broadcast_to([P, GT, EXPERTS]), ALU.add))
                        then(nc.vector.tensor_tensor(group[:], choice[:, :, 0::2], choice[:, :, 1::2], ALU.add))
                        ranks(group, EGROUPS, above4, equal4, before4, rank4)
                        assert step[0] == 7
                    if piece == 1:
                        then(nc.vector.scalar_tensor_tensor(out=choice[:].rearrange("p t (g s) -> p t g s", s=2),
                                                            in0=rank4[:, :, :, None].broadcast_to([P, GT, EGROUPS, 2]), scalar=float(TOP),
                                                            in1=choice[:].rearrange("p t (g s) -> p t g s", s=2), op0=ALU.is_lt, op1=ALU.mult))
                        ranks(choice, EXPERTS, above8, equal8, before8, rank8)
                        assert step[0] == 13
                    if piece == 2:
                        then(nc.vector.scalar_tensor_tensor(out=weight[:], in0=rank8[:], scalar=float(TOP), in1=score[:], op0=ALU.is_lt, op1=ALU.mult))
                        then(nc.vector.tensor_reduce(total[:], weight[:], AX.X, ALU.add))
                        then(nc.vector.tensor_scalar(total[:], total[:], 1e-20, None, ALU.add))
                        then(nc.vector.reciprocal(total[:], total[:]))
                        then(nc.vector.tensor_tensor(weight[:], weight[:], total[:, :, None].broadcast_to([P, GT, EXPERTS]), ALU.mult))
                        nc.vector.tensor_copy(w_parts[:, :, 0, :], weight[:]).then_inc(w_ok_hi, 1)
                        reach(dve, w_ok_hi, j + 1)
                        nc.vector.tensor_tensor(w_parts[:, :, 1, :], weight[:], w_parts[:, :, 0, :], ALU.subtract).then_inc(w_ok, 1)
                        assert step[0] == CH

                w_ok_hi = sem("w_ok_hi")

                def step(j, u):
                    if inside(j, GROUPS):
                        reach(dve, lo_ok, j)
                        for k in range(GT):
                            last = nc.vector.tensor_scalar(normed[:, k, :], m.x[:, j * GT + k, :], m.mean[:, j, k:k + 1],
                                                           m.rstd[:, j, k:k + 1], ALU.subtract, ALU.mult)
                        last.then_inc(norm_ok, 1)
                    for e in range(EXPERTS):
                        if inside(j - 1, GROUPS):
                            expert(j - 1, u - 1, e)
                        if e == 0 and inside(j - 2, GROUPS):
                            t = j - 2
                            reach(dve, down_ok, t * EXPERTS + EXPERTS)
                            for k in range(GT):
                                x = m.x[:, t * GT + k, :]
                                last = nc.vector.scalar_tensor_tensor(out=x, in0=out[k // 2][:, (k % 2) * D:(k % 2 + 1) * D],
                                                                      scalar=res_gate[:, 0:1], in1=x, op0=ALU.mult, op1=ALU.add)
                            last.then_inc(fin_ok, 1)
                        if e == 1 and inside(j, GROUPS):
                            for d in range(DC):
                                reach(dve, t_turn, 2 * j + (d + 1))
                                nc.vector.tensor_copy(n_turned[:, u % 2, d, :, :, :],
                                                      turn[d][:, :].rearrange("p (a t k) -> p a t k", a=2, t=GT)).then_inc(t_copied, 1)
                        if e in (3, 4, 5) and inside(j, GROUPS):
                            route(j, e - 3)
                        if e == EXPERTS - 1 and inside(j, GROUPS):
                            reach(dve, w_turn, j + 1)
                            nc.vector.tensor_copy(w_turned[0:2 * EXPERTS, u % 2, :], route_ps[0:2 * EXPERTS, :].bitcast(F16)[:, 0:GW]).then_inc(w_copied, 1)

                run_steps(dve, step, 2, head, GROUPS, lag)

            @block.scalar
            def _(act):
                nc.scalar.preload_act_table(ACT.Sigmoid)

                def step(j, u):
                    if inside(j, GROUPS):
                        reach(act, norm_ok, j + 1)
                        reach(act, t_turn, 2 * j)
                        nc.scalar.activation(n_parts[:, 0, :, :], normed[:], ACT.Copy).then_inc(hi_ok, 1)
                    for e in range(EXPERTS):
                        if inside(j - 1, GROUPS):
                            n = (j - 1) * EXPERTS + e
                            reach(act, gate_ok, n + 1)
                            reach(act, act1_ok, n - 1)
                            nc.scalar.activation(sig[:, e % 2, :], gate_ps[:, :], ACT.Sigmoid, scale=1.0 / WS).then_inc(sig_ok, 1)
                        if inside(j - 1, GROUPS):
                            reach(act, act3_ok, n + 1)
                            reach(act, down_ok, n - 1)
                            nc.scalar.activation(a_parts[:, e % 2, 0, :], act3[:, e % 2, :], ACT.Copy).then_inc(ahi_ok, 1)
                        if e == 2 and inside(j, GROUPS):
                            reach(act, logits_ok, j + 1)
                            reach(act, w_ok, j)
                            nc.scalar.activation(score[:].rearrange("p t e -> p (t e)"), route_ps[:, 0:GT * EXPERTS], ACT.Sigmoid).then_inc(score_ok, 1)

                run_steps(act, step, 2, head, GROUPS, lag)

            @block.gpsimd
            def _(pool):
                def step(j, u):
                    if inside(j, GROUPS):
                        reach(pool, hi_ok, j + 1)
                        nc.gpsimd.tensor_tensor(n_parts[:, 1, :, :], normed[:], n_parts[:, 0, :, :], ALU.subtract).then_inc(lo_ok, 1)
                    for e in range(EXPERTS):
                        if inside(j - 1, GROUPS):
                            reach(pool, ahi_ok, (j - 1) * EXPERTS + (e + 1))
                            nc.gpsimd.tensor_tensor(a_parts[:, e % 2, 1, :], act3[:, e % 2, :], a_parts[:, e % 2, 0, :],
                                                    ALU.subtract).then_inc(alo_ok, 1)

                run_steps(pool, step, 2, head, GROUPS, lag)


def build_program(nc, io):
    with ExitStack() as ctx:
        m = Shared()

        def sb(name, shape, dt=F32):
            return ctx.enter_context(nc.sbuf_tensor(name, shape, dt))

        def sem(name):
            return ctx.enter_context(nc.semaphore(name))

        m.x = sb("x", [P, TILES, D])
        m.gates, m.tanh_gates = sb("gates", [P, 4]), sb("tanh_gates", [P, 4])
        m.ident32, m.ident16 = sb("ident32", [P, P]), sb("ident16", [P, P], F16)
        m.ones32 = sb("ones32", [P, P])
        m.stats = sb("stats", [P, TILES, 6])
        m.mean2 = sb("mean", [P, TILES])
        m.root = sb("root", [P, TILES])
        m.rstd2 = sb("rstd", [P, TILES])
        m.rstd, m.mean = m.rstd2[:, :], m.mean2[:, :]
        m.router_raw, m.router_bias = sb("router_raw", [P, DC, EXPERTS]), sb("router_bias", [P, EXPERTS])
        m.ctx = sb("ctx", [P, TILES, D])
        m.expert_raw = [m.ctx[:, n * EXPERTS:(n + 1) * EXPERTS, :] for n in range(3)]
        m.expert_loaded = [sem(f"expert_loaded{n}") for n in range(4)]
        load_stage(nc, io, m, sem)
        attention_stage(nc, io, m, 0, sem)
        m.rstd, m.mean = (v[:, :].rearrange("p (j k) -> p j k", k=GT) for v in (m.rstd2, m.mean2))
        bitnet_stage(nc, io, m)
        m.rstd, m.mean = m.rstd2[:, :], m.mean2[:, :]
        attention_stage(nc, io, m, 1, sem)
        deviation_stage(nc, m, sem, "dev3")
        m.rstd, m.mean = (v[:, :].rearrange("p (j k) -> p j k", k=GT) for v in (m.rstd2, m.mean2))
        expert_stage(nc, io, m)


_INS = ["x", "ctx_1024", "g_xattn", "g_ffn", "L0_ffn_w1", "L0_ffn_conv_w", "L0_ffn_conv_b", "L0_ffn_w2",
        "L1_xattn_Wq", "L1_xattn_Wk", "L1_xattn_Wv", "L1_ffn_gate_weight", "L1_ffn_e_score_correction_bias",
        "L1_ffn_gate_proj", "L1_ffn_up_proj", "L1_ffn_down_proj"]


def kernel(**inputs):
    import numpy as np
    import concourse.bacc as bacc
    from concourse import mybir as mb
    from concourse.bass_utils import run_bass_kernel_spmd

    nc = bacc.Bacc("TRN2", target_bir_lowering=False, num_devices=1)
    arrays, io = {}, {}
    for name in _INS:
        a = np.ascontiguousarray(inputs[name])
        arrays[f"in_{name}"] = a
        io[name] = nc.dram_tensor(f"in_{name}", a.shape, mb.dt.from_np(a.dtype), kind="ExternalInput").ap()
    io["out"] = nc.dram_tensor("out", (TILES, P, D), mb.dt.float32, kind="ExternalOutput").ap()
    build_program(nc, io)
    result = run_bass_kernel_spmd(nc, [arrays], core_ids=[0])
    return result.results[0]["out"]
```
